# Optimizing a Trainium2 kernel written in Bass

```python
import numpy as np
import jax
import jax.numpy as jnp

def _softmax(x, axis=-1):
    return jax.nn.softmax(x, axis=axis)

def _gelu(x):
    return jax.nn.gelu(x, approximate=True)

def _silu(x):
    return jax.nn.silu(x)

def _sigmoid(x):
    return jax.nn.sigmoid(x)

def _layernorm(x, axis=-1, eps=1e-05):
    m = jnp.mean(x, axis=axis, keepdims=True)
    v = jnp.var(x, axis=axis, keepdims=True)
    return (x - m) / jnp.sqrt(v + eps)

def _scatter_add(tgt, idx, src, axis=0):
    return tgt.at[idx].add(src)

def _segment_sum(src, seg, n):
    return jax.ops.segment_sum(src, seg, n)
kernel_name = 'mk_adj_preln_d4_adj_r2_87f797'

def setup_inputs(seed: int=0):
    np.random.seed(seed)
    _w = jnp.asarray

    def _rec_inputs():
        import jax
        import jax.numpy as jnp
        _gk = jax.random.key(seed)
        x = -0.0002928 + 1 * jax.random.normal(jax.random.fold_in(_gk, 1), (4096, 256), jnp.float32)
        _w = (1.0 + jnp.arange(4096, dtype=jnp.float32)) ** (-0.5)
        _w = _w / _w.mean()
        _pij = jnp.clip(0.00195312 * _w[:, None] * _w[None, :], 0.0, 1.0)
        _a = jax.random.uniform(jax.random.fold_in(_gk, 2), (4096, 4096)) < _pij
        _af = _a.astype(jnp.float32)
        adj = _af
        return (x, adj)
    x, adj = _rec_inputs()

    def _L0_gnn_setup():
        import jax, jax.numpy as jnp
        import numpy as np
        SIZE_U = 2048
        SIZE_V = 2048
        N = SIZE_U + SIZE_V
        C_IN = 256
        C_OUT = 256
        EDGE_P = 0.005
        LEAKY_SLOPE = 0.01

        def _xavier_uniform(key, shape):
            fan_in, fan_out = shape
            lim = float(np.sqrt(6.0 / (fan_in + fan_out)))
            return jax.random.uniform(key, shape, jnp.float32, minval=-lim, maxval=lim)
        key = jax.random.key(seed)
        k1, k2, k3, k4 = jax.random.split(key, 4)
        x = jax.random.normal(k1, (N, C_IN), jnp.float32)
        adj = (jax.random.uniform(k2, (N, N)) < EDGE_P).astype(jnp.float32)
        weightr = _xavier_uniform(k3, (C_IN, C_OUT))
        weightd = _xavier_uniform(k4, (C_IN, C_OUT))
        bias = jnp.zeros((C_OUT,), jnp.float32)
        return {'x': x, 'adj': adj, 'weightr': weightr, 'weightd': weightd, 'bias': bias}
    _L0_gnn_all = _L0_gnn_setup()
    _L0_gnn_in = {k: v for k, v in _L0_gnn_all.items() if k in ('weightr', 'weightd', 'bias')}
    del _L0_gnn_all

    def _L1_gnn_setup():
        import jax, jax.numpy as jnp
        import numpy as np
        N, NFEAT, NHID = (8192, 256, 256)

        def _gc_layer(x, adj, W):
            support = adj @ x
            h = jnp.concatenate([x, support], axis=1)
            return h @ W
        key = jax.random.key(seed)
        k1, k2, k3, k4 = jax.random.split(key, 4)
        x = jax.random.normal(k1, (N, NFEAT), dtype=jnp.float32)
        adj = jax.random.uniform(k2, (N, N), dtype=jnp.float32)
        stdv1 = 1.0 / np.sqrt(NHID)
        W1 = jax.random.uniform(k3, (2 * NFEAT, NHID), dtype=jnp.float32, minval=-stdv1, maxval=stdv1)
        W2 = jax.random.uniform(k4, (2 * NHID, NHID), dtype=jnp.float32, minval=-stdv1, maxval=stdv1)
        return {'x': x, 'adj': adj, 'W1': W1, 'W2': W2}
    _L1_gnn_all = _L1_gnn_setup()
    _L1_gnn_in = {k: v for k, v in _L1_gnn_all.items() if k in ('W1', 'W2')}
    del _L1_gnn_all

    def _L2_gnn_setup():
        import jax, jax.numpy as jnp
        import numpy as np
        N = 4096
        D_IN = 256
        D_OUT = 256
        key = jax.random.key(seed)
        k1, k2, k3, k4 = jax.random.split(key, 4)
        x = jax.random.normal(k1, (N, D_IN), dtype=jnp.float32)
        adj = jax.random.uniform(k2, (N, N), dtype=jnp.float32)
        bound = 1.0 / np.sqrt(D_IN)
        W = jax.random.uniform(k3, (D_OUT, D_IN), minval=-bound, maxval=bound, dtype=jnp.float32)
        b = jax.random.uniform(k4, (D_OUT,), minval=-bound, maxval=bound, dtype=jnp.float32)
        return {'x': x, 'adj': adj, 'W': W, 'b': b}
    _L2_gnn_all = _L2_gnn_setup()
    _L2_gnn_in = {k: v for k, v in _L2_gnn_all.items() if k in ('W', 'b')}
    del _L2_gnn_all

    def _L3_gnn_setup():
        import jax, jax.numpy as jnp
        import numpy as np
        ALPHA = 0.2
        NEG_INF = -1000000000000.0
        key = jax.random.key(seed)
        k1, k2, k3, k4, k5 = jax.random.split(key, 5)
        N, F = (2048, 256)
        inp = jax.random.normal(k1, (N, F), dtype=jnp.float32)
        adj = jax.random.randint(k2, (N, N), 0, 2).astype(jnp.float32)
        W = jax.random.normal(k3, (F, F), dtype=jnp.float32) * (1.414 / np.sqrt(F))
        a = jax.random.normal(k4, (2 * F, 1), dtype=jnp.float32) * 0.05
        wtrans = jax.random.normal(k5, (2 * F, F), dtype=jnp.float32) * (1.414 / np.sqrt(1.5 * F))
        return {'inp': inp, 'adj': adj, 'W': W, 'a': a, 'wtrans': wtrans}
    _L3_gnn_all = _L3_gnn_setup()
    _L3_gnn_in = {k: v for k, v in _L3_gnn_all.items() if k in ('W', 'a', 'wtrans')}
    del _L3_gnn_all
    return {'x': x, 'adj': adj, 'L0_gnn_weightr': _L0_gnn_in['weightr'], 'L0_gnn_weightd': _L0_gnn_in['weightd'], 'L0_gnn_bias': _L0_gnn_in['bias'], 'L1_gnn_W1': _L1_gnn_in['W1'], 'L1_gnn_W2': _L1_gnn_in['W2'], 'L2_gnn_W': _L2_gnn_in['W'], 'L2_gnn_b': _L2_gnn_in['b'], 'L3_gnn_W': _L3_gnn_in['W'], 'L3_gnn_a': _L3_gnn_in['a'], 'L3_gnn_wtrans': _L3_gnn_in['wtrans']}

def reference(x, adj, L0_gnn_weightr, L0_gnn_weightd, L0_gnn_bias, L1_gnn_W1, L1_gnn_W2, L2_gnn_W, L2_gnn_b, L3_gnn_W, L3_gnn_a, L3_gnn_wtrans):
    import jax
    import jax.numpy as jnp

    def _L0_gnn_ref(x, adj, weightr, weightd, bias):
        import jax, jax.numpy as jnp
        import numpy as np
        SIZE_U = 2048
        SIZE_V = 2048
        N = SIZE_U + SIZE_V
        C_IN = 256
        C_OUT = 256
        EDGE_P = 0.005
        LEAKY_SLOPE = 0.01

        def _xavier_uniform(key, shape):
            fan_in, fan_out = shape
            lim = float(np.sqrt(6.0 / (fan_in + fan_out)))
            return jax.random.uniform(key, shape, jnp.float32, minval=-lim, maxval=lim)
        A = adj + jnp.eye(N, dtype=adj.dtype)
        deg = A.sum(axis=1)
        dinv = jnp.where(deg > 0, jax.lax.rsqrt(deg), 0.0)
        A = A * dinv[:, None] * dinv[None, :]
        R = x[:SIZE_U] @ weightr
        D = x[SIZE_U:] @ weightd
        h = jnp.concatenate([R, D], axis=0)
        out = A @ h + bias
        return jax.nn.leaky_relu(out, negative_slope=LEAKY_SLOPE)

    def _L1_gnn_ref(x, adj, W1, W2):
        import jax, jax.numpy as jnp
        import numpy as np
        N, NFEAT, NHID = (8192, 256, 256)

        def _gc_layer(x, adj, W):
            support = adj @ x
            h = jnp.concatenate([x, support], axis=1)
            return h @ W
        h = jax.nn.relu(_gc_layer(x, adj, W1))
        h = jax.nn.relu(_gc_layer(h, adj, W2))
        return h

    def _L2_gnn_ref(x, adj, W, b):
        import jax, jax.numpy as jnp
        import numpy as np
        N = 4096
        D_IN = 256
        D_OUT = 256
        a = adj + jnp.eye(adj.shape[0], dtype=adj.dtype)
        d = jnp.sum(a, axis=1) ** (-0.5)
        a_norm = d[:, None] * a * d[None, :]
        support = a_norm @ x
        out = support @ W.T + b
        out = jax.nn.relu(out)
        return out

    def _L3_gnn_ref(inp, adj, W, a, wtrans):
        import jax, jax.numpy as jnp
        import numpy as np
        ALPHA = 0.2
        NEG_INF = -1000000000000.0
        F_out = W.shape[1]
        h = inp @ W
        Wh1 = h @ a[:F_out, :]
        Wh2 = h @ a[F_out:, :]
        e = jax.nn.leaky_relu(Wh1 + Wh2.T, ALPHA)
        mask = adj > 0
        attention = jax.nn.softmax(jnp.where(mask, e, NEG_INF), axis=1)
        negative_attention = -jax.nn.softmax(jnp.where(mask, -e, NEG_INF), axis=1)
        h_prime = attention @ inp
        h_prime_negative = negative_attention @ inp
        h_prime_double = jnp.concatenate([h_prime, h_prime_negative], axis=1)
        new_h_prime = h_prime_double @ wtrans
        return jax.nn.elu(new_h_prime)
    h = jnp.maximum(_layernorm(x, axis=-1), 0.0)
    x = x + _L0_gnn_ref(h, adj, L0_gnn_weightr, L0_gnn_weightd, L0_gnn_bias)
    h = jnp.maximum(_layernorm(x, axis=-1), 0.0)
    x = x + _L1_gnn_ref(h, adj, L1_gnn_W1, L1_gnn_W2)
    h = jnp.maximum(_layernorm(x, axis=-1), 0.0)
    x = x + _L2_gnn_ref(h, adj, L2_gnn_W, L2_gnn_b)
    h = jnp.maximum(_layernorm(x, axis=-1), 0.0)
    x = x + _L3_gnn_ref(h, adj, L3_gnn_W, L3_gnn_a, L3_gnn_wtrans)
    return x

_drawn_inputs = setup_inputs


def setup_inputs(seed=0):
    import zlib

    import numpy as np

    out = dict(_drawn_inputs(seed))
    spreads = {'L0_gnn_bias': (0.0, 0.1)}
    factors = {'L2_gnn_W': 3.167, 'L2_gnn_b': 31.656, 'L3_gnn_W': 8.0, 'L3_gnn_a': 21.518}
    for name, (base, spread) in spreads.items():
        noise = np.random.default_rng([zlib.crc32(name.encode()), seed]).standard_normal(out[name].shape)
        drawn = base * np.exp(spread * noise) if base else spread * noise
        out[name] = jnp.asarray(drawn.astype(out[name].dtype))
    for name, factor in factors.items():
        out[name] = (out[name] * factor).astype(out[name].dtype)
    return out
```

```python
import concourse.bass as bass
from concourse import mybir
from contextlib import ExitStack

P = 128


def gnn_stack(nc, x_in, adj_t, adj, w_gcn, b_gcn, w_conv1, w_conv2, w_gcn2, b_gcn2,
              w_att_t, a_att, w_trans, out):
    f32, f16, bf16, u8, i32 = (mybir.dt.float32, mybir.dt.float16, mybir.dt.bfloat16,
                               mybir.dt.uint8, mybir.dt.int32)
    ALU, ACT, AX = mybir.AluOpType, mybir.ActivationFunctionType, mybir.AxisListType

    N, F = x_in.shape
    NT = N // P
    CH = 512
    NC = N // CH
    TPC = CH // P
    FB = F // P
    PANELS = 2
    GROUPS = NT // PANELS
    STAGES = 4
    QW = 1024
    NQ = N // QW
    HALF = N // 2
    YW = F + 1
    RING = 8
    EPS = 1e-5
    SC = 2048.0
    BIG = 3e38
    EVACS = [2, 2, 2, 1]
    KB = [4, 4, 4, 2]
    WQ = 4

    xs = nc.dram_tensor("x_spill", (N, F), f32).ap()
    hs = nc.dram_tensor("h_spill", (N, F), f32).ap()

    def chunk_rows(t, c):
        return t.rearrange("(c t p) f -> c p t f", p=P, t=TPC)[c, :, :, :]

    ctx = ExitStack()
    with ctx:
        def sb(name, shape, dt):
            return ctx.enter_context(nc.sbuf_tensor(name, shape, dt))

        def sem(name):
            return ctx.enter_context(nc.semaphore(name))

        Y_WORDS = NT * 2 * YW
        big = sb("big", [P, Y_WORDS + NT * CH], f32)
        feat = sb("feat", [P, NT * F], f32)
        work = sb("work", [P, 10240], f32)

        def words(t, lo, n):
            return t[:, lo:lo + n]

        adj8 = words(big, 0, N * NT // 4).bitcast(u8).rearrange("p (j n) -> p j n", j=NT)
        feat32 = feat[:, :].rearrange("p (j f) -> p j f", j=NT)
        parts = feat[:, :].bitcast(f16).rearrange("p (j h f) -> p j h f", j=NT, h=2)
        T_all = words(big, Y_WORDS + NT * CH // 2, NT * F).rearrange("p (c k n) -> p c k n", c=NC, k=FB)
        T_sb = words(work, 0, 2048).rearrange("p (k n) -> p k n", k=4)
        stage = words(work, 2048, 2048).bitcast(bf16).rearrange("p (s j n) -> p s j n", s=STAGES, j=PANELS)
        h_ring = words(work, 4096, 2048).bitcast(f16).rearrange("p (s t h f) -> p s t h f", s=2, t=TPC, h=2)
        g_ring = words(work, 4096, 2048).rearrange("p (s t f) -> p s t f", s=2, t=TPC)
        x_ring = words(work, 6144, 2048).rearrange("p (s t f) -> p s t f", s=2, t=TPC)
        w_sb = words(work, 8192, 1024).rearrange("p (k f) -> p k f", k=4)
        bias_row = words(work, 9216, F)
        y_tmp = words(work, 9216 + F, F)
        hs32 = words(work, 9216 + 2 * F, 2 * F).rearrange("p (s f) -> p s f", s=2)
        quarter = words(work, 0, NQ * QW).rearrange("p (q n) -> p q n", q=NQ)
        quarter16 = words(work, 8192, QW).bitcast(bf16).rearrange("p (s n) -> p s n", s=2)
        Yb = words(big, 0, Y_WORDS).rearrange("p (j s f) -> p j s f", j=NT, s=2)
        mask = words(big, Y_WORDS, NT * CH).rearrange("p (j n) -> p j n", j=NT)
        wt_sb = words(work, 8192, 1024).rearrange("p (k f) -> p k f", k=FB)
        t_row = words(work, 0, 4096)
        E = words(work, 4096, RING * CH).rearrange("p (s n) -> p s n", s=RING)
        R = words(work, 8192, 2 * TPC * F).rearrange("p (s t f) -> p s t f", s=2, t=TPC)
        rows = words(feat, 0, 2 * HALF).rearrange("p (s n) -> p s n", s=2)
        AB = words(feat, 4096, WQ * CH).rearrange("p (q n) -> p q n", q=WQ)
        junk = words(feat, 6144, HALF // 4).bitcast(u8)
        mean_y = words(feat, 6656, F)
        x3 = words(feat, 6912, TPC * F).rearrange("p (t f) -> p t f", t=TPC)
        att_cols = words(feat, 7936, 256)
        u_col = att_cols[:, 0:NT]
        v_8 = att_cols[:, NT:3 * NT].rearrange("p (s j) -> p s j", s=2)
        v_2 = att_cols[:, 3 * NT:5 * NT].rearrange("p (s j) -> p s j", s=2)
        tmx = att_cols[:, 160:168].rearrange("p (t h) -> p t h", h=2)
        tmn = att_cols[:, 168:176].rearrange("p (t h) -> p t h", h=2)
        ccol = att_cols[:, 176:176 + 32].rearrange("p (q t) -> p q t", t=TPC)
        rz = att_cols[:, 208:216].rearrange("p (s t) -> p s t", s=2)
        strip = sb("strip", [P, 12, P], f16)
        ident16 = strip[:, 4, :]
        ident32 = sb("ident32", [P, P], f32)
        w3t_sb = sb("w3t_sb", [P, FB, F], f32)
        a_sb = sb("a_sb", [P, FB, 2], f32)
        wa_sb = sb("wa_sb", [P, FB, 2], f32)
        ones16 = sb("ones16", [P, 1], bf16)
        dinv = sb("dinv", [P, NT], f32)
        fac = sb("fac", [P, NT], f32)
        dsc = sb("dsc", [P, NT], f32)
        lone = sb("lone", [P, NT], f32)
        gmax = sb("gmax", [P, NT], f32)
        uv_sb = sb("uv_sb", [P, NT, 2], f32)
        uv_cols = sb("uv_cols", [P, 2, NT], f32)
        stat = sb("stat", [P, TPC, 6], f32)
        mv = sb("mv", [P, TPC, 2], f32)
        mean_c, var_c = mv[:, :, 0], mv[:, :, 1]
        ln = sb("ln", [P, 5, TPC], f32)
        var_e, std, rough, scale_c, shift_c = (ln[:, k, :] for k in range(5))
        deg1, deg_std = uv_cols[:, 0, :], uv_cols[:, 1, :]
        sc = sb("sc", [P, 16], f32)
        g_own, g_all, g_pow, g_scale, g_inv = (sc[:, k:k + 1] for k in range(5))
        v_hi, v_lo, v_rng, v_r, v_R, v_c1, v_c2, v_nR = (sc[:, k:k + 1] for k in range(5, 13))
        vext = sb("vext", [P, 2, NC], f32)
        hsum = sb("hsum", [P, FB, NC], f32)
        hsum1 = sb("hsum1", [P, FB], f32)

        ps = ctx.enter_context(nc.psum_tensor("ps", [P, 8, 512], f32))

        def out_slot(t):
            return ps[:, 6 + t // 2, (t % 2) * F:(t % 2 + 1) * F]

        quarter_in = [sem(f"quarter_in{q}") for q in range(NQ)]
        small_in, weights_in = sem("small_in"), sem("weights_in")
        x_in_s = [sem(f"x_in{s}") for s in range(2)]
        parts_in = [sem(f"parts_in{c}") for c in range(NC)]
        x_out = [sem(f"x_out{s}") for s in range(2)]
        h_out = [sem(f"h_out{s}") for s in range(2)]
        memset_done, consts_ready = sem("memset_done"), sem("consts_ready")
        cast8_done, cast16_done = sem("cast8_done"), sem("cast16_done")
        deg_used, deg_done = sem("deg_used"), sem("deg_done")
        lncol_ready, h0_done = sem("lncol_ready"), sem("h0_done")
        var_ready, std_ready = sem("var_ready"), sem("std_ready")
        wa_ps_ready, wa_ready = sem("wa_ps_ready"), sem("wa_ready")
        dve_step = sem("dve_step")
        scaled_ready, hi_split, split_done = sem("scaled_ready"), sem("hi_split"), sem("split_done")
        panel_ready, group_done = sem("panel_ready"), sem("group_done")
        ht1_ready, evac_done, out_ready = sem("ht1_ready"), sem("evac_done"), sem("out_ready")
        out_used = [sem(f"out_used{l}") for l in range(4)]
        hs_ready, hi_ready, post_done = sem("hs_ready"), sem("hi_ready"), sem("post_done")
        gown_ready, gall_ready = sem("gown_ready"), sem("gall_ready")
        ht_ready, ht_evac, scores_done, ht_summed = sem("ht_ready"), sem("ht_evac"), sem("scores_done"), sem("ht_summed")
        y_ps_ready, y_evac, uv_ready, cols_ready = sem("y_ps_ready"), sem("y_evac"), sem("uv_ready"), sem("cols_ready")
        hsum_ready, my_ps_ready, my_ready = sem("hsum_ready"), sem("my_ps_ready"), sem("my_ready")
        vb_ps_ready, vb_evac, ones_set = sem("vb_ps_ready"), sem("vb_evac"), sem("ones_set")
        mask_in = [sem(f"mask_in{g}") for g in range(NC)]
        row_in = [sem(f"row_in{h}") for h in range(2)]
        row_used = sem("row_used")
        cc_ready, ab_ps_ready, ab_ready = sem("cc_ready"), sem("ab_ps_ready"), sem("ab_ready")
        mask_ready, edge_ready = sem("mask_ready"), sem("edge_ready")
        lin_ready, p_ready, p_used = sem("lin_ready"), sem("p_ready"), sem("p_used")
        rz_ready, att_evac = sem("rz_ready"), sem("att_evac")
        pool_step, elu_in, elu_out, neg_ready = sem("pool_step"), sem("elu_in"), sem("elu_out"), sem("neg_ready")
        x3_in, fin_ready, fin_out = sem("x3_in"), sem("fin_ready"), sem("fin_out")

        def wait(eng, s, v):
            if not isinstance(v, int) or v > 0:
                eng.wait_ge(s, v)

        block = ctx.enter_context(nc.Block())

        LG = NC * GROUPS
        EVAC_BASE = [NC * sum(EVACS[:l]) for l in range(5)]
        X_USES = {0: 1, 2: 2, 3: 3}
        X_STORES = {0: 0, 2: 1, 3: 2}
        HI_BASE = {0: 0, 2: NT, 3: 2 * NT}
        W_NEEDED = [32, 48, 64, 96, 128]
        H = NC // 2

        @block.sync
        def _(sp):
            def load_quarter(j, q):
                sp.dma_start(quarter[:, q, :], adj_t.rearrange("(j p) (q n) -> j q p n", p=P, q=NQ)[j, q, :, :])\
                  .then_inc(quarter_in[q], 16)

            def load_x(src, c, s):
                sp.dma_start(x_ring[:, s, :, :], chunk_rows(src, c)).then_inc(x_in_s[s], 16)

            def load_weights(l):
                src = [w_gcn, w_conv1, w_conv2, w_gcn2][l]
                sp.dma_start(w_sb[:, 0:KB[l], :], src.rearrange("(k p) f -> p k f", p=P)).then_inc(weights_in, 16)
                if l in (0, 3):
                    sp.dma_start(bias_row, (b_gcn if l == 0 else b_gcn2).partition_broadcast(P)).then_inc(weights_in, 16)

            load_x(x_in, 0, 0)
            for q in range(NQ):
                load_quarter(0, q)
            load_x(x_in, 1, 1)
            sp.dma_start(w3t_sb[:, :, :], w_att_t.rearrange("(k p) f -> p k f", p=P)).then_inc(small_in, 16)
            sp.dma_start(a_sb[:, :, :], a_att.rearrange("(k p) f -> p k f", p=P)).then_inc(small_in, 16)

            def panels(c, last):
                for t in range(TPC):
                    if last and t == TPC - 1:
                        continue
                    for q in range(NQ):
                        sp.wait_ge(cast8_done, (c * TPC + t) * NQ + q + 1)
                        sp.wait_ge(cast16_done, (c * TPC + t) * NQ + q + 1)
                        load_quarter(c * TPC + t + 1, q)

            panels(0, False)
            with sp.Fori(0, H - 1) as r:
                for s in range(2):
                    panels(2 * r + s + 1, False)
                    sp.wait_ge(h0_done, (2 * r + s + 1) * TPC)
                    load_x(x_in, 2 * r + s + 2, s)
            panels(NC - 1, True)
            for s in range(2):
                sp.wait_ge(h0_done, (NC - 1 + s) * TPC)
                load_x(x_in, s, s)
            sp.wait_ge(deg_done, 1)
            load_weights(0)

            def reload(l, c):
                sp.wait_ge(group_done, l * LG + (NC - 1) * GROUPS + (c + 1) * TPC // PANELS)
                sp.wait_ge(h_out[c % 2], 16 * (l * H + c // 2 + 1))
                sp.dma_start(feat32[:, c * TPC:(c + 1) * TPC, :], chunk_rows(hs, c)).then_inc(parts_in[c], 16)

            for l in range(4):
                nxt = {0: None, 1: (2, xs), 2: (3, xs), 3: None}[l]

                def store(c, s):
                    sp.wait_ge(post_done, l * NC + c + 1)
                    if l != 1:
                        sp.dma_start(chunk_rows(xs, c), x_ring[:, s, :, :]).then_inc(x_out[s], 16)
                    sp.dma_start(chunk_rows(hs, c), g_ring[:, s, :, :]).then_inc(h_out[s], 16)

                def refill(c, s, cc):
                    sp.wait_ge(x_out[s], 16 * (X_STORES[l] * H + cc + 1))
                    load_x(x_in if l == 0 else xs, c + 2, s)

                with sp.Fori(0, H - 1) as r:
                    for s in range(2):
                        store(2 * r + s, s)
                        if l != 1:
                            refill(2 * r + s, s, r)
                for c in range(4):
                    reload(l, c)
                store(NC - 2, 0)
                for c in range(4, NC - 1):
                    reload(l, c)
                store(NC - 1, 1)
                reload(l, NC - 1)
                if l != 1:
                    for s in range(2):
                        sp.wait_ge(x_out[s], 16 * (X_STORES[l] + 1) * H)
                if l in (0, 2):
                    for s in range(2):
                        load_x(xs, s, s)
                sp.wait_ge(out_ready, (l + 1) * NT)
                if l < 3:
                    load_weights(l + 1)
            for s in range(2):
                sp.dma_start(wt_sb[:, :, s * F:(s + 1) * F],
                             w_trans[s * F:(s + 1) * F, :].rearrange("(k p) f -> p k f", p=P)).then_inc(weights_in, 16)

            def load_mask(c, g):
                src = adj_t.rearrange("(g t p) (c n) -> g c p t n", p=P, t=TPC, n=CH)
                sp.dma_start(mask[:, g * TPC:(g + 1) * TPC, :], src[g, c, :, :, :]).then_inc(mask_in[g], 16)

            def load_row(i, h):
                sp.dma_start(rows[:, h, :], adj.rearrange("(i p) (h n) -> i h p n", p=P, h=2)[i, h, :, :])\
                  .then_inc(row_in[h], 16)

            sp.wait_ge(panel_ready, 4 * LG)
            for g in range(NC // 2):
                load_mask(0, g)
            sp.wait_ge(ht_ready, NC)
            for h in range(2):
                load_row(0, h)

            def chunk_rows_loads(i0):
                for t in range(1, TPC):
                    for h in range(2):
                        sp.wait_ge(row_used, (i0 + t - 1) * 4 + 2 * h + 2)
                        load_row(i0 + t, h)

            chunk_rows_loads(0)
            sp.wait_ge(y_ps_ready, NT)
            for g in range(NC // 2, NC):
                load_mask(0, g)

            def att_loads(c):
                for h in range(2):
                    sp.wait_ge(row_used, (c + 1) * TPC * 4 - 4 + 2 * h + 2)
                    load_row((c + 1) * TPC, h)
                chunk_rows_loads((c + 1) * TPC)
                for g in range(NC):
                    sp.wait_ge(lin_ready, c * NT + (NT + (g + 1) * TPC) // 2)
                    load_mask(c + 1, g)

            with sp.Fori(0, NC - 1) as c:
                att_loads(c)
            for s in range(2):
                sp.wait_ge(x_out[s], 16 * 3 * H)
                sp.wait_ge(h_out[s], 16 * 4 * H)

        @block.gpsimd
        def _(pool):
            nc.gpsimd.memset(strip[:, :, :], 0.0).then_inc(memset_done, 1)
            nc.gpsimd.memset(ident32[:, :], 0.0).then_inc(memset_done, 1)
            nc.gpsimd.memset(ones16[:, :], 1.0).then_inc(consts_ready, 1)
            pool.wait_ge(memset_done, 2)
            eye = strip[:, 4:8, :]
            nc.gpsimd.affine_select(out=eye, in_=eye, compare_op=ALU.not_equal, fill=1.0, base=0,
                                    pattern=[[0, 4], [-1, P]], channel_multiplier=1).then_inc(consts_ready, 1)
            nc.gpsimd.affine_select(out=ident32[:, :], in_=ident32[:, :], compare_op=ALU.not_equal, fill=1.0,
                                    base=0, pattern=[[-1, P]], channel_multiplier=1).then_inc(consts_ready, 1)
            pool.wait_ge(gown_ready, 1)
            nc.gpsimd.partition_all_reduce(g_all, g_own, P, bass.bass_isa.ReduceOp.max).then_inc(gall_ready, 1)

            pool.wait_ge(panel_ready, 4 * LG)
            nc.gpsimd.memset(Yb[:, :, :, F:YW], 1.0).then_inc(ones_set, 1)
            pool.wait_ge(my_ready, 1)

            K = 4

            with pool.Fori(0, NC) as c:
                k = [0]

                def link(ins):
                    k[0] += 1
                    ins.then_inc(pool_step, 1)
                    pool.wait_ge(pool_step, c * K + k[0])

                D, M = R[:, 0, :, :], R[:, 1, :, :]
                pool.wait_ge(att_evac, c * 2 * TPC + 2 * TPC)
                link(nc.gpsimd.tensor_tensor(D, D, M, ALU.add))
                link(nc.gpsimd.tensor_tensor(M, mean_y.rearrange("p (a f) -> p a f", a=1).to_broadcast([P, TPC, F]),
                                             lone[:, bass.ds(c * TPC, TPC)].rearrange("p (t a) -> p t a", a=1)
                                             .to_broadcast([P, TPC, F]), ALU.mult))
                nc.gpsimd.tensor_tensor(D, D, M, ALU.add).then_inc(elu_in, 1)
                pool.wait_ge(x3_in, c * 16 + 16)
                link(nc.gpsimd.tensor_tensor(x3, x3, ones16[:, 0:1].rearrange("p (t a) -> p t a", a=1)
                                             .to_broadcast([P, TPC, F]), ALU.subtract))
                pool.wait_ge(elu_out, c + 1)
                link(nc.gpsimd.tensor_tensor(D, D, x3, ALU.add))
                nc.gpsimd.tensor_tensor(D, D, M, ALU.add).then_inc(fin_ready, 1)

        @block.scalar
        def _(act):
            def copy(out_, in_, **kw):
                return nc.scalar.activation(out_, in_, ACT.Copy, **kw)

            def std_of(n, out_=std, in_=var_e):
                act.wait_ge(var_ready, n)
                nc.scalar.activation(out_, in_, ACT.Sqrt).then_inc(std_ready, 1)

            def load_chunk(c, s, norm):
                for t in range(TPC):
                    for q in range(NQ):
                        act.wait_ge(quarter_in[q], (c * TPC + t) * 16 + 16)
                        wait(act, deg_used, (c * TPC + t) * NQ + (q - 1))
                        copy(quarter16[:, q % 2, :], quarter[:, q, :]).then_inc(cast16_done, 1)
                        if norm and (t, q) == (0, 1):
                            std_of(c)
                        if norm and (t, q) == (1, 0):
                            act.wait_ge(lncol_ready, c)
                        if norm and t in (1, 2) and q % 2 == 0:
                            h0_tile(c - 1, 1 - s, (t - 1) * 2 + q // 2)

            def h0_tile(c, s, t):
                nc.scalar.activation(feat32[:, bass.ds(c * TPC + t, 1), :], x_ring[:, s, t:t + 1, :], ACT.Relu,
                                     bias=shift_c[:, t:t + 1], scale=scale_c[:, t:t + 1]).then_inc(h0_done, 1)

            load_chunk(0, 0, False)
            load_chunk(1, 1, True)
            with act.Fori(1, H) as r:
                for s in range(2):
                    load_chunk(r * 2 + s, s, True)
            std_of(NC)
            act.wait_ge(lncol_ready, NC)
            for t in range(TPC):
                h0_tile(NC - 1, 1, t)
            std_of(NC + 1, deg_std, deg1)
            act.wait_ge(wa_ps_ready, 1)
            copy(wa_sb[:, :, :], ps[:, 7, 0:2 * FB].rearrange("p (k s) -> p k s", s=2)).then_inc(wa_ready, 1)

            def split_hi(base, j):
                act.wait_ge(scaled_ready, base + j + 1)
                copy(parts[:, j, 0, :], hs32[:, j % 2, :]).then_inc(hi_split, 1)

            act.wait_ge(cast8_done, NT * NQ)
            for l in range(4):

                def stage_groups(c, lo, hi):
                    for g in range(lo, hi):
                        n = c * GROUPS + (l * LG + g)
                        wait(act, group_done, n - (STAGES - 1))
                        copy(stage[:, g % STAGES, :, :],
                             adj8[:, g * PANELS:(g + 1) * PANELS, bass.ts(c, CH)]).then_inc(panel_ready, 1)

                def evac(c, e, s):
                    if e == 0:
                        wait(act, out_ready, c * TPC + l * NT)
                    if l in (1, 2) and e == 0:
                        act.wait_ge(ht1_ready, c + (NC * (l - 1) + 1))
                        bank = 4
                    else:
                        half = GROUPS // 2 if (l == 0 and e == 0) else GROUPS
                        act.wait_ge(group_done, c * GROUPS + (l * LG + half))
                        bank = 2 * e if l == 0 else 2 * s
                    copy(T_sb[:, 2 * e:2 * e + 2, :], ps[:, bank:bank + 2, :]).then_inc(evac_done, 1)

                def post_std(c):
                    if l != 1:
                        std_of(c + (NC + 2 + HI_BASE[l] // TPC))

                def post(c, s, cc, tiles):
                    if tiles[0] == 0:
                        wait(act, h_out[s], cc * 16 + 16 * H * l)
                    for t in tiles:
                        if l == 1:
                            act.wait_ge(out_ready, c * TPC + (NT + (t | 1) + 1))
                            nc.scalar.activation(g_ring[:, s, t, :], out_slot(t), ACT.Relu, scale=1.0 / SC)\
                              .then_inc(out_used[1], 1)
                        else:
                            act.wait_ge(hs_ready, c * TPC + (HI_BASE[l] + t + 1))
                            nc.scalar.activation(h_ring[:, s, t, 0, :], hs32[:, t % 2, :], ACT.Relu)\
                              .then_inc(hi_ready, 1)

                def chunk(c, s, cc_prev, last=False):
                    stage_groups(c, 4, 12)
                    if EVACS[l] == 2:
                        evac(c, 0, s)
                    stage_groups(c, 12, 14)
                    if cc_prev is not None:
                        post_std(c - 1)
                    stage_groups(c, 14, 16)
                    if cc_prev is not None:
                        post(c - 1, 1 - s, cc_prev, (0, 1))
                    if not last:
                        stage_groups(c + 1, 0, 2)
                    if cc_prev is not None:
                        post(c - 1, 1 - s, cc_prev, (2, 3))
                    if not last:
                        stage_groups(c + 1, 2, 4)
                    evac(c, EVACS[l] - 1, s)

                if l in (0, 2):
                    stage_groups(0, 0, 2)
                    for g in range(GROUPS):
                        for t in range(PANELS):
                            split_hi(0 if l == 0 else NT, g * PANELS + t)
                        if 0 < g < GROUPS - 1:
                            stage_groups(0, g + 1, g + 2)
                        if g == GROUPS // 2 + 2:
                            evac(0, 0, 0)
                    stage_groups(1, 0, 4)
                    evac(0, 1, 0)
                else:
                    stage_groups(0, 0, 4)
                    chunk(0, 0, None)
                chunk(1, 1, 0)
                chunk(2, 0, 0)
                with act.Fori(1, H - 1) as r:
                    chunk(r * 2 + 1, 1, r)
                    chunk(r * 2 + 2, 0, r)
                chunk(NC - 1, 1, H - 1, last=True)
                post_std(NC - 1)
                post(NC - 1, 1, H - 1, range(TPC))

            def ht_copy(c):
                act.wait_ge(ht_ready, c + 1)
                k = 2 * (c % 2)
                copy(T_all[:, c, :, :], ps[:, k:k + 2, :]).then_inc(ht_evac, 1)

            act.wait_ge(panel_ready, 4 * LG)
            for c in range(NC):
                ht_copy(c)
            act.wait_ge(out_ready, 4 * NT)
            for c in range(NC):
                act.wait_ge(vb_ps_ready, c + 1)
                copy(t_row[:, c * CH:(c + 1) * CH], ps[:, c % 2, :]).then_inc(vb_evac, 1)
            for j in range(NT):
                act.wait_ge(y_ps_ready, j + 1)
                copy(Yb[:, j, :, 0:F], ps[:, 4 + j % 2, :].rearrange("p (s f) -> p s f", s=2),
                     scale=1.0 / SC).then_inc(y_evac, 1)

            def rows_copy(s, n):
                act.wait_ge(ab_ps_ready, n)
                copy(AB[:, 2 * s:2 * s + 2, :], ps[:, 4 * s:4 * s + 2, :]).then_inc(ab_ready, 1)

            def averages(c, s):
                act.wait_ge(rz_ready, c * 2 + (s + 1))
                if s == 0:
                    wait(act, fin_out, c * 16)
                else:
                    wait(act, fin_ready, c)
                for t in range(TPC):
                    nc.scalar.activation(R[:, s, t, :], ps[:, 4 * s + t, 0:F], ACT.Copy, scale=rz[:, s, t:t + 1])\
                      .then_inc(att_evac, 1)

            def elu_exp(c):
                D, M = R[:, 0, :, :], R[:, 1, :, :]
                act.wait_ge(elu_in, c + 1)
                nc.scalar.activation(M, D, ACT.Relu, scale=-1.0).then_inc(neg_ready, 1)
                nc.scalar.activation(D, D, ACT.Relu)
                act.wait_ge(neg_ready, c + 1)
                nc.scalar.activation(M, M, ACT.Exp, scale=-1.0).then_inc(elu_out, 1)

            def store_result(c):
                act.wait_ge(fin_ready, c + 1)
                act.dma_start(chunk_rows(out, c), R[:, 0, :, :]).then_inc(fin_out, 16)

            def load_x3(c):
                act.dma_start(x3, chunk_rows(xs, c)).then_inc(x3_in, 16)

            def mask_exponents(c, g):
                act.wait_ge(mask_in[g], c * 16 + 16)
                m = mask[:, g * TPC:(g + 1) * TPC, :]
                copy(m, m, scale=BIG, bias=-BIG).then_inc(mask_ready, 1)

            def att_chunk(c, first, last):
                for s in range(2):
                    for j in range(NT):
                        if j % 2 == 0:
                            act.wait_ge(lin_ready, c * NT + (s * NT + j) // 2 + 1)
                        nc.scalar.activation(E[:, j % RING, :], E[:, j % RING, :], ACT.Exp, bias=v_2[:, s, j:j + 1])\
                          .then_inc(p_ready, 1)
                        if s == 0 and j % TPC == 0 and j // TPC + 1 < NC:
                            mask_exponents(c, j // TPC + 1)
                        if s == 1 and j == NT - 1 and not last:
                            mask_exponents(c + 1, 0)
                        if s == 0:
                            if j == 9 and not first:
                                averages(c - 1, 1)
                            if j == 14:
                                wait(act, lin_ready, c * NT)
                                rows_copy(1, c * 2 + 2)
                            if j == 22 and not first:
                                elu_exp(c - 1)
                            if j == 28 and not first:
                                store_result(c - 1)
                                load_x3(c)
                        else:
                            if j == 9:
                                averages(c, 0)
                            if j == NT - 1 and not last:
                                rows_copy(0, c * 2 + 3)

            act.wait_ge(cols_ready, 1)
            mask_exponents(0, 0)
            load_x3(0)
            rows_copy(0, 1)
            att_chunk(0, True, False)
            with act.Fori(1, NC - 1) as c:
                att_chunk(c, False, False)
            att_chunk(NC - 1, False, True)
            averages(NC - 1, 1)
            elu_exp(NC - 1)
            store_result(NC - 1)
            act.wait_ge(fin_out, 16 * NC)

        @block.vector
        def _(dve):
            steps = [0]

            class Chain:
                def __init__(self, turn, per_turn):
                    self.turn, self.per_turn, self.k = turn, per_turn, 0

                def link(self, ins):
                    self.k += 1
                    ins.then_inc(dve_step, 1)
                    dve.wait_ge(dve_step, self.turn * self.per_turn + (steps[0] + self.k))

                def end(self, turns):
                    assert self.k == self.per_turn or turns == 1
                    steps[0] += self.k * turns

            def mean_and_variance(t, link):
                link(nc.vector.bn_aggr(mv[:, t, :], stat[:, t, :]))

            def last_variance(link):
                t = TPC - 1
                nc.vector.tensor_scalar(var_e[:, 0:t], var_c[:, 0:t], EPS, None, ALU.add)
                mean_and_variance(t, link)
                nc.vector.tensor_scalar(var_e[:, t:TPC], var_c[:, t:TPC], EPS, None, ALU.add).then_inc(var_ready, 1)

            def one_over_root(n, value, root, est, link):
                dve.wait_ge(std_ready, n)
                link(nc.vector.reciprocal(est, root))
                link(nc.vector.tensor_tensor(root, est, est, ALU.mult))
                link(nc.vector.tensor_tensor(root, root, value, ALU.mult))
                link(nc.vector.tensor_scalar(root, root, -0.5, 1.5, ALU.mult, ALU.add))
                return root

            def norm_columns(c, ch):
                left = one_over_root(c + 1, var_e, std, rough, ch.link)
                wait(dve, h0_done, c * TPC)
                ch.link(nc.vector.tensor_tensor(scale_c, rough, left, ALU.mult))
                nc.vector.scalar_tensor_tensor(shift_c, mean_c, -1.0, scale_c, ALU.mult, ALU.mult)\
                  .then_inc(lncol_ready, 1)
                dve.wait_ge(lncol_ready, c + 1)

            def load_chunk(c, s, cc, ch, norm=True):
                for t in range(TPC):
                    for q in range(NQ):
                        dve.wait_ge(quarter_in[q], (c * TPC + t) * 16 + 16)
                        nc.vector.tensor_copy(adj8[:, bass.ds(c * TPC + t, 1), q * QW:(q + 1) * QW],
                                              quarter[:, q:q + 1, :]).then_inc(cast8_done, 1)
                    if t > 0:
                        mean_and_variance(t - 1, ch.link)
                    else:
                        if norm:
                            norm_columns(c - 1, ch)
                        dve.wait_ge(x_in_s[s], cc * 16 + 16)
                    ch.link(nc.vector.bn_stats(stat[:, t, :], x_ring[:, s, t, :]))
                last_variance(ch.link)

            PER0 = 2 * (2 * TPC + 5)
            ch = Chain(0, 0)
            for s in range(2):
                load_chunk(s, s, 0, ch, norm=(s == 1))
            ch.end(1)
            with dve.Fori(0, H - 1) as r:
                ch = Chain(r, PER0)
                for s in range(2):
                    load_chunk(r * 2 + (s + 2), s, r + 1, ch)
            ch.end(H - 1)

            ch = Chain(0, 0)
            norm_columns(NC - 1, ch)
            dve.wait_ge(deg_done, 1)
            ch.link(nc.vector.tensor_scalar(dsc[:, :], ps[:, 6, 0:NT], 1.0, None, ALU.add))
            nc.vector.tensor_scalar(lone[:, :], dsc[:, :], 1.0, None, ALU.is_equal)
            nc.vector.tensor_scalar(deg1, dsc[:, :], 1e-30, None, ALU.max).then_inc(var_ready, 1)
            left = one_over_root(NC + 1, deg1, deg_std, fac[:, :], ch.link)
            ch.link(nc.vector.tensor_tensor(fac[:, :], fac[:, :], left, ALU.mult))
            ch.link(nc.vector.scalar_tensor_tensor(dinv[:, :], dsc[:, :], 0.0, fac[:, :], ALU.is_gt, ALU.mult))
            ch.link(nc.vector.tensor_scalar(fac[:, :], dinv[:, :], SC, None, ALU.mult))
            ch.link(nc.vector.tensor_scalar(dsc[:, :], dinv[:, :], 1.0 / SC, None, ALU.mult))
            ch.end(1)

            def split(base, column):
                def turn(r, first):
                    for t in range(2):
                        if not first:
                            dve.wait_ge(split_done, r * 2 + (base + t - 1))
                        nc.vector.tensor_scalar(hs32[:, t:t + 1, :], feat32[:, bass.ds(r * 2 + t, 1), :],
                                                column(r * 2 + t), None, ALU.mult).then_inc(scaled_ready, 1)
                    for t in range(2):
                        dve.wait_ge(hi_split, r * 2 + (base + t + 1))
                        nc.vector.tensor_tensor(parts[:, bass.ds(r * 2 + t, 1), 1, :], hs32[:, t:t + 1, :],
                                                parts[:, bass.ds(r * 2 + t, 1), 0, :], ALU.subtract)\
                          .then_inc(split_done, 1)

                turn(0, True)
                with dve.Fori(1, NT // 2) as r:
                    turn(r, False)

            for l in range(4):
                if l == 0:
                    dve.wait_ge(h0_done, NT)
                    split(0, lambda j: fac[:, bass.ds(j, 1)])
                if l == 2:
                    ch = Chain(0, 0)
                    dve.wait_ge(post_done, 2 * NC)
                    ch.link(nc.vector.tensor_reduce(g_own, gmax[:, :], AX.X, ALU.max))
                    nc.vector.tensor_scalar(g_own, g_own, 1e-30, None, ALU.max).then_inc(gown_ready, 1)
                    dve.wait_ge(gall_ready, 1)
                    ch.link(nc.vector.tensor_scalar(g_pow.bitcast(i32), g_all.bitcast(i32), 0x7F800000, None,
                                                    ALU.bitwise_and))
                    ch.link(nc.vector.reciprocal(g_scale, g_pow))
                    ch.link(nc.vector.tensor_scalar(g_inv, g_pow, 2.0 ** -14, None, ALU.mult))
                    ch.link(nc.vector.tensor_scalar(g_scale, g_scale, 2.0 ** 14, None, ALU.mult))
                    ch.end(1)
                    for c in range(NC):
                        dve.wait_ge(parts_in[c], 32)
                    split(NT, lambda j: g_scale)
                if l in (0, 3):
                    dve.wait_ge(weights_in, W_NEEDED[l])

                PER = {0: 5 * TPC + 5, 1: 0, 2: 4 * TPC + 5, 3: 4 * TPC + 5}[l] * 2

                def post(c, s, cc, ch):
                    i0 = c * TPC
                    if l == 1:
                        for t in range(TPC):
                            dve.wait_ge(out_used[1], i0 + (t + 1))
                            ins = nc.vector.tensor_reduce(gmax[:, bass.ds(i0 + t, 1)], g_ring[:, s, t, :], AX.X, ALU.max)
                        ins.then_inc(post_done, 1)
                        return
                    dve.wait_ge(x_in_s[s], cc * 16 + 16 * (X_USES[l] * H + 1))
                    for t in range(TPC):
                        x_t, y_t, o_t = x_ring[:, s, t, :], y_tmp, out_slot(t)
                        dve.wait_ge(out_ready, i0 + (NT * l + (t | 1) + 1))
                        if l == 2:
                            nc.vector.tensor_scalar(y_t, o_t, g_inv, 0.0, ALU.mult, ALU.max).then_inc(out_used[l], 1)
                        else:
                            nc.vector.scalar_tensor_tensor(y_t, o_t, dsc[:, bass.ds(i0 + t, 1)], bias_row,
                                                           ALU.mult, ALU.add).then_inc(out_used[l], 1)
                        if t > 0:
                            mean_and_variance(t - 1, ch.link)
                        dve.wait_ge(out_used[l], i0 + (t + 1))
                        if l == 0:
                            ch.link(nc.vector.scalar_tensor_tensor(y_t, y_t, 0.01, y_t, ALU.mult, ALU.max))
                        if l == 3:
                            ch.link(nc.vector.scalar_tensor_tensor(x_t, y_t, 0.0, x_t, ALU.max, ALU.add))
                        else:
                            ch.link(nc.vector.tensor_tensor(x_t, y_t, x_t, ALU.add))
                        ch.link(nc.vector.bn_stats(stat[:, t, :], x_t))
                    last_variance(ch.link)
                    left = one_over_root(c + (NC + 2 + HI_BASE[l] // TPC), var_e, std, rough, ch.link)
                    ch.link(nc.vector.scalar_tensor_tensor(scale_c, rough, SC, left, ALU.mult, ALU.mult))
                    if l == 2:
                        ch.link(nc.vector.tensor_tensor(scale_c, scale_c, dinv[:, bass.ds(i0, TPC)], ALU.mult))
                    ch.link(nc.vector.scalar_tensor_tensor(shift_c, mean_c, -1.0, scale_c, ALU.mult, ALU.mult))

                    def scaled(t):
                        wait(dve, hi_ready, i0 + (HI_BASE[l] + t - 1))
                        nc.vector.tensor_scalar(hs32[:, t % 2, :], x_ring[:, s, t, :], scale_c[:, t:t + 1],
                                                shift_c[:, t:t + 1], ALU.mult, ALU.add).then_inc(hs_ready, 1)

                    scaled(0)
                    for t in range(TPC):
                        if t + 1 < TPC:
                            scaled(t + 1)
                        dve.wait_ge(hi_ready, i0 + (HI_BASE[l] + t + 1))
                        lo = nc.vector.scalar_tensor_tensor(h_ring[:, s, t, 1, :], hs32[:, t % 2, :], 0.0,
                                                            h_ring[:, s, t, 0, :], ALU.max, ALU.subtract)
                        if t + 1 < TPC:
                            ch.link(lo)
                    lo.then_inc(post_done, 1)

                if l == 2:
                    PER += 2
                ch = Chain(0, PER)
                for s in range(2):
                    post(s, s, 0, ch)
                ch.end(1)
                with dve.Fori(0, H - 1) as r:
                    ch = Chain(r, PER)
                    for s in range(2):
                        post(r * 2 + (2 + s), s, r + 1, ch)
                ch.end(H - 1)

            for c in range(NC):
                dve.wait_ge(ht_evac, c + 1)
                nc.vector.tensor_reduce(hsum[:, :, c:c + 1], T_all[:, c, :, :], AX.X, ALU.add).then_inc(ht_summed, 1)
            ch = Chain(0, 0)
            dve.wait_ge(ht_summed, NC)
            nc.vector.tensor_reduce(hsum1[:, :], hsum[:, :, :], AX.X, ALU.add).then_inc(hsum_ready, 1)
            dve.wait_ge(scores_done, NC)
            nc.vector.tensor_scalar(uv_sb[:, :, :], ps[:, 7, 0:2 * NT].rearrange("p (j s) -> p j s", s=2),
                                    1.0 / SC, None, ALU.mult).then_inc(uv_ready, 1)
            dve.wait_ge(uv_ready, 1)
            nc.vector.tensor_copy(u_col, uv_sb[:, :, 0])
            for s in range(2):
                sign = 1.0 - 2.0 * s
                nc.vector.tensor_scalar(v_8[:, s, :], uv_sb[:, :, 1], 0.8 * sign, None, ALU.mult)
                ins = nc.vector.tensor_scalar(v_2[:, s, :], uv_sb[:, :, 1], 0.2 * sign, None, ALU.mult)
            ins.then_inc(cols_ready, 1)
            for c in range(NC):
                dve.wait_ge(vb_evac, c + 1)
                nc.vector.tensor_reduce(vext[:, 0, c:c + 1], t_row[:, c * CH:(c + 1) * CH], AX.X, ALU.max)
                ins = nc.vector.tensor_reduce(vext[:, 1, c:c + 1], t_row[:, c * CH:(c + 1) * CH], AX.X, ALU.min)
            ch.link(ins)
            nc.vector.tensor_reduce(v_hi, vext[:, 0, :], AX.X, ALU.max)
            ch.link(nc.vector.tensor_reduce(v_lo, vext[:, 1, :], AX.X, ALU.min))
            ch.link(nc.vector.tensor_tensor(v_rng, v_hi, v_lo, ALU.subtract))
            ch.link(nc.vector.tensor_scalar(v_rng, v_rng, 1e-30, None, ALU.max))
            nc.vector.tensor_scalar(v_R, v_rng, 2.0, None, ALU.mult)
            nc.vector.tensor_scalar(v_nR, v_rng, -2.0, None, ALU.mult)
            ch.link(nc.vector.reciprocal(v_r, v_rng))
            nc.vector.scalar_tensor_tensor(v_c1, v_R, -0.25, v_lo, ALU.mult, ALU.add)
            nc.vector.scalar_tensor_tensor(v_c2, v_R, 0.75, v_lo, ALU.mult, ALU.add)
            ch.link(nc.vector.tensor_scalar(v_r, v_r, 0.5, None, ALU.mult))
            ch.link(nc.vector.tensor_scalar(t_row, t_row, v_c1, v_r, ALU.subtract, ALU.mult))
            dve.wait_ge(my_ps_ready, 1)
            ch.link(nc.vector.tensor_scalar(mean_y, ps[:, 6, 0:F], 1.0 / (SC * N), None, ALU.mult))
            nc.vector.scalar_tensor_tensor(mean_y, ps[:, 6, F:2 * F], -1.0 / (SC * N), mean_y, ALU.mult, ALU.add)\
              .then_inc(my_ready, 1)
            ch.end(1)

            def extreme(t, h, low):
                if not low:
                    nc.vector.tensor_tensor_reduce(out=junk, in0=rows[:, h, :], in1=t_row[:, h * HALF:(h + 1) * HALF],
                                                   scale=1.0, scalar=0.0, op0=ALU.mult, op1=ALU.max,
                                                   accum_out=tmx[:, t, h:h + 1]).then_inc(row_used, 1)
                else:
                    nc.vector.tensor_tensor_reduce(out=junk, in0=rows[:, h, :], in1=t_row[:, h * HALF:(h + 1) * HALF],
                                                   scale=1.0, scalar=-1.0, op0=ALU.subtract, op1=ALU.max,
                                                   accum_out=tmn[:, t, h:h + 1]).then_inc(row_used, 1)

            def shifts(c, ch):
                vM, vm, s_p, s_n, l_p, l_n = (ccol[:, 4:5, :], ccol[:, 5:6, :], ccol[:, 4:5, :], ccol[:, 5:6, :],
                                              ccol[:, 6:7, :], ccol[:, 7:8, :])
                u = u_col[:, bass.ds(c * TPC, TPC)].rearrange("p (a t) -> p a t", a=1)
                dve.wait_ge(row_used, c * 4 * TPC + 4 * TPC)
                dve.wait_ge(ab_ps_ready, c * 2) if not (isinstance(c, int) and c == 0) else None
                nc.vector.tensor_tensor(vM, tmx[:, :, 0:1].rearrange("p t a -> p a t"),
                                        tmx[:, :, 1:2].rearrange("p t a -> p a t"), ALU.max)
                ch.link(nc.vector.tensor_tensor(vm, tmn[:, :, 0:1].rearrange("p t a -> p a t"),
                                                tmn[:, :, 1:2].rearrange("p t a -> p a t"), ALU.max))
                nc.vector.tensor_scalar(vM, vM, v_R, v_c1, ALU.mult, ALU.add)
                ch.link(nc.vector.tensor_scalar(vm, vm, v_nR, v_c2, ALU.mult, ALU.add))
                nc.vector.tensor_tensor(s_p, vM, u, ALU.add)
                ch.link(nc.vector.tensor_tensor(s_n, vm, u, ALU.add))
                nc.vector.scalar_tensor_tensor(l_p, s_p, 0.2, s_p, ALU.mult, ALU.max)
                ch.link(nc.vector.scalar_tensor_tensor(l_n, s_n, 0.2, s_n, ALU.mult, ALU.max))
                nc.vector.tensor_tensor(ccol[:, 0:1, :], u, l_p, ALU.subtract)
                nc.vector.scalar_tensor_tensor(ccol[:, 1:2, :], u, 0.2, l_p, ALU.mult, ALU.subtract)
                nc.vector.tensor_tensor(ccol[:, 2:3, :], l_n, u, ALU.subtract)
                nc.vector.scalar_tensor_tensor(ccol[:, 3:4, :], u, -0.2, l_n, ALU.mult, ALU.add).then_inc(cc_ready, 1)

            def reciprocals(c, s, ch):
                dve.wait_ge(p_used, c * 2 * NT + (s + 1) * NT)
                z = rz[:, s, :].rearrange("p (t a) -> p t a", a=1)
                ch.link(nc.vector.tensor_tensor(z, ps[:, 4 * s:4 * s + 4, F:YW],
                                                lone[:, bass.ds(c * TPC, TPC)].rearrange("p (t a) -> p t a", a=1),
                                                ALU.add))
                if s == 1:
                    ch.link(nc.vector.tensor_scalar(z, z, -1.0, None, ALU.mult))
                nc.vector.reciprocal(z, z).then_inc(rz_ready, 1)

            SEARCHES = 4 * TPC
            LAST = NT - 3
            search_at = {m * LAST // (SEARCHES - 1): m for m in range(SEARCHES)}

            def att_chunk(c, ch, first, last):
                for s in range(2):
                    edge = ALU.max if s == 0 else ALU.min
                    dve.wait_ge(ab_ready, c * 2 + (s + 1))
                    for pair in range(NT // 2 + 1):
                        n = s * (NT // 2) + pair
                        m = search_at.get(n) if pair < NT // 2 and not last else None
                        if m is not None:
                            dve.wait_ge(row_used, c * SEARCHES + (SEARCHES + m))
                            if m % 2 == 0:
                                dve.wait_ge(row_in[m // 2 % 2], (c * TPC + (TPC + m // 4)) * 16 + 16)
                        if pair == 4:
                            if s == 1:
                                reciprocals(c, 0, ch)
                            elif not first:
                                reciprocals(c - 1, 1, ch)
                        if n == LAST + 1 and not last:
                            shifts(c + 1, ch)
                        if pair < NT // 2:
                            for j in (2 * pair, 2 * pair + 1):
                                k = s * NT + j
                                if not (first and k < RING):
                                    dve.wait_ge(p_used, c * 2 * NT + (k - RING + 1))
                                ins = nc.vector.scalar_tensor_tensor(E[:, j % RING, :], AB[:, 2 * s, :],
                                                                     v_8[:, s, j:j + 1], AB[:, 2 * s + 1, :],
                                                                     ALU.add, edge)
                            ins.then_inc(edge_ready, 1)
                        if pair >= 1:
                            i = 2 * (pair - 1)
                            if s == 0 and i % TPC == 0:
                                dve.wait_ge(mask_ready, c * NC + (i // TPC + 1))
                            dve.wait_ge(edge_ready, c * NT + (s * NT // 2 + pair))
                            slots = E[:, i % RING:i % RING + 2, :]
                            nc.vector.tensor_tensor(slots, mask[:, i:i + 2, :], slots, ALU.add).then_inc(lin_ready, 1)
                        if m is not None:
                            extreme(m // 4, m // 2 % 2, m % 2)

            for t in range(TPC):
                for h in range(2):
                    dve.wait_ge(row_in[h], t * 16 + 16)
                    wait(dve, row_used, 4 * t + 2 * h)
                    extreme(t, h, 0)
                    dve.wait_ge(row_used, 4 * t + 2 * h + 1)
                    extreme(t, h, 1)
            ch = Chain(0, 0)
            shifts(0, ch)
            att_chunk(0, ch, True, False)
            ch.end(1)
            with dve.Fori(1, NC - 1) as c:
                ch = Chain(c - 1, 8 - 1)
                att_chunk(c, ch, False, False)
            ch.end(NC - 2)
            ch = Chain(0, 0)
            att_chunk(NC - 1, ch, False, True)
            reciprocals(NC - 1, 1, ch)
            ch.end(1)

        @block.tensor
        def _(pe):
            mm = nc.tensor.matmul

            pe.wait_ge(small_in, 32)
            for k in range(FB):
                for f in range(FB):
                    ins = mm(ps[:, 7, 2 * k:2 * k + 2], w3t_sb[:, f, k * P:(k + 1) * P], a_sb[:, f, :],
                             start=(f == 0), stop=(f == FB - 1))
            ins.then_inc(wa_ps_ready, 1)
            pe.wait_ge(consts_ready, 3)
            mm(ps[:, 6, 0:NT], strip[:, 0, :], strip[:, 0, 0:NT], start=True, stop=False, skip_group_check=True)

            with pe.Fori(0, NT) as j:
                for q in range(NQ):
                    pe.wait_ge(cast16_done, j * NQ + (q + 1))
                    for b in range(QW // P):
                        t = q * (QW // P) + b
                        ins = mm(ps[:, 6, t:t + 1], quarter16[:, q % 2, b * P:(b + 1) * P], ones16[:, :],
                                 start=False, stop=False, skip_group_check=True)
                    ins.then_inc(deg_used, 1)
            mm(ps[:, 6, 0:NT], strip[:, 0, :], strip[:, 0, 0:NT], start=False, stop=True,
               skip_group_check=True).then_inc(deg_done, 1)

            for l in range(4):
                def main(c, s, g, split_waits):
                    pe.wait_ge(panel_ready, c * GROUPS + (l * LG + g + 1))
                    for jj in range(PANELS):
                        j = g * PANELS + jj
                        if split_waits:
                            if l in (0, 2):
                                pe.wait_ge(split_done, (0 if l == 0 else NT) + j + 1)
                            elif j % TPC == 0:
                                pe.wait_ge(parts_in[j // TPC], 16 if l == 1 else 48)
                        if l == 0:
                            bank, fresh, end = (0, j == 0, j == NT // 2 - 1) if j < NT // 2 else (2, j == NT // 2, j == NT - 1)
                        else:
                            bank, fresh, end = 2 * s, j == 0, j == NT - 1
                        for f in range(FB):
                            for h in range(2):
                                ins = mm(ps[:, bank + f, :], parts[:, j, h, f * P:(f + 1) * P],
                                         stage[:, g % STAGES, jj, :], start=(fresh and h == 0),
                                         stop=(end and h == 1), skip_group_check=True)
                    ins.then_inc(group_done, 1)

                def own_tiles(c, bank, eye_slot, fresh):
                    for t in range(TPC):
                        for f in range(FB):
                            for h in range(2):
                                ins = mm(ps[:, bank + f, t * P:(t + 1) * P],
                                         parts[:, bass.ds(c * TPC + t, 1), h, f * P:(f + 1) * P].rearrange("p a f -> p (a f)"),
                                         strip[:, bass.ds(eye_slot, 1), :].rearrange("p a f -> p (a f)"),
                                         start=(fresh and h == 0), stop=(fresh and h == 1), skip_group_check=True)
                    return ins

                def project(c, prev_layer):
                    pe.wait_ge(evac_done, c * EVACS[l] + (EVAC_BASE[l] + EVACS[l]))
                    for t in range(TPC):
                        if not prev_layer:
                            pe.wait_ge(out_used[l], c * TPC + ((t | 1) - TPC + 1))
                        elif l > 0:
                            pe.wait_ge(out_used[l - 1], NT)
                        for k in range(KB[l]):
                            ins = mm(out_slot(t), T_sb[:, k, t * P:(t + 1) * P], w_sb[:, k, :],
                                     start=(k == 0), stop=(k == KB[l] - 1), skip_group_check=True)
                        ins.then_inc(out_ready, 1)

                def chunk(c, s, first, prev):
                    if l == 0:
                        if not first:
                            pe.wait_ge(evac_done, c * 2 - 1)
                    elif not first:
                        if l in (1, 2):
                            pe.wait_ge(evac_done, c * 2 + (EVAC_BASE[l] - 1))
                        if not (isinstance(c, int) and c < 2):
                            pe.wait_ge(evac_done, c * EVACS[l] + (EVAC_BASE[l] - EVACS[l]))
                    for g in range(GROUPS // 2):
                        main(c, s, g, first)
                        if g == TPC // PANELS - 1:
                            if l == 0:
                                own_tiles(c, 0, c + 4, False)
                            if l in (1, 2):
                                own_tiles(c, 4, 4, True).then_inc(ht1_ready, 1)
                            if l == 3:
                                own_tiles(c, 2 * s, 4, False)
                    if prev is not None:
                        project(c - 1, prev)
                    if l == 0 and not first:
                        pe.wait_ge(evac_done, c * 2)
                    for g in range(GROUPS // 2, GROUPS):
                        main(c, s, g, first)
                        if l == 0 and g == GROUPS // 2:
                            own_tiles(c, 2, c, False)

                chunk(0, 0, True, None)
                pe.wait_ge(weights_in, W_NEEDED[l])
                chunk(1, 1, False, True)
                chunk(2, 0, False, False)
                with pe.Fori(1, H - 1) as r:
                    chunk(r * 2 + 1, 1, False, False)
                    chunk(r * 2 + 2, 0, False, False)
                chunk(NC - 1, 1, False, False)
                project(NC - 1, False)

            def transposed(c):
                pe.wait_ge(parts_in[c], 64)
                if c >= 2:
                    pe.wait_ge(ht_evac, c - 1)
                k = 2 * (c % 2)
                for t in range(TPC):
                    for f in range(FB):
                        for h in range(2):
                            ins = mm(ps[:, k + f, t * P:(t + 1) * P], parts[:, c * TPC + t, h, f * P:(f + 1) * P],
                                     ident16, start=(h == 0), stop=(h == 1), skip_group_check=True)
                ins.then_inc(ht_ready, 1)

            def scores(c):
                pe.wait_ge(ht_evac, c + 1)
                for t in range(TPC):
                    j = c * TPC + t
                    for k in range(FB):
                        ins = mm(ps[:, 7, 2 * j:2 * j + 2], T_all[:, c, k, t * P:(t + 1) * P], wa_sb[:, k, :],
                                 start=(k == 0), stop=(k == FB - 1), skip_group_check=True)
                ins.then_inc(scores_done, 1)

            def projected(j):
                if j >= 2:
                    pe.wait_ge(y_evac, j - 1)
                c, t = j // TPC, j % TPC
                for k in range(FB):
                    ins = mm(ps[:, 4 + j % 2, :], T_all[:, c, k, t * P:(t + 1) * P], wt_sb[:, k, :],
                             start=(k == 0), stop=(k == FB - 1), skip_group_check=True)
                ins.then_inc(y_ps_ready, 1)

            def spread(out_, column):
                return mm(out_, column.to_broadcast([P, P]), ident32[:, :], start=True, stop=True,
                          skip_group_check=True)

            pe.wait_ge(weights_in, W_NEEDED[4])
            pe.wait_ge(wa_ready, 1)
            pe.wait_ge(out_used[3], NT)
            transposed(0)
            for c in range(NC):
                if c + 1 < NC:
                    transposed(c + 1)
                scores(c)
            pe.wait_ge(hsum_ready, 1)
            for k in range(FB):
                ins = mm(ps[:, 6, :], hsum1[:, k:k + 1].to_broadcast([P, P]), wt_sb[:, k, :],
                         start=(k == 0), stop=(k == FB - 1), skip_group_check=True)
            ins.then_inc(my_ps_ready, 1)
            pe.wait_ge(uv_ready, 1)
            for c in range(NC):
                if c >= 2:
                    pe.wait_ge(vb_evac, c - 1)
                for t in range(TPC):
                    ins = spread(ps[:, c % 2, t * P:(t + 1) * P], uv_sb[:, c * TPC + t, 1:2])
                ins.then_inc(vb_ps_ready, 1)
            for j in range(NT):
                projected(j)

            def spread_rows(s, c):
                pe.wait_ge(cc_ready, c + 1)
                if not (isinstance(c, int) and c == 0):
                    pe.wait_ge(att_evac, c * 2 * TPC + TPC * (s - 1))
                for q in range(2):
                    for t in range(TPC):
                        ins = spread(ps[:, 4 * s + q, t * P:(t + 1) * P], ccol[:, 2 * s + q, t:t + 1])
                ins.then_inc(ab_ps_ready, 1)

            def att_chunk(c, last):
                for s in range(2):
                    pe.wait_ge(ab_ready, c * 2 + (s + 1))
                    for j in range(NT):
                        pe.wait_ge(p_ready, c * 2 * NT + (s * NT + j + 1))
                        for t in range(TPC):
                            ins = mm(ps[:, 4 * s + t, 0:YW], E[:, j % RING, t * P:(t + 1) * P], Yb[:, j, s, :],
                                     start=(j == 0), stop=(j == NT - 1), skip_group_check=True)
                        ins.then_inc(p_used, 1)
                        if s == 0 and j == 10:
                            spread_rows(1, c)
                        if s == 1 and j == 25 and not last:
                            spread_rows(0, c + 1)

            pe.wait_ge(vb_evac, NC)
            spread_rows(0, 0)
            pe.wait_ge(ones_set, 1)
            pe.wait_ge(y_evac, NT)
            att_chunk(0, False)
            with pe.Fori(1, NC - 1) as c:
                att_chunk(c, False)
            att_chunk(NC - 1, True)


def kernel(x, adj, L0_gnn_weightr, L0_gnn_weightd, L0_gnn_bias, L1_gnn_W1, L1_gnn_W2, L2_gnn_W, L2_gnn_b,
           L3_gnn_W, L3_gnn_a, L3_gnn_wtrans):
    import numpy as np
    import concourse.bacc as bacc
    from concourse.bass_utils import run_bass_kernel_spmd

    x, adj = np.asarray(x), np.asarray(adj)
    F = x.shape[1]
    arrays = {
        "x": x,
        "adj_t": np.ascontiguousarray(adj.T),
        "adj": adj,
        "w_gcn": np.concatenate([np.asarray(L0_gnn_weightr), np.asarray(L0_gnn_weightd)], axis=0),
        "b_gcn": np.asarray(L0_gnn_bias),
        "w_conv1": np.asarray(L1_gnn_W1),
        "w_conv2": np.asarray(L1_gnn_W2),
        "w_gcn2": np.ascontiguousarray(np.asarray(L2_gnn_W).T),
        "b_gcn2": np.asarray(L2_gnn_b),
        "w_att_t": np.ascontiguousarray(np.asarray(L3_gnn_W).T),
        "a_att": np.ascontiguousarray(np.asarray(L3_gnn_a).reshape(2, F).T),
        "w_trans": np.asarray(L3_gnn_wtrans),
    }
    nc = bacc.Bacc("TRN2", target_bir_lowering=False, num_devices=1)
    args = [nc.dram_tensor(f"in_{n}", a.shape, mybir.dt.from_np(a.dtype), kind="ExternalInput").ap()
            for n, a in arrays.items()]
    out = nc.dram_tensor("out", x.shape, mybir.dt.float32, kind="ExternalOutput").ap()
    gnn_stack(nc, *args, out)
    r = run_bass_kernel_spmd(nc, [{f"in_{n}": a for n, a in arrays.items()}], core_ids=[0])
    return r.results[0]["out"]
```

```python
import concourse.bass as bass
from concourse import mybir
from contextlib import ExitStack

P = 128


def gnn_stack(nc, x_in, adj_t, adj, w_gcn, b_gcn, w_conv1, w_conv2, w_gcn2, b_gcn2,
              w_att_t, a_att, w_trans, out):
    f32, f16, bf16, u8, i32 = (mybir.dt.float32, mybir.dt.float16, mybir.dt.bfloat16,
                               mybir.dt.uint8, mybir.dt.int32)
    ALU, ACT, AX = mybir.AluOpType, mybir.ActivationFunctionType, mybir.AxisListType

    N, F = x_in.shape
    NT = N // P
    CH = 512
    NC = N // CH
    TPC = CH // P
    FB = F // P
    PANELS = 2
    GROUPS = NT // PANELS
    STAGES = 4
    QW = 1024
    NQ = N // QW
    HALF = N // 2
    YW = F + 1
    RING = 8
    EPS = 1e-5
    SC = 2048.0
    BIG = 3e38
    EVACS = [2, 2, 2, 1]
    KB = [4, 4, 4, 2]
    EARLY = 6
    ROWS_AT = NT - 3
    WQ = 4

    xs = nc.dram_tensor("x_spill", (N, F), f32).ap()
    hs = nc.dram_tensor("h_spill", (N, F), f32).ap()

    def chunk_rows(t, c):
        return t.rearrange("(c t p) f -> c p t f", p=P, t=TPC)[c, :, :, :]

    ctx = ExitStack()
    with ctx:
        def sb(name, shape, dt):
            return ctx.enter_context(nc.sbuf_tensor(name, shape, dt))

        def sem(name):
            return ctx.enter_context(nc.semaphore(name))

        Y_WORDS = NT * 2 * YW
        big = sb("big", [P, Y_WORDS + NT * CH], f32)
        feat = sb("feat", [P, NT * F], f32)
        work = sb("work", [P, 10240], f32)

        def words(t, lo, n):
            return t[:, lo:lo + n]

        adj8 = words(big, 0, N * NT // 4).bitcast(u8).rearrange("p (j n) -> p j n", j=NT)
        feat32 = feat[:, :].rearrange("p (j f) -> p j f", j=NT)
        parts = feat[:, :].bitcast(f16).rearrange("p (j h f) -> p j h f", j=NT, h=2)
        T_all = words(big, Y_WORDS + NT * CH // 2, NT * F).rearrange("p (c k n) -> p c k n", c=NC, k=FB)
        T_sb = words(work, 0, 2048).rearrange("p (k n) -> p k n", k=4)
        stage = words(work, 2048, 2048).bitcast(bf16).rearrange("p (s j n) -> p s j n", s=STAGES, j=PANELS)
        h_ring = words(work, 4096, 2048).bitcast(f16).rearrange("p (s t h f) -> p s t h f", s=2, t=TPC, h=2)
        g_ring = words(work, 4096, 2048).rearrange("p (s t f) -> p s t f", s=2, t=TPC)
        x_ring = words(work, 6144, 2048).rearrange("p (s t f) -> p s t f", s=2, t=TPC)
        w_sb = words(work, 8192, 1024).rearrange("p (k f) -> p k f", k=4)
        wa_rows = words(work, 8192 + 2 * F, 2 * F).rearrange("p (s f) -> p s f", s=2)
        bias_row = words(work, 9216, F)
        y_tmp = words(work, 9216 + F, F)
        hs32 = words(work, 9216 + 2 * F, 2 * F).rearrange("p (s f) -> p s f", s=2)
        quarter = words(work, 0, NQ * QW).rearrange("p (q n) -> p q n", q=NQ)
        quarter16 = words(work, 8192, QW).bitcast(bf16).rearrange("p (s n) -> p s n", s=2)
        Yb = words(big, 0, Y_WORDS).rearrange("p (j s f) -> p j s f", j=NT, s=2)
        mask = words(big, Y_WORDS, NT * CH).rearrange("p (j n) -> p j n", j=NT)
        wt_sb = words(work, 8192, 1024).rearrange("p (k f) -> p k f", k=FB)
        t_row = words(work, 0, 4096)
        E = words(work, 4096, RING * CH).rearrange("p (s n) -> p s n", s=RING)
        R = words(work, 8192, 2 * TPC * F).rearrange("p (s t f) -> p s t f", s=2, t=TPC)
        rows = words(feat, 0, 2 * HALF).rearrange("p (s n) -> p s n", s=2)
        AB = words(feat, 4096, WQ * CH).rearrange("p (q n) -> p q n", q=WQ)
        junk = words(feat, 6144, HALF // 4).bitcast(u8)
        mean_y = words(feat, 6656, F)
        x3 = words(feat, 6912, TPC * F).rearrange("p (t f) -> p t f", t=TPC)
        att_cols = words(feat, 7936, 256)
        u_col = att_cols[:, 0:NT]
        v_8 = att_cols[:, NT:3 * NT].rearrange("p (s j) -> p s j", s=2)
        v_2 = att_cols[:, 3 * NT:5 * NT].rearrange("p (s j) -> p s j", s=2)
        tmx = att_cols[:, 160:168].rearrange("p (t h) -> p t h", h=2)
        tmn = att_cols[:, 168:176].rearrange("p (t h) -> p t h", h=2)
        ccol = att_cols[:, 176:176 + 32].rearrange("p (q t) -> p q t", t=TPC)
        rz = att_cols[:, 208:216].rearrange("p (s t) -> p s t", s=2)
        zeros16 = sb("zeros16", [P, P], f16)
        ident16 = sb("ident16", [P, P], f16)
        ident32 = sb("ident32", [P, P], f32)
        w3t_sb = sb("w3t_sb", [P, FB, F], f32)
        a_sb = sb("a_sb", [P, FB, 2], f32)
        wa_sb = sb("wa_sb", [P, FB, 2], f32)
        ones16 = sb("ones16", [P, 1], bf16)
        dinv = sb("dinv", [P, NT], f32)
        fac = sb("fac", [P, NT], f32)
        dsc = sb("dsc", [P, NT], f32)
        lone = sb("lone", [P, NT], f32)
        gmax = sb("gmax", [P, NT], f32)
        uv_sb = sb("uv_sb", [P, NT, 2], f32)
        uv_cols = sb("uv_cols", [P, 2, NT], f32)
        stat = sb("stat", [P, TPC, 6], f32)
        mv = sb("mv", [P, TPC, 2], f32)
        mean_c, var_c = mv[:, :, 0], mv[:, :, 1]
        ln = sb("ln", [P, 5, TPC], f32)
        var_e, std, rough, scale_c, shift_c = (ln[:, k, :] for k in range(5))
        deg1, deg_std = uv_cols[:, 0, :], uv_cols[:, 1, :]
        sc = sb("sc", [P, 16], f32)
        g_own, g_all, g_pow, g_scale, g_inv = (sc[:, k:k + 1] for k in range(5))
        v_hi, v_lo, v_rng, v_r, v_R, v_c1, v_c2, v_nR = (sc[:, k:k + 1] for k in range(5, 13))
        vext = sb("vext", [P, 2, NC], f32)
        hsum = sb("hsum", [P, FB, NC], f32)
        hsum1 = sb("hsum1", [P, FB], f32)

        ps = ctx.enter_context(nc.psum_tensor("ps", [P, 8, 512], f32))

        def out_slot(t):
            return ps[:, 6 + t // 2, (t % 2) * F:(t % 2 + 1) * F]

        quarter_in = [sem(f"quarter_in{q}") for q in range(NQ)]
        small_in, weights_in = sem("small_in"), sem("weights_in")
        x_in_s = [sem(f"x_in{s}") for s in range(2)]
        parts_in = [sem(f"parts_in{c}") for c in range(NC)]
        x_out = [sem(f"x_out{s}") for s in range(2)]
        h_out = [sem(f"h_out{s}") for s in range(2)]
        memset_done, consts_ready = sem("memset_done"), sem("consts_ready")
        cast8_done, cast16_done = sem("cast8_done"), sem("cast16_done")
        diag_done = sem("diag_done")
        deg_used, deg_done = sem("deg_used"), sem("deg_done")
        lncol_ready, h0_done = sem("lncol_ready"), sem("h0_done")
        var_ready, std_ready = sem("var_ready"), sem("std_ready")
        wa_ps_ready, wa_ready = sem("wa_ps_ready"), sem("wa_ready")
        wa_rows_ps, wa_rows_ready = sem("wa_rows_ps"), sem("wa_rows_ready")
        dve_step = sem("dve_step")
        scaled_ready, hi_split, split_done = sem("scaled_ready"), sem("hi_split"), sem("split_done")
        panel_ready, group_done = sem("panel_ready"), sem("group_done")
        ht1_ready, evac_done, out_ready = sem("ht1_ready"), sem("evac_done"), sem("out_ready")
        out_used = [sem(f"out_used{l}") for l in range(4)]
        hs_ready, hi_ready, post_done = sem("hs_ready"), sem("hi_ready"), sem("post_done")
        gown_ready, gall_ready = sem("gown_ready"), sem("gall_ready")
        ht_ready, ht_evac, ht_summed = sem("ht_ready"), sem("ht_evac"), sem("ht_summed")
        y_ps_ready, y_evac, uv_ready, cols_ready = sem("y_ps_ready"), sem("y_evac"), sem("uv_ready"), sem("cols_ready")
        hsum_ready, my_ps_ready, my_ready = sem("hsum_ready"), sem("my_ps_ready"), sem("my_ready")
        vb_ps_ready, vb_evac, ones_set = sem("vb_ps_ready"), sem("vb_evac"), sem("ones_set")
        mask_in = [sem(f"mask_in{g}") for g in range(NC)]
        row_in = [sem(f"row_in{h}") for h in range(2)]
        row_used = sem("row_used")
        cc_ready, ab_ps_ready, ab_ready = sem("cc_ready"), sem("ab_ps_ready"), sem("ab_ready")
        mask_ready, edge_ready = sem("mask_ready"), sem("edge_ready")
        lin_ready, p_ready, p_used = sem("lin_ready"), sem("p_ready"), sem("p_used")
        rz_ready, att_evac = sem("rz_ready"), sem("att_evac")
        pool_step, elu_in, elu_out, neg_ready = sem("pool_step"), sem("elu_in"), sem("elu_out"), sem("neg_ready")
        last_in, last_out = sem("last_in"), sem("last_out")
        x3_in, fin_ready, fin_out = sem("x3_in"), sem("fin_ready"), sem("fin_out")

        def wait(eng, s, v):
            if not isinstance(v, int) or v > 0:
                eng.wait_ge(s, v)

        block = ctx.enter_context(nc.Block())

        LG = NC * GROUPS
        EVAC_BASE = [NC * sum(EVACS[:l]) for l in range(5)]
        X_USES = {0: 1, 2: 2, 3: 3}
        X_STORES = {0: 0, 2: 1, 3: 2}
        HI_BASE = {0: 0, 2: NT, 3: 2 * NT}
        W_NEEDED = [32, 48, 64, 96, 128]
        H = NC // 2

        @block.sync
        def _(sp):
            def load_quarter(j, q):
                sp.dma_start(quarter[:, q, :], adj_t.rearrange("(j p) (q n) -> j q p n", p=P, q=NQ)[j, q, :, :])\
                  .then_inc(quarter_in[q], 16)

            def load_x(src, c, s):
                sp.dma_start(x_ring[:, s, :, :], chunk_rows(src, c)).then_inc(x_in_s[s], 16)

            def load_weights(l):
                src = [w_gcn, w_conv1, w_conv2, w_gcn2][l]
                sp.dma_start(w_sb[:, 0:KB[l], :], src.rearrange("(k p) f -> p k f", p=P)).then_inc(weights_in, 16)
                if l in (0, 3):
                    sp.dma_start(bias_row, (b_gcn if l == 0 else b_gcn2).partition_broadcast(P)).then_inc(weights_in, 16)

            load_x(x_in, 0, 0)
            for q in range(NQ):
                load_quarter(0, q)
            load_x(x_in, 1, 1)
            sp.dma_start(w3t_sb[:, :, :], w_att_t.rearrange("(k p) f -> p k f", p=P)).then_inc(small_in, 16)
            sp.dma_start(a_sb[:, :, :], a_att.rearrange("(k p) f -> p k f", p=P)).then_inc(small_in, 16)

            def panels(c, last):
                for t in range(TPC):
                    if last and t == TPC - 1:
                        continue
                    for q in range(NQ):
                        sp.wait_ge(cast8_done, (c * TPC + t) * NQ + q + 1)
                        sp.wait_ge(cast16_done, (c * TPC + t) * NQ + q + 1)
                        load_quarter(c * TPC + t + 1, q)

            panels(0, False)
            with sp.Fori(0, H - 1) as r:
                for s in range(2):
                    panels(2 * r + s + 1, False)
                    sp.wait_ge(h0_done, (2 * r + s + 1) * TPC)
                    load_x(x_in, 2 * r + s + 2, s)
            panels(NC - 1, True)
            for s in range(2):
                sp.wait_ge(h0_done, (NC - 1 + s) * TPC)
                load_x(x_in, s, s)
            sp.wait_ge(deg_done, 1)
            load_weights(0)

            def reload(l, c):
                sp.wait_ge(group_done, l * LG + (NC - 1) * GROUPS + (c + 1) * TPC // PANELS)
                sp.wait_ge(h_out[c % 2], 16 * (l * H + c // 2 + 1))
                sp.dma_start(feat32[:, c * TPC:(c + 1) * TPC, :], chunk_rows(hs, c)).then_inc(parts_in[c], 16)

            for l in range(4):
                nxt = {0: None, 1: (2, xs), 2: (3, xs), 3: None}[l]

                def store(c, s):
                    sp.wait_ge(post_done, l * NC + c + 1)
                    if l != 1:
                        sp.dma_start(chunk_rows(xs, c), x_ring[:, s, :, :]).then_inc(x_out[s], 16)
                    sp.dma_start(chunk_rows(hs, c), g_ring[:, s, :, :]).then_inc(h_out[s], 16)

                def refill(c, s, cc):
                    sp.wait_ge(x_out[s], 16 * (X_STORES[l] * H + cc + 1))
                    load_x(x_in if l == 0 else xs, c + 2, s)

                with sp.Fori(0, H - 1) as r:
                    for s in range(2):
                        store(2 * r + s, s)
                        if l != 1:
                            refill(2 * r + s, s, r)
                for c in range(4):
                    reload(l, c)
                store(NC - 2, 0)
                for c in range(4, NC - 1):
                    reload(l, c)
                store(NC - 1, 1)
                reload(l, NC - 1)
                if l != 1:
                    for s in range(2):
                        sp.wait_ge(x_out[s], 16 * (X_STORES[l] + 1) * H)
                if l in (0, 2):
                    for s in range(2):
                        load_x(xs, s, s)
                sp.wait_ge(out_ready, (l + 1) * NT)
                if l < 3:
                    load_weights(l + 1)
            sp.wait_ge(uv_ready, 1)
            for s in range(2):
                sp.dma_start(wt_sb[:, :, s * F:(s + 1) * F],
                             w_trans[s * F:(s + 1) * F, :].rearrange("(k p) f -> p k f", p=P)).then_inc(weights_in, 16)

            def load_mask(c, g):
                src = adj_t.rearrange("(g t p) (c n) -> g c p t n", p=P, t=TPC, n=CH)
                sp.dma_start(mask[:, g * TPC:(g + 1) * TPC, :], src[g, c, :, :, :]).then_inc(mask_in[g], 16)

            def load_row(i, h):
                sp.dma_start(rows[:, h, :], adj.rearrange("(i p) (h n) -> i h p n", p=P, h=2)[i, h, :, :])\
                  .then_inc(row_in[h], 16)

            sp.wait_ge(panel_ready, 4 * LG)
            for g in range(NC // 2):
                load_mask(0, g)
            sp.wait_ge(ht_ready, NC)
            for h in range(2):
                load_row(0, h)

            def next_row(i, h):
                sp.wait_ge(row_used, (i - 1) * 4 + 2 * h + 2)
                load_row(i, h)

            for i in range(1, TPC + 1):
                for h in range(2):
                    next_row(i, h)
            sp.wait_ge(y_ps_ready, NT)
            for g in range(NC // 2, NC):
                load_mask(0, g)

            def att_loads(c, first, last):
                for t in range(1 if first else 2, TPC):
                    for h in range(2):
                        next_row((c + 1) * TPC + t, h)
                rows_after = {} if last else {0: (0, 0), 2: (0, 1), 5: (1, 0), 6: (1, 1)}
                for g in range(NC):
                    sp.wait_ge(lin_ready, c * NT + (NT + (g + 1) * TPC) // 2)
                    load_mask(c + 1, g)
                    if g in rows_after:
                        t, h = rows_after[g]
                        next_row((c + 2) * TPC + t, h)

            att_loads(0, True, False)
            with sp.Fori(1, NC - 2) as c:
                att_loads(c, False, False)
            att_loads(NC - 2, False, True)
            for s in range(2):
                sp.wait_ge(x_out[s], 16 * 3 * H)
                sp.wait_ge(h_out[s], 16 * 4 * H)

        @block.gpsimd
        def _(pool):
            nc.gpsimd.memset(zeros16[:, :], 0.0).then_inc(consts_ready, 1)
            nc.gpsimd.memset(ident16[:, :], 0.0).then_inc(memset_done, 1)
            nc.gpsimd.memset(ident32[:, :], 0.0).then_inc(memset_done, 1)
            nc.gpsimd.memset(ones16[:, :], 1.0).then_inc(consts_ready, 1)
            pool.wait_ge(memset_done, 2)
            for eye in (ident16, ident32):
                nc.gpsimd.affine_select(out=eye[:, :], in_=eye[:, :], compare_op=ALU.not_equal, fill=1.0, base=0,
                                        pattern=[[-1, P]], channel_multiplier=1).then_inc(consts_ready, 1)
            pool.wait_ge(gown_ready, 1)
            nc.gpsimd.partition_all_reduce(g_all, g_own, P, bass.bass_isa.ReduceOp.max).then_inc(gall_ready, 1)

            pool.wait_ge(panel_ready, 4 * LG)
            nc.gpsimd.memset(Yb[:, :, :, F:YW], 1.0).then_inc(ones_set, 1)
            pool.wait_ge(my_ready, 1)

            K = 4

            with pool.Fori(0, NC - 1) as c:
                k = [0]

                def link(ins):
                    k[0] += 1
                    ins.then_inc(pool_step, 1)
                    pool.wait_ge(pool_step, c * K + k[0])

                D, M = R[:, 0, :, :], R[:, 1, :, :]
                pool.wait_ge(att_evac, c * 2 * TPC + 2 * TPC)
                link(nc.gpsimd.tensor_tensor(D, D, M, ALU.add))
                link(nc.gpsimd.tensor_tensor(M, mean_y.rearrange("p (a f) -> p a f", a=1).to_broadcast([P, TPC, F]),
                                             lone[:, bass.ds(c * TPC, TPC)].rearrange("p (t a) -> p t a", a=1)
                                             .to_broadcast([P, TPC, F]), ALU.mult))
                nc.gpsimd.tensor_tensor(D, D, M, ALU.add).then_inc(elu_in, 1)
                pool.wait_ge(x3_in, c * 16 + 16)
                link(nc.gpsimd.tensor_tensor(x3, x3, ones16[:, 0:1].rearrange("p (t a) -> p t a", a=1)
                                             .to_broadcast([P, TPC, F]), ALU.subtract))
                pool.wait_ge(elu_out, c + 1)
                link(nc.gpsimd.tensor_tensor(D, D, x3, ALU.add))
                nc.gpsimd.tensor_tensor(D, D, M, ALU.add).then_inc(fin_ready, 1)

        @block.scalar
        def _(act):
            def copy(out_, in_, **kw):
                return nc.scalar.activation(out_, in_, ACT.Copy, **kw)

            def std_of(n, out_=std, in_=var_e):
                act.wait_ge(var_ready, n)
                nc.scalar.activation(out_, in_, ACT.Sqrt).then_inc(std_ready, 1)

            def load_chunk(c, s, norm):
                for t in range(TPC):
                    for q in range(NQ):
                        act.wait_ge(quarter_in[q], (c * TPC + t) * 16 + 16)
                        wait(act, deg_used, (c * TPC + t) * NQ + (q - 1))
                        copy(quarter16[:, q % 2, :], quarter[:, q, :]).then_inc(cast16_done, 1)
                        if norm and (t, q) == (0, 1):
                            std_of(c)
                        if norm and (t, q) == (1, 0):
                            act.wait_ge(lncol_ready, c)
                        if norm and t in (1, 2) and q % 2 == 0:
                            h0_tile(c - 1, 1 - s, (t - 1) * 2 + q // 2)

            def h0_tile(c, s, t):
                nc.scalar.activation(feat32[:, bass.ds(c * TPC + t, 1), :], x_ring[:, s, t:t + 1, :], ACT.Relu,
                                     bias=shift_c[:, t:t + 1], scale=scale_c[:, t:t + 1]).then_inc(h0_done, 1)

            load_chunk(0, 0, False)
            load_chunk(1, 1, True)
            with act.Fori(1, H) as r:
                for s in range(2):
                    load_chunk(r * 2 + s, s, True)
            std_of(NC)
            act.wait_ge(lncol_ready, NC)
            for t in range(TPC):
                h0_tile(NC - 1, 1, t)
            std_of(NC + 1, deg_std, deg1)
            act.wait_ge(wa_ps_ready, 1)
            copy(wa_sb[:, :, :], ps[:, 7, 0:2 * FB].rearrange("p (k s) -> p k s", s=2)).then_inc(wa_ready, 1)

            def split_hi(base, j):
                act.wait_ge(scaled_ready, base + j + 1)
                copy(parts[:, j, 0, :], hs32[:, j % 2, :]).then_inc(hi_split, 1)

            def ht_copy(c):
                if c == 0:
                    act.wait_ge(panel_ready, 4 * LG)
                act.wait_ge(ht_ready, c + 1)
                k = 2 * (c % 2)
                copy(T_all[:, c, :, :], ps[:, k:k + 2, :]).then_inc(ht_evac, 1)

            act.wait_ge(diag_done, NT)
            for l in range(4):

                def stage_groups(c, lo, hi, l=l):
                    if lo == 0 and l in (1, 3):
                        act.wait_ge(diag_done, c + (NT + 1 if l == 1 else NT + NC + 1))
                    for g in range(lo, hi):
                        n = c * GROUPS + (l * LG + g)
                        wait(act, group_done, n - (STAGES - 1))
                        copy(stage[:, g % STAGES, :, :],
                             adj8[:, g * PANELS:(g + 1) * PANELS, bass.ts(c, CH)]).then_inc(panel_ready, 1)

                def evac(c, e, s):
                    if e == 0:
                        wait(act, out_ready, c * TPC + l * NT)
                    if l in (1, 2) and e == 0:
                        act.wait_ge(ht1_ready, c + (NC * (l - 1) + 1))
                        bank = 4
                    else:
                        half = GROUPS // 2 if (l == 0 and e == 0) else GROUPS
                        act.wait_ge(group_done, c * GROUPS + (l * LG + half))
                        bank = 2 * e if l == 0 else 2 * s
                    copy(T_sb[:, 2 * e:2 * e + 2, :], ps[:, bank:bank + 2, :]).then_inc(evac_done, 1)

                def post_std(c):
                    if l != 1:
                        std_of(c + (NC + 2 + HI_BASE[l] // TPC))

                def post(c, s, cc, tiles):
                    if tiles[0] == 0:
                        wait(act, h_out[s], cc * 16 + 16 * H * l)
                    for t in tiles:
                        if l == 1:
                            act.wait_ge(out_ready, c * TPC + (NT + (t | 1) + 1))
                            nc.scalar.activation(g_ring[:, s, t, :], out_slot(t), ACT.Relu, scale=1.0 / SC)\
                              .then_inc(out_used[1], 1)
                        else:
                            act.wait_ge(hs_ready, c * TPC + (HI_BASE[l] + t + 1))
                            nc.scalar.activation(h_ring[:, s, t, 0, :], hs32[:, t % 2, :], ACT.Relu)\
                              .then_inc(hi_ready, 1)

                def chunk(c, s, cc_prev, last=False, staged=4):
                    stage_groups(c, staged, 12)
                    if EVACS[l] == 2:
                        evac(c, 0, s)
                    stage_groups(c, 12, 14)
                    if cc_prev is not None:
                        post_std(c - 1)
                    stage_groups(c, 14, 16)
                    if cc_prev is not None:
                        post(c - 1, 1 - s, cc_prev, (0, 1))
                    if not last:
                        stage_groups(c + 1, 0, 2)
                    if cc_prev is not None:
                        post(c - 1, 1 - s, cc_prev, (2, 3))
                    if not last:
                        stage_groups(c + 1, 2, 4)
                    evac(c, EVACS[l] - 1, s)

                if l in (0, 2):
                    stage_groups(0, 0, 2)
                    for g in range(GROUPS):
                        for t in range(PANELS):
                            split_hi(0 if l == 0 else NT, g * PANELS + t)
                        if 0 < g < GROUPS - 1:
                            stage_groups(0, g + 1, g + 2)
                        if g == GROUPS // 2 + 2:
                            evac(0, 0, 0)
                    stage_groups(1, 0, 4)
                    evac(0, 1, 0)
                else:
                    chunk(0, 0, None, staged=7)
                chunk(1, 1, 0)
                chunk(2, 0, 0)
                with act.Fori(1, H - 1) as r:
                    chunk(r * 2 + 1, 1, r)
                    chunk(r * 2 + 2, 0, r)
                chunk(NC - 1, 1, H - 1, last=True)
                if l in (0, 2):
                    stage_groups(0, 0, 4, l + 1)
                if l == 3:
                    ht_copy(0)
                post_std(NC - 1)
                if l in (0, 2):
                    stage_groups(0, 4, 6, l + 1)
                if l == 2:
                    act.wait_ge(wa_rows_ps, 1)
                    copy(wa_rows, ps[:, 4, :].rearrange("p (s f) -> p s f", s=2)).then_inc(wa_rows_ready, 1)
                if l == 3:
                    ht_copy(1)
                post(NC - 1, 1, H - 1, (0, 1))
                if l in (0, 2):
                    stage_groups(0, 6, 7, l + 1)
                post(NC - 1, 1, H - 1, (2, 3))

            for c in range(2, EARLY):
                ht_copy(c)
            act.wait_ge(out_ready, 4 * NT)
            for c in range(NC):
                act.wait_ge(vb_ps_ready, c + 1)
                copy(t_row[:, c * CH:(c + 1) * CH], ps[:, 6 + c % 2, :]).then_inc(vb_evac, 1)
            for c in range(EARLY, NC):
                ht_copy(c)
            def rows_copy(s, n):
                act.wait_ge(ab_ps_ready, n)
                copy(AB[:, 2 * s:2 * s + 2, :], ps[:, 4 * s:4 * s + 2, :]).then_inc(ab_ready, 1)

            def mask_exponents(c, g):
                act.wait_ge(mask_in[g], c * 16 + 16)
                m = mask[:, g * TPC:(g + 1) * TPC, :]
                copy(m, m, scale=BIG, bias=-BIG).then_inc(mask_ready, 1)

            mask_exponents(0, 0)
            for j in range(NT):
                if j == ROWS_AT:
                    rows_copy(0, 1)
                act.wait_ge(y_ps_ready, j + 1)
                copy(Yb[:, j, :, 0:F], ps[:, 2 + j % 2, :].rearrange("p (s f) -> p s f", s=2),
                     scale=1.0 / SC).then_inc(y_evac, 1)

            def averages(c, s):
                act.wait_ge(rz_ready, c * 2 + (s + 1))
                if s == 0:
                    wait(act, fin_out, c * 16)
                else:
                    wait(act, fin_ready, c)
                for t in range(TPC):
                    nc.scalar.activation(R[:, s, t, :], ps[:, 4 * s + t, 0:F], ACT.Copy, scale=rz[:, s, t:t + 1])\
                      .then_inc(att_evac, 1)

            def elu_exp(c):
                D, M = R[:, 0, :, :], R[:, 1, :, :]
                act.wait_ge(elu_in, c + 1)
                nc.scalar.activation(M, D, ACT.Relu, scale=-1.0).then_inc(neg_ready, 1)
                nc.scalar.activation(D, D, ACT.Relu)
                act.wait_ge(neg_ready, c + 1)
                nc.scalar.activation(M, M, ACT.Exp, scale=-1.0).then_inc(elu_out, 1)

            def store_result(c):
                act.wait_ge(fin_ready, c + 1)
                act.dma_start(chunk_rows(out, c), R[:, 0, :, :]).then_inc(fin_out, 16)

            def load_x3(c):
                act.dma_start(x3, chunk_rows(xs, c)).then_inc(x3_in, 16)

            def att_chunk(c, first, last):
                for s in range(2):
                    for j in range(NT):
                        if j % 2 == 0:
                            act.wait_ge(lin_ready, c * NT + (s * NT + j) // 2 + 1)
                        nc.scalar.activation(E[:, j % RING, :], E[:, j % RING, :], ACT.Exp, bias=v_2[:, s, j:j + 1])\
                          .then_inc(p_ready, 1)
                        if s == 0 and j % TPC == 0 and j // TPC + 1 < NC:
                            mask_exponents(c, j // TPC + 1)
                        if s == 1 and j == NT - 1 and not last:
                            mask_exponents(c + 1, 0)
                        if s == 0:
                            if j == 9 and not first:
                                averages(c - 1, 1)
                            if j == 14:
                                wait(act, lin_ready, c * NT)
                                rows_copy(1, c * 2 + 2)
                            if j == 22 and not first:
                                elu_exp(c - 1)
                            if j == 28 and not first:
                                store_result(c - 1)
                                load_x3(c)
                        else:
                            if j == 9:
                                averages(c, 0)
                            if j == 24 and not last:
                                rows_copy(0, c * 2 + 3)

            act.wait_ge(cols_ready, 1)
            load_x3(0)
            att_chunk(0, True, False)
            with act.Fori(1, NC - 1) as c:
                att_chunk(c, False, False)
            att_chunk(NC - 1, False, True)
            for t in range(TPC):
                D, M = R[:, 0, t, :], R[:, 1, t, :]
                act.wait_ge(last_in, t + 1)
                nc.scalar.activation(M, D, ACT.Relu, scale=-1.0).then_inc(neg_ready, 1)
                nc.scalar.activation(D, D, ACT.Relu)
                act.wait_ge(neg_ready, NC + t)
                nc.scalar.activation(M, M, ACT.Exp, scale=-1.0).then_inc(last_out, 1)
            store_result(NC - 1)
            act.wait_ge(fin_out, 16 * NC)

        @block.vector
        def _(dve):
            steps = [0]

            class Chain:
                def __init__(self, turn, per_turn):
                    self.turn, self.per_turn, self.k = turn, per_turn, 0

                def link(self, ins):
                    self.k += 1
                    ins.then_inc(dve_step, 1)
                    dve.wait_ge(dve_step, self.turn * self.per_turn + (steps[0] + self.k))

                def end(self, turns):
                    assert self.k == self.per_turn or turns == 1
                    steps[0] += self.k * turns

            def mean_and_variance(t, link):
                link(nc.vector.bn_aggr(mv[:, t, :], stat[:, t, :]))

            def last_variance(link):
                t = TPC - 1
                nc.vector.tensor_scalar(var_e[:, 0:t], var_c[:, 0:t], EPS, None, ALU.add)
                mean_and_variance(t, link)
                nc.vector.tensor_scalar(var_e[:, t:TPC], var_c[:, t:TPC], EPS, None, ALU.add).then_inc(var_ready, 1)

            def one_over_root(n, value, root, est, link):
                dve.wait_ge(std_ready, n)
                link(nc.vector.reciprocal(est, root))
                link(nc.vector.tensor_tensor(root, est, est, ALU.mult))
                link(nc.vector.tensor_tensor(root, root, value, ALU.mult))
                link(nc.vector.tensor_scalar(root, root, -0.5, 1.5, ALU.mult, ALU.add))
                return root

            def on_diagonal(j, op):
                block = adj8[:, bass.ds(j, 1), bass.ds(j * P, P)]
                return nc.vector.tensor_tensor(block, block, ident16[:, :].rearrange("p (a n) -> p a n", a=1), op)

            dve.wait_ge(consts_ready, 4)

            def norm_columns(c, ch):
                left = one_over_root(c + 1, var_e, std, rough, ch.link)
                wait(dve, h0_done, c * TPC)
                ch.link(nc.vector.tensor_tensor(scale_c, rough, left, ALU.mult))
                nc.vector.scalar_tensor_tensor(shift_c, mean_c, -1.0, scale_c, ALU.mult, ALU.mult)\
                  .then_inc(lncol_ready, 1)
                dve.wait_ge(lncol_ready, c + 1)

            def load_chunk(c, s, cc, ch, norm=True):
                for t in range(TPC):
                    for q in range(NQ):
                        dve.wait_ge(quarter_in[q], (c * TPC + t) * 16 + 16)
                        nc.vector.tensor_copy(adj8[:, bass.ds(c * TPC + t, 1), q * QW:(q + 1) * QW],
                                              quarter[:, q:q + 1, :]).then_inc(cast8_done, 1)
                    dve.wait_ge(cast8_done, (c * TPC + t) * NQ + NQ)
                    on_diagonal(c * TPC + t, ALU.add).then_inc(diag_done, 1)
                    if t > 0:
                        mean_and_variance(t - 1, ch.link)
                    else:
                        if norm:
                            norm_columns(c - 1, ch)
                        dve.wait_ge(x_in_s[s], cc * 16 + 16)
                    ch.link(nc.vector.bn_stats(stat[:, t, :], x_ring[:, s, t, :]))
                last_variance(ch.link)

            PER0 = 2 * (2 * TPC + 5)
            ch = Chain(0, 0)
            for s in range(2):
                load_chunk(s, s, 0, ch, norm=(s == 1))
            ch.end(1)
            with dve.Fori(0, H - 1) as r:
                ch = Chain(r, PER0)
                for s in range(2):
                    load_chunk(r * 2 + (s + 2), s, r + 1, ch)
            ch.end(H - 1)

            ch = Chain(0, 0)
            norm_columns(NC - 1, ch)
            dve.wait_ge(deg_done, 1)
            ch.link(nc.vector.tensor_scalar(dsc[:, :], ps[:, 6, 0:NT], 1.0, None, ALU.add))
            nc.vector.tensor_scalar(lone[:, :], dsc[:, :], 1.0, None, ALU.is_equal)
            nc.vector.tensor_scalar(deg1, dsc[:, :], 1e-30, None, ALU.max).then_inc(var_ready, 1)
            left = one_over_root(NC + 1, deg1, deg_std, fac[:, :], ch.link)
            ch.link(nc.vector.tensor_tensor(fac[:, :], fac[:, :], left, ALU.mult))
            ch.link(nc.vector.scalar_tensor_tensor(dinv[:, :], dsc[:, :], 0.0, fac[:, :], ALU.is_gt, ALU.mult))
            ch.link(nc.vector.tensor_scalar(fac[:, :], dinv[:, :], SC, None, ALU.mult))
            ch.link(nc.vector.tensor_scalar(dsc[:, :], dinv[:, :], 1.0 / SC, None, ALU.mult))
            ch.end(1)

            def split(base, column):
                def turn(r, first):
                    for t in range(2):
                        if not first:
                            dve.wait_ge(split_done, r * 2 + (base + t - 1))
                        nc.vector.tensor_scalar(hs32[:, t:t + 1, :], feat32[:, bass.ds(r * 2 + t, 1), :],
                                                column(r * 2 + t), None, ALU.mult).then_inc(scaled_ready, 1)
                    for t in range(2):
                        dve.wait_ge(hi_split, r * 2 + (base + t + 1))
                        nc.vector.tensor_tensor(parts[:, bass.ds(r * 2 + t, 1), 1, :], hs32[:, t:t + 1, :],
                                                parts[:, bass.ds(r * 2 + t, 1), 0, :], ALU.subtract)\
                          .then_inc(split_done, 1)

                turn(0, True)
                with dve.Fori(1, NT // 2) as r:
                    turn(r, False)

            for l in range(4):
                if l == 0:
                    dve.wait_ge(h0_done, NT)
                    split(0, lambda j: fac[:, bass.ds(j, 1)])
                if l == 2:
                    ch = Chain(0, 0)
                    dve.wait_ge(post_done, 2 * NC)
                    ch.link(nc.vector.tensor_reduce(g_own, gmax[:, :], AX.X, ALU.max))
                    nc.vector.tensor_scalar(g_own, g_own, 1e-30, None, ALU.max).then_inc(gown_ready, 1)
                    dve.wait_ge(gall_ready, 1)
                    ch.link(nc.vector.tensor_scalar(g_pow.bitcast(i32), g_all.bitcast(i32), 0x7F800000, None,
                                                    ALU.bitwise_and))
                    ch.link(nc.vector.reciprocal(g_scale, g_pow))
                    ch.link(nc.vector.tensor_scalar(g_inv, g_pow, 2.0 ** -14, None, ALU.mult))
                    ch.link(nc.vector.tensor_scalar(g_scale, g_scale, 2.0 ** 14, None, ALU.mult))
                    ch.end(1)
                    for c in range(NC):
                        dve.wait_ge(parts_in[c], 32)
                    split(NT, lambda j: g_scale)
                if l in (0, 3):
                    dve.wait_ge(weights_in, W_NEEDED[l])
                if l == 3:
                    dve.wait_ge(wa_rows_ready, 1)

                PER = {0: 5 * TPC + 5, 1: 0, 2: 4 * TPC + 5, 3: 6 * TPC + 5}[l] * 2

                def post(c, s, cc, ch):
                    i0 = c * TPC
                    if l == 1:
                        for t in range(TPC):
                            dve.wait_ge(out_used[1], i0 + (t + 1))
                            ins = nc.vector.tensor_reduce(gmax[:, bass.ds(i0 + t, 1)], g_ring[:, s, t, :], AX.X, ALU.max)
                        ins.then_inc(post_done, 1)
                        return
                    dve.wait_ge(x_in_s[s], cc * 16 + 16 * (X_USES[l] * H + 1))
                    for t in range(TPC):
                        x_t, y_t, o_t = x_ring[:, s, t, :], y_tmp, out_slot(t)
                        dve.wait_ge(out_ready, i0 + (NT * l + (t | 1) + 1))
                        if l == 2:
                            nc.vector.tensor_scalar(y_t, o_t, g_inv, 0.0, ALU.mult, ALU.max).then_inc(out_used[l], 1)
                        else:
                            nc.vector.scalar_tensor_tensor(y_t, o_t, dsc[:, bass.ds(i0 + t, 1)], bias_row,
                                                           ALU.mult, ALU.add).then_inc(out_used[l], 1)
                        if t > 0:
                            mean_and_variance(t - 1, ch.link)
                        dve.wait_ge(out_used[l], i0 + (t + 1))
                        if l == 0:
                            ch.link(nc.vector.scalar_tensor_tensor(y_t, y_t, 0.01, y_t, ALU.mult, ALU.max))
                        if l == 3:
                            ch.link(nc.vector.scalar_tensor_tensor(x_t, y_t, 0.0, x_t, ALU.max, ALU.add))
                        else:
                            ch.link(nc.vector.tensor_tensor(x_t, y_t, x_t, ALU.add))
                        ch.link(nc.vector.bn_stats(stat[:, t, :], x_t))
                    last_variance(ch.link)
                    left = one_over_root(c + (NC + 2 + HI_BASE[l] // TPC), var_e, std, rough, ch.link)
                    ch.link(nc.vector.scalar_tensor_tensor(scale_c, rough, SC, left, ALU.mult, ALU.mult))
                    if l == 2:
                        ch.link(nc.vector.tensor_tensor(scale_c, scale_c, dinv[:, bass.ds(i0, TPC)], ALU.mult))
                    ch.link(nc.vector.scalar_tensor_tensor(shift_c, mean_c, -1.0, scale_c, ALU.mult, ALU.mult))

                    def scaled(t):
                        wait(dve, hi_ready, i0 + (HI_BASE[l] + t - 1))
                        nc.vector.tensor_scalar(hs32[:, t % 2, :], x_ring[:, s, t, :], scale_c[:, t:t + 1],
                                                shift_c[:, t:t + 1], ALU.mult, ALU.add).then_inc(hs_ready, 1)

                    scaled(0)
                    for t in range(TPC):
                        if t + 1 < TPC:
                            scaled(t + 1)
                        dve.wait_ge(hi_ready, i0 + (HI_BASE[l] + t + 1))
                        lo = nc.vector.scalar_tensor_tensor(h_ring[:, s, t, 1, :], hs32[:, t % 2, :], 0.0,
                                                            h_ring[:, s, t, 0, :], ALU.max, ALU.subtract)
                        if t + 1 < TPC:
                            ch.link(lo)
                        else:
                            lo.then_inc(post_done, 1)
                        if l == 3:
                            for k in range(2):
                                ch.link(nc.vector.scalar_tensor_tensor(
                                    y_tmp, hs32[:, t % 2, :], 0.0, wa_rows[:, k, :], ALU.max, ALU.mult,
                                    accum_out=uv_sb[:, bass.ds(i0 + t, 1), k]))

                    if l != 3:
                        dve.wait_ge(panel_ready, c * GROUPS + (l * LG + GROUPS))
                        dve.wait_ge(diag_done, NT if l == 0 else NT + NC)
                        for t in range(TPC):
                            ins = on_diagonal(i0 + t, ALU.subtract if l == 0 else ALU.add)
                        ins.then_inc(diag_done, 1)

                if l == 2:
                    PER += 2
                ch = Chain(0, PER)
                for s in range(2):
                    post(s, s, 0, ch)
                ch.end(1)
                with dve.Fori(0, H - 1) as r:
                    ch = Chain(r, PER)
                    for s in range(2):
                        post(r * 2 + (2 + s), s, r + 1, ch)
                ch.end(H - 1)

            ch = Chain(0, 0)
            nc.vector.tensor_scalar(uv_sb[:, :, :], uv_sb[:, :, :], 1.0 / SC, None, ALU.mult).then_inc(uv_ready, 1)
            dve.wait_ge(uv_ready, 1)
            for c in range(NC):
                dve.wait_ge(vb_evac, c + 1)
                nc.vector.tensor_reduce(vext[:, 0, c:c + 1], t_row[:, c * CH:(c + 1) * CH], AX.X, ALU.max)
                ins = nc.vector.tensor_reduce(vext[:, 1, c:c + 1], t_row[:, c * CH:(c + 1) * CH], AX.X, ALU.min)
            ch.link(ins)
            nc.vector.tensor_reduce(v_hi, vext[:, 0, :], AX.X, ALU.max)
            ch.link(nc.vector.tensor_reduce(v_lo, vext[:, 1, :], AX.X, ALU.min))
            ch.link(nc.vector.tensor_tensor(v_rng, v_hi, v_lo, ALU.subtract))
            ch.link(nc.vector.tensor_scalar(v_rng, v_rng, 1e-30, None, ALU.max))
            nc.vector.tensor_scalar(v_R, v_rng, 2.0, None, ALU.mult)
            nc.vector.tensor_scalar(v_nR, v_rng, -2.0, None, ALU.mult)
            ch.link(nc.vector.reciprocal(v_r, v_rng))
            nc.vector.scalar_tensor_tensor(v_c1, v_R, -0.25, v_lo, ALU.mult, ALU.add)
            nc.vector.scalar_tensor_tensor(v_c2, v_R, 0.75, v_lo, ALU.mult, ALU.add)
            ch.link(nc.vector.tensor_scalar(v_r, v_r, 0.5, None, ALU.mult))
            ch.link(nc.vector.tensor_scalar(t_row, t_row, v_c1, v_r, ALU.subtract, ALU.mult))
            for c in range(NC):
                dve.wait_ge(ht_evac, c + 1)
                nc.vector.tensor_reduce(hsum[:, :, c:c + 1], T_all[:, c, :, :], AX.X, ALU.add).then_inc(ht_summed, 1)
            dve.wait_ge(ht_summed, NC)
            nc.vector.tensor_reduce(hsum1[:, :], hsum[:, :, :], AX.X, ALU.add).then_inc(hsum_ready, 1)
            dve.wait_ge(ht_ready, NC)
            nc.vector.tensor_copy(u_col, uv_sb[:, :, 0])
            for s in range(2):
                sign = 1.0 - 2.0 * s
                nc.vector.tensor_scalar(v_8[:, s, :], uv_sb[:, :, 1], 0.8 * sign, None, ALU.mult)
                ins = nc.vector.tensor_scalar(v_2[:, s, :], uv_sb[:, :, 1], 0.2 * sign, None, ALU.mult)
            ins.then_inc(cols_ready, 1)
            ch.end(1)

            def extreme(t, h, low):
                if not low:
                    nc.vector.tensor_tensor_reduce(out=junk, in0=rows[:, h, :], in1=t_row[:, h * HALF:(h + 1) * HALF],
                                                   scale=1.0, scalar=0.0, op0=ALU.mult, op1=ALU.max,
                                                   accum_out=tmx[:, t, h:h + 1]).then_inc(row_used, 1)
                else:
                    nc.vector.tensor_tensor_reduce(out=junk, in0=rows[:, h, :], in1=t_row[:, h * HALF:(h + 1) * HALF],
                                                   scale=1.0, scalar=-1.0, op0=ALU.subtract, op1=ALU.max,
                                                   accum_out=tmn[:, t, h:h + 1]).then_inc(row_used, 1)

            def shifts(c, ch):
                vM, vm, s_p, s_n, l_p, l_n = (ccol[:, 4:5, :], ccol[:, 5:6, :], ccol[:, 4:5, :], ccol[:, 5:6, :],
                                              ccol[:, 6:7, :], ccol[:, 7:8, :])
                u = u_col[:, bass.ds(c * TPC, TPC)].rearrange("p (a t) -> p a t", a=1)
                dve.wait_ge(row_used, c * 4 * TPC + 4 * TPC)
                dve.wait_ge(ab_ps_ready, c * 2) if not (isinstance(c, int) and c == 0) else None
                nc.vector.tensor_tensor(vM, tmx[:, :, 0:1].rearrange("p t a -> p a t"),
                                        tmx[:, :, 1:2].rearrange("p t a -> p a t"), ALU.max)
                ch.link(nc.vector.tensor_tensor(vm, tmn[:, :, 0:1].rearrange("p t a -> p a t"),
                                                tmn[:, :, 1:2].rearrange("p t a -> p a t"), ALU.max))
                nc.vector.tensor_scalar(vM, vM, v_R, v_c1, ALU.mult, ALU.add)
                ch.link(nc.vector.tensor_scalar(vm, vm, v_nR, v_c2, ALU.mult, ALU.add))
                nc.vector.tensor_tensor(s_p, vM, u, ALU.add)
                ch.link(nc.vector.tensor_tensor(s_n, vm, u, ALU.add))
                nc.vector.scalar_tensor_tensor(l_p, s_p, 0.2, s_p, ALU.mult, ALU.max)
                ch.link(nc.vector.scalar_tensor_tensor(l_n, s_n, 0.2, s_n, ALU.mult, ALU.max))
                nc.vector.tensor_tensor(ccol[:, 0:1, :], u, l_p, ALU.subtract)
                nc.vector.scalar_tensor_tensor(ccol[:, 1:2, :], u, 0.2, l_p, ALU.mult, ALU.subtract)
                nc.vector.tensor_tensor(ccol[:, 2:3, :], l_n, u, ALU.subtract)
                nc.vector.scalar_tensor_tensor(ccol[:, 3:4, :], u, -0.2, l_n, ALU.mult, ALU.add).then_inc(cc_ready, 1)

            def reciprocals(c, s, ch):
                dve.wait_ge(p_used, c * 2 * NT + (s + 1) * NT)
                z = rz[:, s, :].rearrange("p (t a) -> p t a", a=1)
                ch.link(nc.vector.tensor_tensor(z, ps[:, 4 * s:4 * s + 4, F:YW],
                                                lone[:, bass.ds(c * TPC, TPC)].rearrange("p (t a) -> p t a", a=1),
                                                ALU.add))
                if s == 1:
                    ch.link(nc.vector.tensor_scalar(z, z, -1.0, None, ALU.mult))
                nc.vector.reciprocal(z, z).then_inc(rz_ready, 1)

            SEARCHES = 4 * TPC
            SHIFT = 23
            AHEAD = (NT - SHIFT) // 2

            def searches(c, first):
                if first:
                    plan = {m * (SHIFT - 1) // (SEARCHES - 1): (c + 1, m) for m in range(SEARCHES)}
                else:
                    plan = {2 * (m - AHEAD): (c + 1, m) for m in range(AHEAD, SEARCHES)}
                if not (isinstance(c, int) and c == NC - 2):
                    plan.update({SHIFT + 1 + 2 * m: (c + 2, m) for m in range(AHEAD)})
                return plan

            def att_chunk(c, ch, first, last):
                plan = {} if last else searches(c, first)
                for s in range(2):
                    edge = ALU.max if s == 0 else ALU.min
                    dve.wait_ge(ab_ready, c * 2 + (s + 1))
                    for pair in range(NT // 2 + 1):
                        n = s * (NT // 2) + pair
                        c_m, m = plan.get(n, (0, None)) if pair < NT // 2 else (0, None)
                        if m is not None:
                            dve.wait_ge(row_used, c_m * SEARCHES + m)
                            if m % 2 == 0:
                                dve.wait_ge(row_in[m // 2 % 2], (c_m * TPC + m // 4) * 16 + 16)
                        if pair == 4:
                            if s == 1:
                                reciprocals(c, 0, ch)
                            elif not first:
                                reciprocals(c - 1, 1, ch)
                        if n == SHIFT and pair < NT // 2 and not last:
                            shifts(c + 1, ch)
                        if pair < NT // 2:
                            for j in (2 * pair, 2 * pair + 1):
                                k = s * NT + j
                                if not (first and k < RING):
                                    dve.wait_ge(p_used, c * 2 * NT + (k - RING + 1))
                                ins = nc.vector.scalar_tensor_tensor(E[:, j % RING, :], AB[:, 2 * s, :],
                                                                     v_8[:, s, j:j + 1], AB[:, 2 * s + 1, :],
                                                                     ALU.add, edge)
                            ins.then_inc(edge_ready, 1)
                        if pair >= 1:
                            i = 2 * (pair - 1)
                            if s == 0 and i % TPC == 0:
                                dve.wait_ge(mask_ready, c * NC + (i // TPC + 1))
                            dve.wait_ge(edge_ready, c * NT + (s * NT // 2 + pair))
                            slots = E[:, i % RING:i % RING + 2, :]
                            nc.vector.tensor_tensor(slots, mask[:, i:i + 2, :], slots, ALU.add).then_inc(lin_ready, 1)
                        if m is not None:
                            extreme(m // 4, m // 2 % 2, m % 2)

            for t in range(TPC):
                for h in range(2):
                    dve.wait_ge(row_in[h], t * 16 + 16)
                    wait(dve, row_used, 4 * t + 2 * h)
                    extreme(t, h, 0)
                    dve.wait_ge(row_used, 4 * t + 2 * h + 1)
                    extreme(t, h, 1)
            ch = Chain(0, 0)
            shifts(0, ch)
            dve.wait_ge(my_ps_ready, 1)
            ch.link(nc.vector.tensor_scalar(mean_y, ps[:, 5, 0:F], 1.0 / (SC * N), None, ALU.mult))
            nc.vector.scalar_tensor_tensor(mean_y, ps[:, 5, F:2 * F], -1.0 / (SC * N), mean_y, ALU.mult, ALU.add)\
              .then_inc(my_ready, 1)
            att_chunk(0, ch, True, False)
            ch.end(1)
            with dve.Fori(1, NC - 2) as c:
                ch = Chain(c - 1, 8 - 1)
                att_chunk(c, ch, False, False)
            ch.end(NC - 3)
            ch = Chain(0, 0)
            att_chunk(NC - 2, ch, False, False)
            ch.end(1)
            ch = Chain(0, 0)
            att_chunk(NC - 1, ch, False, True)
            dve.wait_ge(x3_in, 16 * NC)
            nc.vector.tensor_scalar(x3, x3, -1.0, None, ALU.add)
            reciprocals(NC - 1, 1, ch)
            dve.wait_ge(rz_ready, 2 * NC)
            dve.wait_ge(att_evac, 2 * TPC * NC - TPC)
            for t in range(TPC):
                i, D = NT - TPC + t, R[:, 0, t, :]
                ch.link(nc.vector.scalar_tensor_tensor(D, ps[:, 4 + t, 0:F], rz[:, 1, t:t + 1], D, ALU.mult, ALU.add))
                nc.vector.scalar_tensor_tensor(D, mean_y, lone[:, i:i + 1], D, ALU.mult, ALU.add).then_inc(last_in, 1)
            for t in range(TPC):
                D, M = R[:, 0, t, :], R[:, 1, t, :]
                dve.wait_ge(last_out, t + 1)
                ch.link(nc.vector.tensor_tensor(D, D, x3[:, t, :], ALU.add))
                ins = nc.vector.tensor_tensor(D, D, M, ALU.add)
            ins.then_inc(fin_ready, 1)
            ch.end(1)

        @block.tensor
        def _(pe):
            mm = nc.tensor.matmul

            pe.wait_ge(small_in, 32)
            for k in range(FB):
                for f in range(FB):
                    ins = mm(ps[:, 7, 2 * k:2 * k + 2], w3t_sb[:, f, k * P:(k + 1) * P], a_sb[:, f, :],
                             start=(f == 0), stop=(f == FB - 1))
            ins.then_inc(wa_ps_ready, 1)
            pe.wait_ge(consts_ready, 4)
            mm(ps[:, 6, 0:NT], zeros16[:, :], zeros16[:, 0:NT], start=True, stop=False, skip_group_check=True)

            with pe.Fori(0, NT) as j:
                for q in range(NQ):
                    pe.wait_ge(cast16_done, j * NQ + (q + 1))
                    for b in range(QW // P):
                        t = q * (QW // P) + b
                        ins = mm(ps[:, 6, t:t + 1], quarter16[:, q % 2, b * P:(b + 1) * P], ones16[:, :],
                                 start=False, stop=False, skip_group_check=True)
                    ins.then_inc(deg_used, 1)
            mm(ps[:, 6, 0:NT], zeros16[:, :], zeros16[:, 0:NT], start=False, stop=True,
               skip_group_check=True).then_inc(deg_done, 1)

            def spread(out_, column):
                return mm(out_, column.to_broadcast([P, P]), ident32[:, :], start=True, stop=True,
                          skip_group_check=True)

            for l in range(4):
                def main(c, s, g, split_waits):
                    pe.wait_ge(panel_ready, c * GROUPS + (l * LG + g + 1))
                    for jj in range(PANELS):
                        j = g * PANELS + jj
                        if split_waits:
                            if l in (0, 2):
                                pe.wait_ge(split_done, (0 if l == 0 else NT) + j + 1)
                            elif j % TPC == 0:
                                pe.wait_ge(parts_in[j // TPC], 16 if l == 1 else 48)
                        if l == 0:
                            bank, fresh, end = (0, j == 0, j == NT // 2 - 1) if j < NT // 2 else (2, j == NT // 2, j == NT - 1)
                        else:
                            bank, fresh, end = 2 * s, j == 0, j == NT - 1
                        for f in range(FB):
                            for h in range(2):
                                ins = mm(ps[:, bank + f, :], parts[:, j, h, f * P:(f + 1) * P],
                                         stage[:, g % STAGES, jj, :], start=(fresh and h == 0),
                                         stop=(end and h == 1), skip_group_check=True)
                    ins.then_inc(group_done, 1)

                def own_features(c):
                    for t in range(TPC):
                        for f in range(FB):
                            for h in range(2):
                                ins = mm(ps[:, 4 + f, t * P:(t + 1) * P],
                                         parts[:, bass.ds(c * TPC + t, 1), h, f * P:(f + 1) * P].rearrange("p a f -> p (a f)"),
                                         ident16[:, :], start=(h == 0), stop=(h == 1), skip_group_check=True)
                    ins.then_inc(ht1_ready, 1)

                def project(c, prev_layer):
                    pe.wait_ge(evac_done, c * EVACS[l] + (EVAC_BASE[l] + EVACS[l]))
                    for t in range(TPC):
                        if not prev_layer:
                            pe.wait_ge(out_used[l], c * TPC + ((t | 1) - TPC + 1))
                        elif l > 0:
                            pe.wait_ge(out_used[l - 1], NT)
                        for k in range(KB[l]):
                            ins = mm(out_slot(t), T_sb[:, k, t * P:(t + 1) * P], w_sb[:, k, :],
                                     start=(k == 0), stop=(k == KB[l] - 1), skip_group_check=True)
                        ins.then_inc(out_ready, 1)

                def chunk(c, s, first, prev):
                    if l == 0:
                        if not first:
                            pe.wait_ge(evac_done, c * 2 - 1)
                    elif not first:
                        if l in (1, 2):
                            pe.wait_ge(evac_done, c * 2 + (EVAC_BASE[l] - 1))
                        if not (isinstance(c, int) and c < 2):
                            pe.wait_ge(evac_done, c * EVACS[l] + (EVAC_BASE[l] - EVACS[l]))
                    for g in range(GROUPS // 2):
                        main(c, s, g, first)
                        if g == TPC // PANELS - 1 and l in (1, 2):
                            own_features(c)
                    if prev is not None:
                        project(c - 1, prev)
                    if l == 0 and not first:
                        pe.wait_ge(evac_done, c * 2)
                    for g in range(GROUPS // 2, GROUPS):
                        main(c, s, g, first)

                if l == 3:
                    pe.wait_ge(wa_ready, 1)
                    for k in range(2):
                        for f in range(FB):
                            ins = spread(ps[:, 4, k * F + f * P:k * F + (f + 1) * P], wa_sb[:, f, k:k + 1])
                    ins.then_inc(wa_rows_ps, 1)
                chunk(0, 0, True, None)
                pe.wait_ge(weights_in, W_NEEDED[l])
                chunk(1, 1, False, True)
                chunk(2, 0, False, False)
                with pe.Fori(1, H - 1) as r:
                    chunk(r * 2 + 1, 1, False, False)
                    chunk(r * 2 + 2, 0, False, False)
                chunk(NC - 1, 1, False, False)
                project(NC - 1, False)

            def transposed(c):
                pe.wait_ge(parts_in[c], 64)
                if c >= 2:
                    pe.wait_ge(ht_evac, c - 1)
                k = 2 * (c % 2)
                for t in range(TPC):
                    for f in range(FB):
                        for h in range(2):
                            ins = mm(ps[:, k + f, t * P:(t + 1) * P], parts[:, c * TPC + t, h, f * P:(f + 1) * P],
                                     ident16[:, :], start=(h == 0), stop=(h == 1), skip_group_check=True)
                ins.then_inc(ht_ready, 1)

            def projected(j):
                if j >= 2:
                    pe.wait_ge(y_evac, j - 1)
                c, t = j // TPC, j % TPC
                for k in range(FB):
                    ins = mm(ps[:, 2 + j % 2, :], T_all[:, c, k, t * P:(t + 1) * P], wt_sb[:, k, :],
                             start=(k == 0), stop=(k == FB - 1), skip_group_check=True)
                ins.then_inc(y_ps_ready, 1)

            def spread_rows(s, c):
                pe.wait_ge(cc_ready, c + 1)
                if not (isinstance(c, int) and c == 0):
                    pe.wait_ge(att_evac, c * 2 * TPC + TPC * (s - 1))
                for q in range(2):
                    for t in range(TPC):
                        ins = spread(ps[:, 4 * s + q, t * P:(t + 1) * P], ccol[:, 2 * s + q, t:t + 1])
                ins.then_inc(ab_ps_ready, 1)

            def att_chunk(c, last):
                for s in range(2):
                    pe.wait_ge(ab_ready, c * 2 + (s + 1))
                    for j in range(NT):
                        pe.wait_ge(p_ready, c * 2 * NT + (s * NT + j + 1))
                        for t in range(TPC):
                            ins = mm(ps[:, 4 * s + t, 0:YW], E[:, j % RING, t * P:(t + 1) * P], Yb[:, j, s, :],
                                     start=(j == 0), stop=(j == NT - 1), skip_group_check=True)
                        ins.then_inc(p_used, 1)
                        if s == 0 and j == 10:
                            spread_rows(1, c)
                        if s == 1 and j == 16 and not last:
                            spread_rows(0, c + 1)

            for c in range(EARLY):
                transposed(c)
            pe.wait_ge(uv_ready, 1)
            for c in range(NC):
                if c >= 2:
                    pe.wait_ge(vb_evac, c - 1)
                for t in range(TPC):
                    ins = spread(ps[:, 6 + c % 2, t * P:(t + 1) * P], uv_sb[:, c * TPC + t, 1:2])
                ins.then_inc(vb_ps_ready, 1)
            for c in range(EARLY, NC):
                transposed(c)
            pe.wait_ge(weights_in, W_NEEDED[4])
            pe.wait_ge(ht_evac, NC)
            for j in range(NT):
                if j == ROWS_AT:
                    pe.wait_ge(vb_evac, NC)
                    spread_rows(0, 0)
                if j == NT // 2:
                    pe.wait_ge(hsum_ready, 1)
                    for k in range(FB):
                        ins = mm(ps[:, 5, :], hsum1[:, k:k + 1].to_broadcast([P, P]), wt_sb[:, k, :],
                                 start=(k == 0), stop=(k == FB - 1), skip_group_check=True)
                    ins.then_inc(my_ps_ready, 1)
                projected(j)
            pe.wait_ge(out_used[3], NT)
            pe.wait_ge(ones_set, 1)
            pe.wait_ge(y_evac, NT)
            att_chunk(0, False)
            with pe.Fori(1, NC - 1) as c:
                att_chunk(c, False)
            att_chunk(NC - 1, True)


def kernel(x, adj, L0_gnn_weightr, L0_gnn_weightd, L0_gnn_bias, L1_gnn_W1, L1_gnn_W2, L2_gnn_W, L2_gnn_b,
           L3_gnn_W, L3_gnn_a, L3_gnn_wtrans):
    import numpy as np
    import concourse.bacc as bacc
    from concourse.bass_utils import run_bass_kernel_spmd

    x, adj = np.asarray(x), np.asarray(adj)
    F = x.shape[1]
    arrays = {
        "x": x,
        "adj_t": np.ascontiguousarray(adj.T),
        "adj": adj,
        "w_gcn": np.concatenate([np.asarray(L0_gnn_weightr), np.asarray(L0_gnn_weightd)], axis=0),
        "b_gcn": np.asarray(L0_gnn_bias),
        "w_conv1": np.asarray(L1_gnn_W1),
        "w_conv2": np.asarray(L1_gnn_W2),
        "w_gcn2": np.ascontiguousarray(np.asarray(L2_gnn_W).T),
        "b_gcn2": np.asarray(L2_gnn_b),
        "w_att_t": np.ascontiguousarray(np.asarray(L3_gnn_W).T),
        "a_att": np.ascontiguousarray(np.asarray(L3_gnn_a).reshape(2, F).T),
        "w_trans": np.asarray(L3_gnn_wtrans),
    }
    nc = bacc.Bacc("TRN2", target_bir_lowering=False, num_devices=1)
    args = [nc.dram_tensor(f"in_{n}", a.shape, mybir.dt.from_np(a.dtype), kind="ExternalInput").ap()
            for n, a in arrays.items()]
    out = nc.dram_tensor("out", x.shape, mybir.dt.float32, kind="ExternalOutput").ap()
    gnn_stack(nc, *args, out)
    r = run_bass_kernel_spmd(nc, [{f"in_{n}": a for n, a in arrays.items()}], core_ids=[0])
    return r.results[0]["out"]
```

```python
import concourse.bass as bass
from concourse import mybir
from contextlib import ExitStack

P = 128


def gnn_stack(nc, x_in, adj_t, adj, w_gcn, b_gcn, w_conv1, w_conv2, w_gcn2, b_gcn2,
              w_att_t, a_att, w_trans, out):
    f32, f16, bf16, u8, i32 = (mybir.dt.float32, mybir.dt.float16, mybir.dt.bfloat16,
                               mybir.dt.uint8, mybir.dt.int32)
    ALU, ACT, AX = mybir.AluOpType, mybir.ActivationFunctionType, mybir.AxisListType

    N, F = x_in.shape
    NT = N // P
    CH = 512
    NC = N // CH
    TPC = CH // P
    FB = F // P
    PANELS = 2
    GROUPS = NT // PANELS
    STAGES = 4
    NQ = 4
    HALF = N // 2
    YW = F + 1
    RING = 8
    EPS = 1e-5
    SC = 2048.0
    BIG = 3e38
    EVACS = [2, 2, 2, 1]
    KB = [4, 4, 4, 2]
    EARLY = 5
    ROWS_AT = NT - 3
    WQ = 4

    xs = nc.dram_tensor("x_spill", (N, F), f32).ap()
    hs = nc.dram_tensor("h_spill", (N, F), f32).ap()

    def chunk_rows(t, c):
        return t.rearrange("(c t p) f -> c p t f", p=P, t=TPC)[c, :, :, :]

    ctx = ExitStack()
    with ctx:
        def sb(name, shape, dt):
            return ctx.enter_context(nc.sbuf_tensor(name, shape, dt))

        def sem(name):
            return ctx.enter_context(nc.semaphore(name))

        Y_WORDS = NT * 2 * YW
        big = sb("big", [P, Y_WORDS + NT * CH], f32)
        feat = sb("feat", [P, NT * F], f32)
        work = sb("work", [P, 10240], f32)

        def words(t, lo, n):
            return t[:, lo:lo + n]

        adj8 = words(big, 0, N * NT // 4).bitcast(u8).rearrange("p (j n) -> p j n", j=NT)
        feat32 = feat[:, :].rearrange("p (j f) -> p j f", j=NT)
        parts = feat[:, :].bitcast(f16).rearrange("p (j h f) -> p j h f", j=NT, h=2)
        T_all = words(big, Y_WORDS + NT * CH // 2, NT * F).rearrange("p (c k n) -> p c k n", c=NC, k=FB)
        T_sb = words(work, 0, 2048).rearrange("p (k n) -> p k n", k=4)
        stage = words(work, 2048, 2048).bitcast(bf16).rearrange("p (s j n) -> p s j n", s=STAGES, j=PANELS)
        h_ring = words(work, 4096, 2048).bitcast(f16).rearrange("p (s t h f) -> p s t h f", s=2, t=TPC, h=2)
        g_ring = words(work, 4096, 2048).rearrange("p (s t f) -> p s t f", s=2, t=TPC)
        x_ring = words(work, 6144, 2048).rearrange("p (s t f) -> p s t f", s=2, t=TPC)
        w_sb = words(work, 8192, 1024).rearrange("p (k f) -> p k f", k=4)
        wa_rows = words(work, 8192 + 2 * F, 2 * F).rearrange("p (s f) -> p s f", s=2)
        bias_row = words(work, 9216, F)
        y_tmp = words(work, 9216 + F, F)
        hs32 = words(work, 9216 + 2 * F, 2 * F).rearrange("p (s f) -> p s f", s=2)
        piece = words(work, 0, NQ * PANELS * CH).rearrange("p (q j n) -> p q j n", q=NQ, j=PANELS)
        piece16 = words(work, 8192, PANELS * CH).bitcast(bf16).rearrange("p (s j n) -> p s j n", s=2, j=PANELS)
        stage0 = words(work, 4096, PANELS * CH).bitcast(bf16).rearrange("p (s j n) -> p s j n", s=2, j=PANELS)
        first_half1 = words(work, 4096 + PANELS * CH, FB * CH).rearrange("p (k n) -> p k n", k=FB)
        Yb = words(big, 0, Y_WORDS).rearrange("p (j s f) -> p j s f", j=NT, s=2)
        mask = words(big, Y_WORDS, NT * CH).rearrange("p (j n) -> p j n", j=NT)
        wt_sb = words(work, 8192, 1024).rearrange("p (k f) -> p k f", k=FB)
        t_row = words(work, 0, 4096)
        E = words(work, 4096, RING * CH).rearrange("p (s n) -> p s n", s=RING)
        R = words(work, 8192, 2 * TPC * F).rearrange("p (s t f) -> p s t f", s=2, t=TPC)
        rows = words(feat, 0, 2 * HALF).rearrange("p (s n) -> p s n", s=2)
        AB = words(feat, 4096, WQ * CH).rearrange("p (q n) -> p q n", q=WQ)
        junk = words(feat, 6144, HALF // 4).bitcast(u8)
        mean_y = words(feat, 6656, F)
        x3 = words(feat, 6912, TPC * F).rearrange("p (t f) -> p t f", t=TPC)
        att_cols = words(feat, 7936, 256)
        u_col = att_cols[:, 0:NT]
        v_8 = att_cols[:, NT:3 * NT].rearrange("p (s j) -> p s j", s=2)
        v_2 = att_cols[:, 3 * NT:5 * NT].rearrange("p (s j) -> p s j", s=2)
        tmx = att_cols[:, 160:168].rearrange("p (t h) -> p t h", h=2)
        tmn = att_cols[:, 168:176].rearrange("p (t h) -> p t h", h=2)
        ccol = att_cols[:, 176:176 + 32].rearrange("p (q t) -> p q t", t=TPC)
        rz = att_cols[:, 208:216].rearrange("p (s t) -> p s t", s=2)
        zeros16 = sb("zeros16", [P, P], f16)
        ident16 = sb("ident16", [P, P], f16)
        ident32 = sb("ident32", [P, P], f32)
        first_half2 = sb("first_half2", [P, FB, CH], f32)
        w3t_sb = first_half2[:, 0, :].rearrange("p (k f) -> p k f", k=FB)
        a_sb = sb("a_sb", [P, FB, 2], f32)
        wa_sb = sb("wa_sb", [P, FB, 2], f32)
        ones16 = sb("ones16", [P, 1], bf16)
        dinv = sb("dinv", [P, NT], f32)
        dsc = sb("dsc", [P, NT], f32)
        lone = sb("lone", [P, NT], f32)
        gmax = sb("gmax", [P, NT], f32)
        uv_sb = sb("uv_sb", [P, NT, 2], f32)
        load_cols = sb("load_cols", [P, 3, 2, TPC], f32)
        stat = sb("stat", [P, TPC, 6], f32)
        mv = sb("mv", [P, TPC, 2], f32)
        mean_c, var_c = mv[:, :, 0], mv[:, :, 1]
        ln = sb("ln", [P, 5, TPC], f32)
        var_e, std, rough, scale_c, shift_c = (ln[:, k, :] for k in range(5))
        sc = sb("sc", [P, 16], f32)
        g_own, g_all, g_pow, g_scale, g_inv = (sc[:, k:k + 1] for k in range(5))
        v_hi, v_lo, v_rng, v_r, v_R, v_c1, v_c2, v_nR = (sc[:, k:k + 1] for k in range(5, 13))
        vext = sb("vext", [P, 2, NC], f32)
        hsum = sb("hsum", [P, FB, NC], f32)
        hsum1 = sb("hsum1", [P, FB], f32)

        ps = ctx.enter_context(nc.psum_tensor("ps", [P, 8, 512], f32))

        def out_slot(t):
            return ps[:, 6 + t // 2, (t % 2) * F:(t % 2 + 1) * F]

        piece_in = [sem(f"piece_in{q}") for q in range(NQ)]
        small_in, weights_in = sem("small_in"), sem("weights_in")
        x_in_s = [sem(f"x_in{s}") for s in range(2)]
        parts_in = [sem(f"parts_in{c}") for c in range(NC)]
        x_out = [sem(f"x_out{s}") for s in range(2)]
        h_out = [sem(f"h_out{s}") for s in range(2)]
        memset_done, consts_ready = sem("memset_done"), sem("consts_ready")
        cast8_done, cast16_done = sem("cast8_done"), sem("cast16_done")
        diag_done = sem("diag_done")
        blk_staged, blk_used, half_saved = sem("blk_staged"), sem("blk_used"), sem("half_saved")
        deg_used, deg_done = sem("deg_used"), sem("deg_done")
        lncol_ready, h0_done = sem("lncol_ready"), sem("h0_done")
        var_ready, std_ready = sem("var_ready"), sem("std_ready")
        wa_ps_ready, wa_ready = sem("wa_ps_ready"), sem("wa_ready")
        wa_rows_ps, wa_rows_ready = sem("wa_rows_ps"), sem("wa_rows_ready")
        dve_step = sem("dve_step")
        scaled_ready, hi_split, split_done = sem("scaled_ready"), sem("hi_split"), sem("split_done")
        panel_ready, group_done = sem("panel_ready"), sem("group_done")
        ht1_ready, evac_done, out_ready = sem("ht1_ready"), sem("evac_done"), sem("out_ready")
        out_used = [sem(f"out_used{l}") for l in range(4)]
        hs_ready, hi_ready, post_done = sem("hs_ready"), sem("hi_ready"), sem("post_done")
        gown_ready, gall_ready = sem("gown_ready"), sem("gall_ready")
        ht_ready, ht_evac, ht_summed = sem("ht_ready"), sem("ht_evac"), sem("ht_summed")
        y_ps_ready, y_evac, uv_ready, cols_ready = sem("y_ps_ready"), sem("y_evac"), sem("uv_ready"), sem("cols_ready")
        hsum_ready, my_ps_ready, my_ready = sem("hsum_ready"), sem("my_ps_ready"), sem("my_ready")
        vb_ps_ready, vb_evac, ones_set = sem("vb_ps_ready"), sem("vb_evac"), sem("ones_set")
        mask_in = [sem(f"mask_in{g}") for g in range(NC)]
        row_in = [sem(f"row_in{h}") for h in range(2)]
        row_used = sem("row_used")
        cc_ready, ab_ps_ready, ab_ready = sem("cc_ready"), sem("ab_ps_ready"), sem("ab_ready")
        mask_ready, edge_ready = sem("mask_ready"), sem("edge_ready")
        lin_ready, p_ready, p_used = sem("lin_ready"), sem("p_ready"), sem("p_used")
        rz_ready, att_evac = sem("rz_ready"), sem("att_evac")
        pool_step, elu_in, elu_out, neg_ready = sem("pool_step"), sem("elu_in"), sem("elu_out"), sem("neg_ready")
        last_in, last_out = sem("last_in"), sem("last_out")
        x3_in, fin_ready, fin_out = sem("x3_in"), sem("fin_ready"), sem("fin_out")

        def wait(eng, s, v):
            if not isinstance(v, int) or v > 0:
                eng.wait_ge(s, v)

        block = ctx.enter_context(nc.Block())

        LG = NC * GROUPS
        AHEAD_CHUNKS = 2
        AHEAD_GROUPS = AHEAD_CHUNKS * GROUPS + GROUPS // 2
        def staged(l):
            return l * LG - AHEAD_GROUPS
        EVAC_BASE = [NC * sum(EVACS[:l]) for l in range(5)]
        X_USES = {0: 1, 2: 2, 3: 3}
        X_STORES = {0: 0, 2: 1, 3: 2}
        HI_BASE = {0: 0, 2: NT, 3: 2 * NT}
        W_NEEDED = [32, 48, 64, 96, 128]
        H = NC // 2

        def blocks(k):
            early = {1: [(1, 0), (1, 2)], 2: [(2, 0), (2, 2), (2, 4), (2, 6)], 3: [(2, 8), (2, 10)]}.get(k, [])
            into = [i for i in range(AHEAD_CHUNKS) if i <= k] + ([2] if k == 3 else [])
            return early + [(i, k * TPC + pair) for pair in range(0, TPC, PANELS) for i in into]

        def blocks_before(k):
            return sum(len(blocks(kk)) for kk in range(k))

        STAGE_AT = {0: (6, 12), 1: (1, 3, 6, 8, 12, 14), 2: (1, 2, 4, 6, 8, 10, 12, 14),
                    3: (1, 2, 6, 8, 11, 13, 14, 15)}
        TAKE_AT = {0: (10, 14), 1: (4, 6, 10, 12, 14, 15), 2: (2, 4, 6, 8, 10, 12, 14, 15),
                   3: (2, 4, 10, 12, 13, 14, 15, 15)}

        def blocks_at(k, g, times, otherwise):
            n = blocks_before(k)
            return [(n + m, block) for m, (at, block) in enumerate(zip(times.get(k, otherwise), blocks(k))) if at == g]

        def staged_at(k, g):
            return blocks_at(k, g, STAGE_AT, (6, 8, 12, 14))

        def taken_at(k, g):
            return blocks_at(k, g, TAKE_AT, (10, 12, 14, 15))

        last_blocks = [(blocks_before(NC - 1) + m, block) for m, block in enumerate(blocks(NC - 1))]

        @block.sync
        def _(sp):
            def load_piece(c, g):
                sp.dma_start(piece[:, g % NQ, :, :], adj_t.rearrange("(g j p) (c n) -> g c p j n", p=P, j=PANELS, n=CH)
                             [g, c, :, :, :]).then_inc(piece_in[g % NQ], 16)

            def load_x(src, c, s):
                sp.dma_start(x_ring[:, s, :, :], chunk_rows(src, c)).then_inc(x_in_s[s], 16)

            def load_weights(l):
                src = [w_gcn, w_conv1, w_conv2, w_gcn2][l]
                sp.dma_start(w_sb[:, 0:KB[l], :], src.rearrange("(k p) f -> p k f", p=P)).then_inc(weights_in, 16)
                if l in (0, 3):
                    sp.dma_start(bias_row, (b_gcn if l == 0 else b_gcn2).partition_broadcast(P)).then_inc(weights_in, 16)

            load_x(x_in, 0, 0)
            for g in range(NQ):
                load_piece(0, g)
            load_x(x_in, 1, 1)
            sp.dma_start(w3t_sb[:, :, :], w_att_t.rearrange("(k p) f -> p k f", p=P)).then_inc(small_in, 16)
            sp.dma_start(a_sb[:, :, :], a_att.rearrange("(k p) f -> p k f", p=P)).then_inc(small_in, 16)

            def pieces(c, first=0):
                for g in range(first, GROUPS):
                    sp.wait_ge(cast8_done, c * GROUPS + (g - NQ + 1))
                    sp.wait_ge(cast16_done, c * GROUPS + (g - NQ + 1))
                    load_piece(c, g)

            pieces(0, NQ)
            with sp.Fori(0, H - 1) as r:
                for s in range(2):
                    pieces(2 * r + s + 1)
                    sp.wait_ge(h0_done, (2 * r + s + 1) * TPC)
                    load_x(x_in, 2 * r + s + 2, s)
            pieces(NC - 1)
            for s in range(2):
                sp.wait_ge(h0_done, (NC - 1 + s) * TPC)
                load_x(x_in, s, s)
            sp.wait_ge(deg_done, NC)
            load_weights(0)

            def reload(l, c):
                sp.wait_ge(group_done, staged(l) + (NC - 1) * GROUPS + (c + 1) * TPC // PANELS)
                sp.wait_ge(h_out[c % 2], 16 * (l * H + c // 2 + 1))
                sp.dma_start(feat32[:, c * TPC:(c + 1) * TPC, :], chunk_rows(hs, c)).then_inc(parts_in[c], 16)

            for l in range(4):
                nxt = {0: None, 1: (2, xs), 2: (3, xs), 3: None}[l]

                def store(c, s):
                    sp.wait_ge(post_done, l * NC + c + 1)
                    if l != 1:
                        sp.dma_start(chunk_rows(xs, c), x_ring[:, s, :, :]).then_inc(x_out[s], 16)
                    sp.dma_start(chunk_rows(hs, c), g_ring[:, s, :, :]).then_inc(h_out[s], 16)

                def refill(c, s, cc):
                    sp.wait_ge(x_out[s], 16 * (X_STORES[l] * H + cc + 1))
                    load_x(x_in if l == 0 else xs, c + 2, s)

                with sp.Fori(0, H - 1) as r:
                    for s in range(2):
                        store(2 * r + s, s)
                        if l != 1:
                            refill(2 * r + s, s, r)
                for c in range(4):
                    reload(l, c)
                store(NC - 2, 0)
                for c in range(4, NC - 1):
                    reload(l, c)
                store(NC - 1, 1)
                reload(l, NC - 1)
                if l != 1:
                    for s in range(2):
                        sp.wait_ge(x_out[s], 16 * (X_STORES[l] + 1) * H)
                if l in (0, 2):
                    for s in range(2):
                        load_x(xs, s, s)
                sp.wait_ge(out_ready, (l + 1) * NT)
                if l < 3:
                    load_weights(l + 1)
            sp.wait_ge(uv_ready, 1)
            for s in range(2):
                sp.dma_start(wt_sb[:, :, s * F:(s + 1) * F],
                             w_trans[s * F:(s + 1) * F, :].rearrange("(k p) f -> p k f", p=P)).then_inc(weights_in, 16)

            def load_mask(c, g):
                src = adj_t.rearrange("(g t p) (c n) -> g c p t n", p=P, t=TPC, n=CH)
                sp.dma_start(mask[:, g * TPC:(g + 1) * TPC, :], src[g, c, :, :, :]).then_inc(mask_in[g], 16)

            def load_row(i, h):
                sp.dma_start(rows[:, h, :], adj.rearrange("(i p) (h n) -> i h p n", p=P, h=2)[i, h, :, :])\
                  .then_inc(row_in[h], 16)

            sp.wait_ge(panel_ready, staged(4))
            for g in range(NC // 2):
                load_mask(0, g)
            sp.wait_ge(ht_ready, NC)
            for h in range(2):
                load_row(0, h)

            def next_row(i, h):
                sp.wait_ge(row_used, (i - 1) * 4 + 2 * h + 2)
                load_row(i, h)

            for i in range(1, TPC + 1):
                for h in range(2):
                    next_row(i, h)
            sp.wait_ge(y_ps_ready, NT)
            for g in range(NC // 2, NC):
                load_mask(0, g)

            def att_loads(c, first, last):
                for t in range(1 if first else 2, TPC):
                    for h in range(2):
                        next_row((c + 1) * TPC + t, h)
                rows_after = {} if last else {0: (0, 0), 2: (0, 1), 5: (1, 0), 6: (1, 1)}
                for g in range(NC):
                    sp.wait_ge(lin_ready, c * NT + (NT + (g + 1) * TPC) // 2)
                    load_mask(c + 1, g)
                    if g in rows_after:
                        t, h = rows_after[g]
                        next_row((c + 2) * TPC + t, h)

            att_loads(0, True, False)
            with sp.Fori(1, NC - 2) as c:
                att_loads(c, False, False)
            att_loads(NC - 2, False, True)
            for s in range(2):
                sp.wait_ge(x_out[s], 16 * 3 * H)
                sp.wait_ge(h_out[s], 16 * 4 * H)

        @block.gpsimd
        def _(pool):
            nc.gpsimd.memset(zeros16[:, :], 0.0).then_inc(consts_ready, 1)
            nc.gpsimd.memset(ident16[:, :], 0.0).then_inc(memset_done, 1)
            nc.gpsimd.memset(ident32[:, :], 0.0).then_inc(memset_done, 1)
            nc.gpsimd.memset(ones16[:, :], 1.0).then_inc(consts_ready, 1)
            pool.wait_ge(memset_done, 2)
            for eye in (ident16, ident32):
                nc.gpsimd.affine_select(out=eye[:, :], in_=eye[:, :], compare_op=ALU.not_equal, fill=1.0, base=0,
                                        pattern=[[-1, P]], channel_multiplier=1).then_inc(consts_ready, 1)
            pool.wait_ge(gown_ready, 1)
            nc.gpsimd.partition_all_reduce(g_all, g_own, P, bass.bass_isa.ReduceOp.max).then_inc(gall_ready, 1)

            pool.wait_ge(panel_ready, staged(4))
            nc.gpsimd.memset(Yb[:, :, :, F:YW], 1.0).then_inc(ones_set, 1)
            pool.wait_ge(my_ready, 1)

            K = 4

            with pool.Fori(0, NC - 1) as c:
                k = [0]

                def link(ins):
                    k[0] += 1
                    ins.then_inc(pool_step, 1)
                    pool.wait_ge(pool_step, c * K + k[0])

                D, M = R[:, 0, :, :], R[:, 1, :, :]
                pool.wait_ge(att_evac, c * 2 * TPC + 2 * TPC)
                link(nc.gpsimd.tensor_tensor(D, D, M, ALU.add))
                link(nc.gpsimd.tensor_tensor(M, mean_y.rearrange("p (a f) -> p a f", a=1).to_broadcast([P, TPC, F]),
                                             lone[:, bass.ds(c * TPC, TPC)].rearrange("p (t a) -> p t a", a=1)
                                             .to_broadcast([P, TPC, F]), ALU.mult))
                nc.gpsimd.tensor_tensor(D, D, M, ALU.add).then_inc(elu_in, 1)
                pool.wait_ge(x3_in, c * 16 + 16)
                link(nc.gpsimd.tensor_tensor(x3, x3, ones16[:, 0:1].rearrange("p (t a) -> p t a", a=1)
                                             .to_broadcast([P, TPC, F]), ALU.subtract))
                pool.wait_ge(elu_out, c + 1)
                link(nc.gpsimd.tensor_tensor(D, D, x3, ALU.add))
                nc.gpsimd.tensor_tensor(D, D, M, ALU.add).then_inc(fin_ready, 1)

        @block.scalar
        def _(act):
            def copy(out_, in_, **kw):
                return nc.scalar.activation(out_, in_, ACT.Copy, **kw)

            def std_of(n, out_=std, in_=var_e):
                act.wait_ge(var_ready, n)
                nc.scalar.activation(out_, in_, ACT.Sqrt).then_inc(std_ready, 1)

            def first_tile(c, t):
                j = c * TPC + t
                if t == 0:
                    act.wait_ge(lncol_ready, c + 1)
                wait(act, split_done, j - 1)
                nc.scalar.activation(hs32[:, t % 2, :], x_ring[:, c % 2, t, :], ACT.Relu,
                                     bias=shift_c[:, t:t + 1], scale=scale_c[:, t:t + 1]).then_inc(h0_done, 1)
                act.wait_ge(h0_done, j + 1)
                copy(parts[:, j, 0, :], hs32[:, t % 2, :]).then_inc(hi_split, 1)

            values, roots = load_cols[:, 0, :, :], load_cols[:, 1, :, :]
            for c in range(NC):
                for g in range(GROUPS):
                    n = c * GROUPS + g
                    act.wait_ge(piece_in[g % NQ], (n // NQ + 1) * 16)
                    wait(act, deg_used, n - 1)
                    copy(piece16[:, g % 2, :, :], piece[:, g % NQ, :, :]).then_inc(cast16_done, 1)
                    if c > 0 and g == 2:
                        std_of(c, roots, values)
                    if c > 0 and g in (5, 7, 9, 11):
                        first_tile(c - 1, (g - 5) // 2)
                    if c == 0 and g == GROUPS - 1:
                        act.wait_ge(wa_ps_ready, 1)
                        copy(wa_sb[:, :, :], ps[:, 3, 0:2 * FB].rearrange("p (k s) -> p k s", s=2)).then_inc(wa_ready, 1)
                    if c == H + 1 and g == 3:
                        act.wait_ge(blk_used, blocks_before(H))
                        copy(first_half1, ps[:, 4:6, :]).then_inc(half_saved, 1)
                    if c == H + 1 and g == 6:
                        copy(first_half2[:, :, :], ps[:, 2:4, :]).then_inc(half_saved, 1)
            std_of(NC, roots, values)
            for t in range(TPC):
                first_tile(NC - 1, t)

            def split_hi(j):
                act.wait_ge(scaled_ready, j + 1)
                copy(parts[:, j, 0, :], hs32[:, j % 2, :]).then_inc(hi_split, 1)

            def ht_copy(c):
                if c == 0:
                    act.wait_ge(panel_ready, staged(4))
                act.wait_ge(ht_ready, c + 1)
                k = 2 * (c % 2)
                copy(T_all[:, c, :, :], ps[:, k:k + 2, :]).then_inc(ht_evac, 1)

            act.wait_ge(diag_done, NT)
            for l in range(4):

                def stage_groups(c, lo, hi, l=l):
                    if lo == 0 and l in (1, 3):
                        act.wait_ge(diag_done, c + (NT + 1 if l == 1 else NT + NC + 1))
                    for g in range(lo, hi):
                        n = c * GROUPS + (staged(l) + g)
                        wait(act, group_done, n - (STAGES - 1))
                        copy(stage[:, g % STAGES, :, :],
                             adj8[:, g * PANELS:(g + 1) * PANELS, bass.ts(c, CH)]).then_inc(panel_ready, 1)

                def evac(c, e, s):
                    if e == 0:
                        wait(act, out_ready, c * TPC + l * NT)
                    if l in (1, 2) and e == 0:
                        act.wait_ge(ht1_ready, c + (NC * (l - 1) + 1))
                        bank = 4
                    else:
                        half = GROUPS // 2 if (l == 0 and e == 0) else GROUPS
                        if l == 0 and isinstance(c, int) and (c < AHEAD_CHUNKS or (c == 2 and e == 0)):
                            act.wait_ge(blk_used, AHEAD_GROUPS)
                        else:
                            act.wait_ge(group_done, c * GROUPS + (staged(l) + half))
                        bank = 2 * e if l == 0 else 2 * s
                        if l == 0 and isinstance(c, int) and c in (1, 2) and e == 0:
                            act.wait_ge(half_saved, 2)
                            copy(T_sb[:, 0:2, :], first_half1 if c == 1 else first_half2[:, :, :]).then_inc(evac_done, 1)
                            return
                        if l == 0 and isinstance(c, int) and c == 1:
                            bank = 4
                    copy(T_sb[:, 2 * e:2 * e + 2, :], ps[:, bank:bank + 2, :]).then_inc(evac_done, 1)

                def post_std(c):
                    if l != 1:
                        std_of(c + (NC + 1 + HI_BASE[l] // TPC))

                def post(c, s, cc, tiles):
                    if tiles[0] == 0:
                        wait(act, h_out[s], cc * 16 + 16 * H * l)
                    for t in tiles:
                        if l == 1:
                            act.wait_ge(out_ready, c * TPC + (NT + (t | 1) + 1))
                            nc.scalar.activation(g_ring[:, s, t, :], out_slot(t), ACT.Relu, scale=1.0 / SC)\
                              .then_inc(out_used[1], 1)
                        else:
                            act.wait_ge(hs_ready, c * TPC + (HI_BASE[l] + t + 1))
                            nc.scalar.activation(h_ring[:, s, t, 0, :], hs32[:, t % 2, :], ACT.Relu)\
                              .then_inc(hi_ready, 1)

                def chunk(c, s, cc_prev, last=False, staged=4):
                    stage_groups(c, staged, 12)
                    if EVACS[l] == 2:
                        evac(c, 0, s)
                    stage_groups(c, 12, 14)
                    if cc_prev is not None:
                        post_std(c - 1)
                    stage_groups(c, 14, 16)
                    if cc_prev is not None:
                        post(c - 1, 1 - s, cc_prev, (0, 1))
                    if not last:
                        stage_groups(c + 1, 0, 2)
                    if cc_prev is not None:
                        post(c - 1, 1 - s, cc_prev, (2, 3))
                    if not last:
                        stage_groups(c + 1, 2, 4)
                    evac(c, EVACS[l] - 1, s)

                if l == 0:
                    act.wait_ge(cast8_done, NC * GROUPS)
                    half = GROUPS // 2
                    stage_groups(2, half, half + 4)
                    evac(0, 0, 0)
                    evac(0, 1, 0)
                    evac(1, 0, 0)
                    evac(1, 1, 0)
                    stage_groups(2, half + 4, half + 6)
                    post_std(0)
                    stage_groups(2, half + 6, half + 7)
                    post(0, 0, 0, (0, 1))
                    stage_groups(2, half + 7, half + 8)
                    evac(2, 0, 0)
                    post(0, 0, 0, (2, 3))
                    stage_groups(3, 0, 3)
                    evac(2, 1, 0)
                    stage_groups(3, 3, 6)
                    post_std(1)
                    stage_groups(3, 6, 7)
                    post(1, 1, 0, (0, 1))
                    stage_groups(3, 7, 8)
                    post(1, 1, 0, (2, 3))
                    chunk(3, 1, 1, staged=8)
                    chunk(4, 0, 1)
                elif l == 2:
                    stage_groups(0, 0, 2)
                    for g in range(GROUPS):
                        for t in range(PANELS):
                            split_hi(g * PANELS + t)
                        if 0 < g < GROUPS - 1:
                            stage_groups(0, g + 1, g + 2)
                        if g == GROUPS // 2 + 2:
                            evac(0, 0, 0)
                    stage_groups(1, 0, 4)
                    evac(0, 1, 0)
                else:
                    chunk(0, 0, None, staged=7)
                if l > 0:
                    chunk(1, 1, 0)
                    chunk(2, 0, 0)
                with act.Fori(2 if l == 0 else 1, H - 1) as r:
                    chunk(r * 2 + 1, 1, r)
                    chunk(r * 2 + 2, 0, r)
                chunk(NC - 1, 1, H - 1, last=True)
                if l in (0, 2):
                    stage_groups(0, 0, 4, l + 1)
                if l == 3:
                    ht_copy(0)
                post_std(NC - 1)
                if l in (0, 2):
                    stage_groups(0, 4, 6, l + 1)
                if l == 2:
                    act.wait_ge(wa_rows_ps, 1)
                    copy(wa_rows, ps[:, 4, :].rearrange("p (s f) -> p s f", s=2)).then_inc(wa_rows_ready, 1)
                if l == 3:
                    ht_copy(1)
                post(NC - 1, 1, H - 1, (0, 1))
                if l in (0, 2):
                    stage_groups(0, 6, 7, l + 1)
                post(NC - 1, 1, H - 1, (2, 3))

            for c in range(2, EARLY):
                ht_copy(c)
            act.wait_ge(out_ready, 4 * NT)
            for c in range(NC):
                act.wait_ge(vb_ps_ready, c + 1)
                copy(t_row[:, c * CH:(c + 1) * CH], ps[:, 6 + c % 2, :]).then_inc(vb_evac, 1)
            for c in range(EARLY, NC):
                ht_copy(c)
            def rows_copy(s, n):
                act.wait_ge(ab_ps_ready, n)
                copy(AB[:, 2 * s:2 * s + 2, :], ps[:, 4 * s:4 * s + 2, :]).then_inc(ab_ready, 1)

            def mask_exponents(c, g):
                act.wait_ge(mask_in[g], c * 16 + 16)
                m = mask[:, g * TPC:(g + 1) * TPC, :]
                copy(m, m, scale=BIG, bias=-BIG).then_inc(mask_ready, 1)

            mask_exponents(0, 0)
            for j in range(NT):
                if j == ROWS_AT:
                    rows_copy(0, 1)
                act.wait_ge(y_ps_ready, j + 1)
                copy(Yb[:, j, :, 0:F], ps[:, 2 + j % 2, :].rearrange("p (s f) -> p s f", s=2),
                     scale=1.0 / SC).then_inc(y_evac, 1)

            def averages(c, s):
                act.wait_ge(rz_ready, c * 2 + (s + 1))
                if s == 0:
                    wait(act, fin_out, c * 16)
                else:
                    wait(act, fin_ready, c)
                for t in range(TPC):
                    nc.scalar.activation(R[:, s, t, :], ps[:, 4 * s + t, 0:F], ACT.Copy, scale=rz[:, s, t:t + 1])\
                      .then_inc(att_evac, 1)

            def elu_exp(c):
                D, M = R[:, 0, :, :], R[:, 1, :, :]
                act.wait_ge(elu_in, c + 1)
                nc.scalar.activation(M, D, ACT.Relu, scale=-1.0).then_inc(neg_ready, 1)
                nc.scalar.activation(D, D, ACT.Relu)
                act.wait_ge(neg_ready, c + 1)
                nc.scalar.activation(M, M, ACT.Exp, scale=-1.0).then_inc(elu_out, 1)

            def store_result(c):
                act.wait_ge(fin_ready, c + 1)
                act.dma_start(chunk_rows(out, c), R[:, 0, :, :]).then_inc(fin_out, 16)

            def load_x3(c):
                act.dma_start(x3, chunk_rows(xs, c)).then_inc(x3_in, 16)

            def att_chunk(c, first, last):
                for s in range(2):
                    for j in range(NT):
                        if j % 2 == 0:
                            act.wait_ge(lin_ready, c * NT + (s * NT + j) // 2 + 1)
                        nc.scalar.activation(E[:, j % RING, :], E[:, j % RING, :], ACT.Exp, bias=v_2[:, s, j:j + 1])\
                          .then_inc(p_ready, 1)
                        if s == 0 and j % TPC == 0 and j // TPC + 1 < NC:
                            mask_exponents(c, j // TPC + 1)
                        if s == 1 and j == NT - 1 and not last:
                            mask_exponents(c + 1, 0)
                        if s == 0:
                            if j == 9 and not first:
                                averages(c - 1, 1)
                            if j == 14:
                                wait(act, lin_ready, c * NT)
                                rows_copy(1, c * 2 + 2)
                            if j == 22 and not first:
                                elu_exp(c - 1)
                            if j == 28 and not first:
                                store_result(c - 1)
                                load_x3(c)
                        else:
                            if j == 9:
                                averages(c, 0)
                            if j == 24 and not last:
                                rows_copy(0, c * 2 + 3)

            act.wait_ge(cols_ready, 1)
            load_x3(0)
            att_chunk(0, True, False)
            with act.Fori(1, NC - 1) as c:
                att_chunk(c, False, False)
            att_chunk(NC - 1, False, True)
            for t in range(TPC):
                D, M = R[:, 0, t, :], R[:, 1, t, :]
                act.wait_ge(last_in, t + 1)
                nc.scalar.activation(M, D, ACT.Relu, scale=-1.0).then_inc(neg_ready, 1)
                nc.scalar.activation(D, D, ACT.Relu)
                act.wait_ge(neg_ready, NC + t)
                nc.scalar.activation(M, M, ACT.Exp, scale=-1.0).then_inc(last_out, 1)
            store_result(NC - 1)
            act.wait_ge(fin_out, 16 * NC)

        @block.vector
        def _(dve):
            steps = [0]

            class Chain:
                def __init__(self, turn, per_turn):
                    self.turn, self.per_turn, self.k = turn, per_turn, 0

                def link(self, ins):
                    self.k += 1
                    ins.then_inc(dve_step, 1)
                    dve.wait_ge(dve_step, self.turn * self.per_turn + (steps[0] + self.k))

                def end(self, turns):
                    assert self.k == self.per_turn or turns == 1
                    steps[0] += self.k * turns

            def mean_and_variance(t, link):
                link(nc.vector.bn_aggr(mv[:, t, :], stat[:, t, :]))

            def last_variance(link):
                t = TPC - 1
                nc.vector.tensor_scalar(var_e[:, 0:t], var_c[:, 0:t], EPS, None, ALU.add)
                mean_and_variance(t, link)
                nc.vector.tensor_scalar(var_e[:, t:TPC], var_c[:, t:TPC], EPS, None, ALU.add).then_inc(var_ready, 1)

            def one_over_root(n, value, root, est, link):
                dve.wait_ge(std_ready, n)
                link(nc.vector.reciprocal(est, root))
                link(nc.vector.tensor_tensor(root, est, est, ALU.mult))
                link(nc.vector.tensor_tensor(root, root, value, ALU.mult))
                link(nc.vector.tensor_scalar(root, root, -0.5, 1.5, ALU.mult, ALU.add))
                return root

            def on_diagonal(j, op):
                block = adj8[:, bass.ds(j, 1), bass.ds(j * P, P)]
                return nc.vector.tensor_tensor(block, block, ident16[:, :].rearrange("p (a n) -> p a n", a=1), op)

            dve.wait_ge(consts_ready, 4)

            ch = Chain(0, 0)
            values, roots, inverses = (load_cols[:, k, :, :] for k in range(3))

            def degrees(c):
                of = slice(c * TPC, (c + 1) * TPC)
                dve.wait_ge(deg_done, c + 1)
                ch.link(nc.vector.tensor_scalar(dsc[:, of], ps[:, 6 + c % 2, 0:TPC], 1.0, None, ALU.add))
                nc.vector.tensor_scalar(lone[:, of], dsc[:, of], 1.0, None, ALU.is_equal)
                nc.vector.tensor_scalar(values[:, 1, :], dsc[:, of], 1e-30, None, ALU.max).then_inc(var_ready, 1)

            def norm_columns(c):
                of = slice(c * TPC, (c + 1) * TPC)
                left = one_over_root(c + 1, values, roots, inverses, ch.link)
                wait(dve, h0_done, c * TPC)
                ch.link(nc.vector.tensor_tensor(inverses, inverses, left, ALU.mult))
                ch.link(nc.vector.scalar_tensor_tensor(dinv[:, of], dsc[:, of], 0.0, inverses[:, 1, :],
                                                       ALU.is_gt, ALU.mult))
                nc.vector.tensor_scalar(dsc[:, of], dinv[:, of], 1.0 / SC, None, ALU.mult)
                ch.link(nc.vector.scalar_tensor_tensor(scale_c, inverses[:, 0, :], SC, dinv[:, of], ALU.mult, ALU.mult))
                nc.vector.scalar_tensor_tensor(shift_c, mean_c, -1.0, scale_c, ALU.mult, ALU.mult)\
                  .then_inc(lncol_ready, 1)
                dve.wait_ge(lncol_ready, c + 1)

            def low_part(c, t):
                j = c * TPC + t
                dve.wait_ge(hi_split, j + 1)
                nc.vector.tensor_tensor(parts[:, j, 1, :], hs32[:, t % 2, :], parts[:, j, 0, :], ALU.subtract)\
                  .then_inc(split_done, 1)

            def stage_block(n, block, k):
                i, j = block
                dve.wait_ge(cast8_done, (k + 1) * GROUPS)
                dve.wait_ge(diag_done, (k + 1) * TPC)
                wait(dve, blk_used, n - 1)
                nc.vector.tensor_copy(stage0[:, n % 2, :, :], adj8[:, j:j + PANELS, i * CH:(i + 1) * CH])\
                  .then_inc(blk_staged, 1)

            for c in range(NC):
                for g in range(GROUPS):
                    n = c * GROUPS + g
                    dve.wait_ge(piece_in[g % NQ], (n // NQ + 1) * 16)
                    nc.vector.tensor_copy(adj8[:, g * PANELS:(g + 1) * PANELS, c * CH:(c + 1) * CH],
                                          piece[:, g % NQ, :, :]).then_inc(cast8_done, 1)
                    if g * PANELS // TPC == c:
                        dve.wait_ge(cast8_done, n + 1)
                        for j in range(g * PANELS, (g + 1) * PANELS):
                            on_diagonal(j, ALU.add).then_inc(diag_done, 1)
                    if c > 0:
                        if g == 0:
                            degrees(c - 1)
                        if g == 4:
                            norm_columns(c - 1)
                        if g in (7, 9, 11, 13):
                            low_part(c - 1, (g - 7) // 2)
                        for k, block in staged_at(c - 1, g):
                            stage_block(k, block, c - 1)
                    if g in (6, 8, 10, 12):
                        t = (g - 6) // 2
                        if t > 0:
                            mean_and_variance(t - 1, ch.link)
                        else:
                            dve.wait_ge(x_in_s[c % 2], (c // 2 + 1) * 16)
                        ch.link(nc.vector.bn_stats(stat[:, t, :], x_ring[:, c % 2, t, :]))
                    if g == 14:
                        mean_and_variance(TPC - 1, ch.link)
                        ch.link(nc.vector.tensor_scalar(values[:, 0, :], var_c, EPS, None, ALU.add))
            for n, block in last_blocks[:2]:
                stage_block(n, block, NC - 1)
            degrees(NC - 1)
            norm_columns(NC - 1)
            for t in range(TPC):
                low_part(NC - 1, t)
            for n, block in last_blocks[2:]:
                stage_block(n, block, NC - 1)
            ch.end(1)

            def split_g():
                for j in range(0, NT, 2):
                    for t in range(2):
                        if (j + t) % TPC == 0:
                            dve.wait_ge(parts_in[(j + t) // TPC], 32)
                        if j > 0:
                            dve.wait_ge(split_done, NT + j + t - 1)
                        nc.vector.tensor_scalar(hs32[:, t, :], feat32[:, j + t, :], g_scale, None, ALU.mult)\
                          .then_inc(scaled_ready, 1)
                    for t in range(2):
                        dve.wait_ge(hi_split, NT + j + t + 1)
                        nc.vector.tensor_tensor(parts[:, j + t, 1, :], hs32[:, t, :], parts[:, j + t, 0, :],
                                                ALU.subtract).then_inc(split_done, 1)

            for l in range(4):
                if l == 2:
                    ch = Chain(0, 0)
                    dve.wait_ge(post_done, 2 * NC)
                    ch.link(nc.vector.tensor_reduce(g_own, gmax[:, :], AX.X, ALU.max))
                    nc.vector.tensor_scalar(g_own, g_own, 1e-30, None, ALU.max).then_inc(gown_ready, 1)
                    dve.wait_ge(gall_ready, 1)
                    ch.link(nc.vector.tensor_scalar(g_pow.bitcast(i32), g_all.bitcast(i32), 0x7F800000, None,
                                                    ALU.bitwise_and))
                    ch.link(nc.vector.reciprocal(g_scale, g_pow))
                    ch.link(nc.vector.tensor_scalar(g_inv, g_pow, 2.0 ** -14, None, ALU.mult))
                    ch.link(nc.vector.tensor_scalar(g_scale, g_scale, 2.0 ** 14, None, ALU.mult))
                    ch.end(1)
                    split_g()
                if l in (0, 3):
                    dve.wait_ge(weights_in, W_NEEDED[l])
                if l == 3:
                    dve.wait_ge(wa_rows_ready, 1)

                PER = {0: 5 * TPC + 5, 1: 0, 2: 4 * TPC + 5, 3: 6 * TPC + 5}[l] * 2

                def post(c, s, cc, ch):
                    i0 = c * TPC
                    if l == 1:
                        for t in range(TPC):
                            dve.wait_ge(out_used[1], i0 + (t + 1))
                            ins = nc.vector.tensor_reduce(gmax[:, bass.ds(i0 + t, 1)], g_ring[:, s, t, :], AX.X, ALU.max)
                        ins.then_inc(post_done, 1)
                        return
                    dve.wait_ge(x_in_s[s], cc * 16 + 16 * (X_USES[l] * H + 1))
                    for t in range(TPC):
                        x_t, y_t, o_t = x_ring[:, s, t, :], y_tmp, out_slot(t)
                        dve.wait_ge(out_ready, i0 + (NT * l + (t | 1) + 1))
                        if l == 2:
                            nc.vector.tensor_scalar(y_t, o_t, g_inv, 0.0, ALU.mult, ALU.max).then_inc(out_used[l], 1)
                        else:
                            nc.vector.scalar_tensor_tensor(y_t, o_t, dsc[:, bass.ds(i0 + t, 1)], bias_row,
                                                           ALU.mult, ALU.add).then_inc(out_used[l], 1)
                        if t > 0:
                            mean_and_variance(t - 1, ch.link)
                        dve.wait_ge(out_used[l], i0 + (t + 1))
                        if l == 0:
                            ch.link(nc.vector.scalar_tensor_tensor(y_t, y_t, 0.01, y_t, ALU.mult, ALU.max))
                        if l == 3:
                            ch.link(nc.vector.scalar_tensor_tensor(x_t, y_t, 0.0, x_t, ALU.max, ALU.add))
                        else:
                            ch.link(nc.vector.tensor_tensor(x_t, y_t, x_t, ALU.add))
                        ch.link(nc.vector.bn_stats(stat[:, t, :], x_t))
                    last_variance(ch.link)
                    left = one_over_root(c + (NC + 1 + HI_BASE[l] // TPC), var_e, std, rough, ch.link)
                    ch.link(nc.vector.scalar_tensor_tensor(scale_c, rough, SC, left, ALU.mult, ALU.mult))
                    if l == 2:
                        ch.link(nc.vector.tensor_tensor(scale_c, scale_c, dinv[:, bass.ds(i0, TPC)], ALU.mult))
                    ch.link(nc.vector.scalar_tensor_tensor(shift_c, mean_c, -1.0, scale_c, ALU.mult, ALU.mult))

                    def scaled(t):
                        wait(dve, hi_ready, i0 + (HI_BASE[l] + t - 1))
                        nc.vector.tensor_scalar(hs32[:, t % 2, :], x_ring[:, s, t, :], scale_c[:, t:t + 1],
                                                shift_c[:, t:t + 1], ALU.mult, ALU.add).then_inc(hs_ready, 1)

                    scaled(0)
                    for t in range(TPC):
                        if t + 1 < TPC:
                            scaled(t + 1)
                        dve.wait_ge(hi_ready, i0 + (HI_BASE[l] + t + 1))
                        lo = nc.vector.scalar_tensor_tensor(h_ring[:, s, t, 1, :], hs32[:, t % 2, :], 0.0,
                                                            h_ring[:, s, t, 0, :], ALU.max, ALU.subtract)
                        if t + 1 < TPC:
                            ch.link(lo)
                        else:
                            lo.then_inc(post_done, 1)
                        if l == 3:
                            for k in range(2):
                                ch.link(nc.vector.scalar_tensor_tensor(
                                    y_tmp, hs32[:, t % 2, :], 0.0, wa_rows[:, k, :], ALU.max, ALU.mult,
                                    accum_out=uv_sb[:, bass.ds(i0 + t, 1), k]))

                    if l != 3:
                        if not (l == 0 and isinstance(c, int) and c < AHEAD_CHUNKS):
                            dve.wait_ge(panel_ready, c * GROUPS + (staged(l) + GROUPS))
                        dve.wait_ge(diag_done, NT if l == 0 else NT + NC)
                        dve.wait_ge(blk_used, AHEAD_GROUPS)
                        for t in range(TPC):
                            ins = on_diagonal(i0 + t, ALU.subtract if l == 0 else ALU.add)
                        ins.then_inc(diag_done, 1)

                if l == 2:
                    PER += 2
                ch = Chain(0, PER)
                for s in range(2):
                    post(s, s, 0, ch)
                ch.end(1)
                with dve.Fori(0, H - 1) as r:
                    ch = Chain(r, PER)
                    for s in range(2):
                        post(r * 2 + (2 + s), s, r + 1, ch)
                ch.end(H - 1)

            ch = Chain(0, 0)
            nc.vector.tensor_scalar(uv_sb[:, :, :], uv_sb[:, :, :], 1.0 / SC, None, ALU.mult).then_inc(uv_ready, 1)
            dve.wait_ge(uv_ready, 1)
            for c in range(NC):
                dve.wait_ge(vb_evac, c + 1)
                nc.vector.tensor_reduce(vext[:, 0, c:c + 1], t_row[:, c * CH:(c + 1) * CH], AX.X, ALU.max)
                ins = nc.vector.tensor_reduce(vext[:, 1, c:c + 1], t_row[:, c * CH:(c + 1) * CH], AX.X, ALU.min)
            ch.link(ins)
            nc.vector.tensor_reduce(v_hi, vext[:, 0, :], AX.X, ALU.max)
            ch.link(nc.vector.tensor_reduce(v_lo, vext[:, 1, :], AX.X, ALU.min))
            ch.link(nc.vector.tensor_tensor(v_rng, v_hi, v_lo, ALU.subtract))
            ch.link(nc.vector.tensor_scalar(v_rng, v_rng, 1e-30, None, ALU.max))
            nc.vector.tensor_scalar(v_R, v_rng, 2.0, None, ALU.mult)
            nc.vector.tensor_scalar(v_nR, v_rng, -2.0, None, ALU.mult)
            ch.link(nc.vector.reciprocal(v_r, v_rng))
            nc.vector.scalar_tensor_tensor(v_c1, v_R, -0.25, v_lo, ALU.mult, ALU.add)
            nc.vector.scalar_tensor_tensor(v_c2, v_R, 0.75, v_lo, ALU.mult, ALU.add)
            ch.link(nc.vector.tensor_scalar(v_r, v_r, 0.5, None, ALU.mult))
            ch.link(nc.vector.tensor_scalar(t_row, t_row, v_c1, v_r, ALU.subtract, ALU.mult))
            for c in range(NC):
                dve.wait_ge(ht_evac, c + 1)
                nc.vector.tensor_reduce(hsum[:, :, c:c + 1], T_all[:, c, :, :], AX.X, ALU.add).then_inc(ht_summed, 1)
            dve.wait_ge(ht_summed, NC)
            nc.vector.tensor_reduce(hsum1[:, :], hsum[:, :, :], AX.X, ALU.add).then_inc(hsum_ready, 1)
            dve.wait_ge(ht_ready, NC)
            nc.vector.tensor_copy(u_col, uv_sb[:, :, 0])
            for s in range(2):
                sign = 1.0 - 2.0 * s
                nc.vector.tensor_scalar(v_8[:, s, :], uv_sb[:, :, 1], 0.8 * sign, None, ALU.mult)
                ins = nc.vector.tensor_scalar(v_2[:, s, :], uv_sb[:, :, 1], 0.2 * sign, None, ALU.mult)
            ins.then_inc(cols_ready, 1)
            ch.end(1)

            def extreme(t, h, low):
                if not low:
                    nc.vector.tensor_tensor_reduce(out=junk, in0=rows[:, h, :], in1=t_row[:, h * HALF:(h + 1) * HALF],
                                                   scale=1.0, scalar=0.0, op0=ALU.mult, op1=ALU.max,
                                                   accum_out=tmx[:, t, h:h + 1]).then_inc(row_used, 1)
                else:
                    nc.vector.tensor_tensor_reduce(out=junk, in0=rows[:, h, :], in1=t_row[:, h * HALF:(h + 1) * HALF],
                                                   scale=1.0, scalar=-1.0, op0=ALU.subtract, op1=ALU.max,
                                                   accum_out=tmn[:, t, h:h + 1]).then_inc(row_used, 1)

            def shifts(c, ch):
                vM, vm, s_p, s_n, l_p, l_n = (ccol[:, 4:5, :], ccol[:, 5:6, :], ccol[:, 4:5, :], ccol[:, 5:6, :],
                                              ccol[:, 6:7, :], ccol[:, 7:8, :])
                u = u_col[:, bass.ds(c * TPC, TPC)].rearrange("p (a t) -> p a t", a=1)
                dve.wait_ge(row_used, c * 4 * TPC + 4 * TPC)
                dve.wait_ge(ab_ps_ready, c * 2) if not (isinstance(c, int) and c == 0) else None
                nc.vector.tensor_tensor(vM, tmx[:, :, 0:1].rearrange("p t a -> p a t"),
                                        tmx[:, :, 1:2].rearrange("p t a -> p a t"), ALU.max)
                ch.link(nc.vector.tensor_tensor(vm, tmn[:, :, 0:1].rearrange("p t a -> p a t"),
                                                tmn[:, :, 1:2].rearrange("p t a -> p a t"), ALU.max))
                nc.vector.tensor_scalar(vM, vM, v_R, v_c1, ALU.mult, ALU.add)
                ch.link(nc.vector.tensor_scalar(vm, vm, v_nR, v_c2, ALU.mult, ALU.add))
                nc.vector.tensor_tensor(s_p, vM, u, ALU.add)
                ch.link(nc.vector.tensor_tensor(s_n, vm, u, ALU.add))
                nc.vector.scalar_tensor_tensor(l_p, s_p, 0.2, s_p, ALU.mult, ALU.max)
                ch.link(nc.vector.scalar_tensor_tensor(l_n, s_n, 0.2, s_n, ALU.mult, ALU.max))
                nc.vector.tensor_tensor(ccol[:, 0:1, :], u, l_p, ALU.subtract)
                nc.vector.scalar_tensor_tensor(ccol[:, 1:2, :], u, 0.2, l_p, ALU.mult, ALU.subtract)
                nc.vector.tensor_tensor(ccol[:, 2:3, :], l_n, u, ALU.subtract)
                nc.vector.scalar_tensor_tensor(ccol[:, 3:4, :], u, -0.2, l_n, ALU.mult, ALU.add).then_inc(cc_ready, 1)

            def reciprocals(c, s, ch):
                dve.wait_ge(p_used, c * 2 * NT + (s + 1) * NT)
                z = rz[:, s, :].rearrange("p (t a) -> p t a", a=1)
                ch.link(nc.vector.tensor_tensor(z, ps[:, 4 * s:4 * s + 4, F:YW],
                                                lone[:, bass.ds(c * TPC, TPC)].rearrange("p (t a) -> p t a", a=1),
                                                ALU.add))
                if s == 1:
                    ch.link(nc.vector.tensor_scalar(z, z, -1.0, None, ALU.mult))
                nc.vector.reciprocal(z, z).then_inc(rz_ready, 1)

            SEARCHES = 4 * TPC
            SHIFT = 23
            AHEAD = (NT - SHIFT) // 2

            def searches(c, first):
                if first:
                    plan = {m * (SHIFT - 1) // (SEARCHES - 1): (c + 1, m) for m in range(SEARCHES)}
                else:
                    plan = {2 * (m - AHEAD): (c + 1, m) for m in range(AHEAD, SEARCHES)}
                if not (isinstance(c, int) and c == NC - 2):
                    plan.update({SHIFT + 1 + 2 * m: (c + 2, m) for m in range(AHEAD)})
                return plan

            def att_chunk(c, ch, first, last):
                plan = {} if last else searches(c, first)
                for s in range(2):
                    edge = ALU.max if s == 0 else ALU.min
                    dve.wait_ge(ab_ready, c * 2 + (s + 1))
                    for pair in range(NT // 2 + 1):
                        n = s * (NT // 2) + pair
                        c_m, m = plan.get(n, (0, None)) if pair < NT // 2 else (0, None)
                        if m is not None:
                            dve.wait_ge(row_used, c_m * SEARCHES + m)
                            if m % 2 == 0:
                                dve.wait_ge(row_in[m // 2 % 2], (c_m * TPC + m // 4) * 16 + 16)
                        if pair == 4:
                            if s == 1:
                                reciprocals(c, 0, ch)
                            elif not first:
                                reciprocals(c - 1, 1, ch)
                        if n == SHIFT and pair < NT // 2 and not last:
                            shifts(c + 1, ch)
                        if pair < NT // 2:
                            for j in (2 * pair, 2 * pair + 1):
                                k = s * NT + j
                                if not (first and k < RING):
                                    dve.wait_ge(p_used, c * 2 * NT + (k - RING + 1))
                                ins = nc.vector.scalar_tensor_tensor(E[:, j % RING, :], AB[:, 2 * s, :],
                                                                     v_8[:, s, j:j + 1], AB[:, 2 * s + 1, :],
                                                                     ALU.add, edge)
                            ins.then_inc(edge_ready, 1)
                        if pair >= 1:
                            i = 2 * (pair - 1)
                            if s == 0 and i % TPC == 0:
                                dve.wait_ge(mask_ready, c * NC + (i // TPC + 1))
                            dve.wait_ge(edge_ready, c * NT + (s * NT // 2 + pair))
                            slots = E[:, i % RING:i % RING + 2, :]
                            nc.vector.tensor_tensor(slots, mask[:, i:i + 2, :], slots, ALU.add).then_inc(lin_ready, 1)
                        if m is not None:
                            extreme(m // 4, m // 2 % 2, m % 2)

            for t in range(TPC):
                for h in range(2):
                    dve.wait_ge(row_in[h], t * 16 + 16)
                    wait(dve, row_used, 4 * t + 2 * h)
                    extreme(t, h, 0)
                    dve.wait_ge(row_used, 4 * t + 2 * h + 1)
                    extreme(t, h, 1)
            ch = Chain(0, 0)
            shifts(0, ch)
            dve.wait_ge(my_ps_ready, 1)
            ch.link(nc.vector.tensor_scalar(mean_y, ps[:, 5, 0:F], 1.0 / (SC * N), None, ALU.mult))
            nc.vector.scalar_tensor_tensor(mean_y, ps[:, 5, F:2 * F], -1.0 / (SC * N), mean_y, ALU.mult, ALU.add)\
              .then_inc(my_ready, 1)
            att_chunk(0, ch, True, False)
            ch.end(1)
            with dve.Fori(1, NC - 2) as c:
                ch = Chain(c - 1, 8 - 1)
                att_chunk(c, ch, False, False)
            ch.end(NC - 3)
            ch = Chain(0, 0)
            att_chunk(NC - 2, ch, False, False)
            ch.end(1)
            ch = Chain(0, 0)
            att_chunk(NC - 1, ch, False, True)
            dve.wait_ge(x3_in, 16 * NC)
            nc.vector.tensor_scalar(x3, x3, -1.0, None, ALU.add)
            reciprocals(NC - 1, 1, ch)
            dve.wait_ge(rz_ready, 2 * NC)
            dve.wait_ge(att_evac, 2 * TPC * NC - TPC)
            for t in range(TPC):
                i, D = NT - TPC + t, R[:, 0, t, :]
                ch.link(nc.vector.scalar_tensor_tensor(D, ps[:, 4 + t, 0:F], rz[:, 1, t:t + 1], D, ALU.mult, ALU.add))
                nc.vector.scalar_tensor_tensor(D, mean_y, lone[:, i:i + 1], D, ALU.mult, ALU.add).then_inc(last_in, 1)
            for t in range(TPC):
                D, M = R[:, 0, t, :], R[:, 1, t, :]
                dve.wait_ge(last_out, t + 1)
                ch.link(nc.vector.tensor_tensor(D, D, x3[:, t, :], ALU.add))
                ins = nc.vector.tensor_tensor(D, D, M, ALU.add)
            ins.then_inc(fin_ready, 1)
            ch.end(1)

        @block.tensor
        def _(pe):
            mm = nc.tensor.matmul

            pe.wait_ge(small_in, 32)
            for k in range(FB):
                for f in range(FB):
                    ins = mm(ps[:, 3, 2 * k:2 * k + 2], w3t_sb[:, f, k * P:(k + 1) * P], a_sb[:, f, :],
                             start=(f == 0), stop=(f == FB - 1))
            ins.then_inc(wa_ps_ready, 1)
            pe.wait_ge(consts_ready, 4)

            def block_product(n, block):
                i, j0 = block
                pe.wait_ge(blk_staged, n + 1)
                pe.wait_ge(split_done, j0 + PANELS)
                for jj in range(PANELS):
                    j = j0 + jj
                    bank = {0: 0 if j < NT // 2 else 2, 1: 4, 2: 2}[i]
                    for f in range(FB):
                        for h in range(2):
                            ins = mm(ps[:, bank + f, :], parts[:, j, h, f * P:(f + 1) * P], stage0[:, n % 2, jj, :],
                                     start=(j % (NT // 2) == 0 and h == 0), stop=(j % (NT // 2) == NT // 2 - 1 and h == 1),
                                     skip_group_check=True)
                ins.then_inc(blk_used, 1)

            for c in range(NC):
                if c >= 2:
                    pe.wait_ge(var_ready, c - 1)
                deg = ps[:, 6 + c % 2, 0:TPC]
                mm(deg, zeros16[:, :], zeros16[:, 0:TPC], start=True, stop=False, skip_group_check=True)
                for g in range(GROUPS):
                    pe.wait_ge(cast16_done, c * GROUPS + g + 1)
                    for jj in range(PANELS):
                        for t in range(TPC):
                            ins = mm(deg[:, t:t + 1], piece16[:, g % 2, jj, t * P:(t + 1) * P], ones16[:, :],
                                     start=False, stop=False, skip_group_check=True)
                    ins.then_inc(deg_used, 1)
                    if g == GROUPS - 1:
                        mm(deg, zeros16[:, :], zeros16[:, 0:TPC], start=False, stop=True,
                           skip_group_check=True).then_inc(deg_done, 1)
                    if c > 0:
                        if c == 3 and g == 0:
                            pe.wait_ge(wa_ready, 1)
                        if c == H + 1 and g == 10:
                            pe.wait_ge(half_saved, 2)
                        for n, block in taken_at(c - 1, g):
                            block_product(n, block)
            for n, block in last_blocks:
                block_product(n, block)

            def spread(out_, column):
                return mm(out_, column.to_broadcast([P, P]), ident32[:, :], start=True, stop=True,
                          skip_group_check=True)

            for l in range(4):
                def main(c, s, g, split_waits):
                    pe.wait_ge(panel_ready, c * GROUPS + (staged(l) + g + 1))
                    for jj in range(PANELS):
                        j = g * PANELS + jj
                        if split_waits:
                            if l == 2:
                                pe.wait_ge(split_done, NT + j + 1)
                            elif j % TPC == 0:
                                pe.wait_ge(parts_in[j // TPC], 16 if l == 1 else 48)
                        if l == 0:
                            bank, fresh, end = (0, j == 0, j == NT // 2 - 1) if j < NT // 2 else (2, j == NT // 2, j == NT - 1)
                        else:
                            bank, fresh, end = 2 * s, j == 0, j == NT - 1
                        for f in range(FB):
                            for h in range(2):
                                ins = mm(ps[:, bank + f, :], parts[:, j, h, f * P:(f + 1) * P],
                                         stage[:, g % STAGES, jj, :], start=(fresh and h == 0),
                                         stop=(end and h == 1), skip_group_check=True)
                    ins.then_inc(group_done, 1)

                def own_features(c):
                    for t in range(TPC):
                        for f in range(FB):
                            for h in range(2):
                                ins = mm(ps[:, 4 + f, t * P:(t + 1) * P],
                                         parts[:, bass.ds(c * TPC + t, 1), h, f * P:(f + 1) * P].rearrange("p a f -> p (a f)"),
                                         ident16[:, :], start=(h == 0), stop=(h == 1), skip_group_check=True)
                    ins.then_inc(ht1_ready, 1)

                def project(c, prev_layer):
                    pe.wait_ge(evac_done, c * EVACS[l] + (EVAC_BASE[l] + EVACS[l]))
                    for t in range(TPC):
                        if not prev_layer:
                            pe.wait_ge(out_used[l], c * TPC + ((t | 1) - TPC + 1))
                        elif l > 0:
                            pe.wait_ge(out_used[l - 1], NT)
                        for k in range(KB[l]):
                            ins = mm(out_slot(t), T_sb[:, k, t * P:(t + 1) * P], w_sb[:, k, :],
                                     start=(k == 0), stop=(k == KB[l] - 1), skip_group_check=True)
                        ins.then_inc(out_ready, 1)

                def chunk_after_load():
                    half = GROUPS // 2
                    for g in range(half, GROUPS):
                        if g == half:
                            pe.wait_ge(evac_done, 2)
                        if g == half + 2:
                            pe.wait_ge(weights_in, W_NEEDED[0])
                            project(0, True)
                        if g == half + 4:
                            project(1, False)
                        main(2, 0, g, False)

                def chunk(c, s, first, prev):
                    if l == 0:
                        pe.wait_ge(evac_done, c * 2 - 1)
                    elif not first:
                        if l in (1, 2):
                            pe.wait_ge(evac_done, c * 2 + (EVAC_BASE[l] - 1))
                        if not (isinstance(c, int) and c < 2):
                            pe.wait_ge(evac_done, c * EVACS[l] + (EVAC_BASE[l] - EVACS[l]))
                    for g in range(GROUPS // 2):
                        main(c, s, g, first)
                        if g == TPC // PANELS - 1 and l in (1, 2):
                            own_features(c)
                    if prev is not None:
                        project(c - 1, prev)
                    if l == 0:
                        pe.wait_ge(evac_done, c * 2)
                    for g in range(GROUPS // 2, GROUPS):
                        main(c, s, g, first)

                if l == 3:
                    pe.wait_ge(wa_ready, 1)
                    for k in range(2):
                        for f in range(FB):
                            ins = spread(ps[:, 4, k * F + f * P:k * F + (f + 1) * P], wa_sb[:, f, k:k + 1])
                    ins.then_inc(wa_rows_ps, 1)
                if l == 0:
                    chunk_after_load()
                else:
                    chunk(0, 0, True, None)
                    pe.wait_ge(weights_in, W_NEEDED[l])
                    chunk(1, 1, False, True)
                    chunk(2, 0, False, False)
                with pe.Fori(1, H - 1) as r:
                    chunk(r * 2 + 1, 1, False, False)
                    chunk(r * 2 + 2, 0, False, False)
                chunk(NC - 1, 1, False, False)
                project(NC - 1, False)

            def transposed(c):
                pe.wait_ge(parts_in[c], 64)
                if c >= 2:
                    pe.wait_ge(ht_evac, c - 1)
                k = 2 * (c % 2)
                for t in range(TPC):
                    for f in range(FB):
                        for h in range(2):
                            ins = mm(ps[:, k + f, t * P:(t + 1) * P], parts[:, c * TPC + t, h, f * P:(f + 1) * P],
                                     ident16[:, :], start=(h == 0), stop=(h == 1), skip_group_check=True)
                ins.then_inc(ht_ready, 1)

            def projected(j):
                if j >= 2:
                    pe.wait_ge(y_evac, j - 1)
                c, t = j // TPC, j % TPC
                for k in range(FB):
                    ins = mm(ps[:, 2 + j % 2, :], T_all[:, c, k, t * P:(t + 1) * P], wt_sb[:, k, :],
                             start=(k == 0), stop=(k == FB - 1), skip_group_check=True)
                ins.then_inc(y_ps_ready, 1)

            def spread_rows(s, c):
                pe.wait_ge(cc_ready, c + 1)
                if not (isinstance(c, int) and c == 0):
                    pe.wait_ge(att_evac, c * 2 * TPC + TPC * (s - 1))
                for q in range(2):
                    for t in range(TPC):
                        ins = spread(ps[:, 4 * s + q, t * P:(t + 1) * P], ccol[:, 2 * s + q, t:t + 1])
                ins.then_inc(ab_ps_ready, 1)

            def att_chunk(c, last):
                for s in range(2):
                    pe.wait_ge(ab_ready, c * 2 + (s + 1))
                    for j in range(NT):
                        pe.wait_ge(p_ready, c * 2 * NT + (s * NT + j + 1))
                        for t in range(TPC):
                            ins = mm(ps[:, 4 * s + t, 0:YW], E[:, j % RING, t * P:(t + 1) * P], Yb[:, j, s, :],
                                     start=(j == 0), stop=(j == NT - 1), skip_group_check=True)
                        ins.then_inc(p_used, 1)
                        if s == 0 and j == 10:
                            spread_rows(1, c)
                        if s == 1 and j == 16 and not last:
                            spread_rows(0, c + 1)

            for c in range(EARLY):
                transposed(c)
            pe.wait_ge(uv_ready, 1)
            for c in range(NC):
                if c >= 2:
                    pe.wait_ge(vb_evac, c - 1)
                for t in range(TPC):
                    ins = spread(ps[:, 6 + c % 2, t * P:(t + 1) * P], uv_sb[:, c * TPC + t, 1:2])
                ins.then_inc(vb_ps_ready, 1)
            for c in range(EARLY, NC):
                transposed(c)
            pe.wait_ge(weights_in, W_NEEDED[4])
            pe.wait_ge(ht_evac, NC)
            for j in range(NT):
                if j == ROWS_AT:
                    pe.wait_ge(vb_evac, NC)
                    spread_rows(0, 0)
                if j == NT // 2:
                    pe.wait_ge(hsum_ready, 1)
                    for k in range(FB):
                        ins = mm(ps[:, 5, :], hsum1[:, k:k + 1].to_broadcast([P, P]), wt_sb[:, k, :],
                                 start=(k == 0), stop=(k == FB - 1), skip_group_check=True)
                    ins.then_inc(my_ps_ready, 1)
                projected(j)
            pe.wait_ge(out_used[3], NT)
            pe.wait_ge(ones_set, 1)
            pe.wait_ge(y_evac, NT)
            att_chunk(0, False)
            with pe.Fori(1, NC - 1) as c:
                att_chunk(c, False)
            att_chunk(NC - 1, True)


def kernel(x, adj, L0_gnn_weightr, L0_gnn_weightd, L0_gnn_bias, L1_gnn_W1, L1_gnn_W2, L2_gnn_W, L2_gnn_b,
           L3_gnn_W, L3_gnn_a, L3_gnn_wtrans):
    import numpy as np
    import concourse.bacc as bacc
    from concourse.bass_utils import run_bass_kernel_spmd

    x, adj = np.asarray(x), np.asarray(adj)
    F = x.shape[1]
    arrays = {
        "x": x,
        "adj_t": np.ascontiguousarray(adj.T),
        "adj": adj,
        "w_gcn": np.concatenate([np.asarray(L0_gnn_weightr), np.asarray(L0_gnn_weightd)], axis=0),
        "b_gcn": np.asarray(L0_gnn_bias),
        "w_conv1": np.asarray(L1_gnn_W1),
        "w_conv2": np.asarray(L1_gnn_W2),
        "w_gcn2": np.ascontiguousarray(np.asarray(L2_gnn_W).T),
        "b_gcn2": np.asarray(L2_gnn_b),
        "w_att_t": np.ascontiguousarray(np.asarray(L3_gnn_W).T),
        "a_att": np.ascontiguousarray(np.asarray(L3_gnn_a).reshape(2, F).T),
        "w_trans": np.asarray(L3_gnn_wtrans),
    }
    nc = bacc.Bacc("TRN2", target_bir_lowering=False, num_devices=1)
    args = [nc.dram_tensor(f"in_{n}", a.shape, mybir.dt.from_np(a.dtype), kind="ExternalInput").ap()
            for n, a in arrays.items()]
    out = nc.dram_tensor("out", x.shape, mybir.dt.float32, kind="ExternalOutput").ap()
    gnn_stack(nc, *args, out)
    r = run_bass_kernel_spmd(nc, [{f"in_{n}": a for n, a in arrays.items()}], core_ids=[0])
    return r.results[0]["out"]
```
